# Optimizing a Trainium2 kernel written in Bass

```python
import numpy as np
import jax
import jax.numpy as jnp

def _softmax(x, axis=-1):
    return jax.nn.softmax(x, axis=axis)

def _gelu(x):
    return jax.nn.gelu(x, approximate=True)

def _silu(x):
    return jax.nn.silu(x)

def _sigmoid(x):
    return jax.nn.sigmoid(x)

def _layernorm(x, axis=-1, eps=1e-05):
    m = jnp.mean(x, axis=axis, keepdims=True)
    v = jnp.var(x, axis=axis, keepdims=True)
    return (x - m) / jnp.sqrt(v + eps)

def _scatter_add(tgt, idx, src, axis=0):
    return tgt.at[idx].add(src)

def _segment_sum(src, seg, n):
    return jax.ops.segment_sum(src, seg, n)
kernel_name = 'mk_early_fusion_d1_tok_img768_r4_27a20b'

def setup_inputs(seed: int=0):
    np.random.seed(seed)
    _w = jnp.asarray

    def _rec_inputs():
        import jax
        import jax.numpy as jnp
        _rk = jax.random.key(seed)
        x = -0.000356955 + 1 * jax.random.normal(jax.random.fold_in(_rk, 1), (16, 3, 112, 112), jnp.float32)
        txt = 8.44072e-05 + 0.997355 * jax.random.normal(jax.random.fold_in(_rk, 2), (16, 128, 192), jnp.float32)
        return (x, txt)
    x, txt = _rec_inputs()

    def _L0_tok_setup():
        import jax, jax.numpy as jnp
        import numpy as np
        P = 16

        def _patchify(x):
            B, C, H, Wd = x.shape
            Hp, Wp = (H // P, Wd // P)
            x = x.reshape(B, C, Hp, P, Wp, P)
            x = x.transpose(0, 2, 4, 1, 3, 5)
            return x.reshape(B, Hp * Wp, C * P * P)
        key = jax.random.key(seed)
        k1, k2, k3 = jax.random.split(key, 3)
        B, C, H, W_img = (128, 3, 224, 224)
        E = 192
        x = jax.random.normal(k1, (B, C, H, W_img), dtype=jnp.float32)
        W = jax.random.normal(k2, (C * P * P, E), dtype=jnp.float32) * (1.0 / np.sqrt(C * P * P))
        b = jnp.zeros((E,), dtype=jnp.float32)
        cls_token = jax.random.normal(k3, (1, 1, E), dtype=jnp.float32) * 0.02
        return {'x': x, 'W': W, 'b': b, 'cls_token': cls_token}
    _L0_tok_all = _L0_tok_setup()
    _L0_tok_in = {k: v for k, v in _L0_tok_all.items() if k in ('W', 'b', 'cls_token')}
    del _L0_tok_all

    def _L0_attn_setup():
        import jax, jax.numpy as jnp
        import numpy as np
        EMBED_DIM = 192
        NUM_HEADS = 12
        HEAD_DIM = EMBED_DIM // NUM_HEADS
        SCALING = HEAD_DIM ** (-0.5)
        B, N = (4, 512)
        key = jax.random.key(seed)
        k_x, k_wqkv, k_bqkv, k_wo, k_bo = jax.random.split(key, 5)
        s = EMBED_DIM ** (-0.5)
        return {'x_q': jax.random.normal(k_x, (B, N, EMBED_DIM), dtype=jnp.float32), 'w_qkv': jax.random.normal(k_wqkv, (3 * EMBED_DIM, EMBED_DIM), dtype=jnp.float32) * s, 'b_qkv': jax.random.normal(k_bqkv, (3 * EMBED_DIM,), dtype=jnp.float32) * s, 'w_out': jax.random.normal(k_wo, (EMBED_DIM, EMBED_DIM), dtype=jnp.float32) * s, 'b_out': jax.random.normal(k_bo, (EMBED_DIM,), dtype=jnp.float32) * s}
    _L0_attn_all = _L0_attn_setup()
    _L0_attn_in = {k: v for k, v in _L0_attn_all.items() if k in ('w_qkv', 'b_qkv', 'w_out', 'b_out')}
    del _L0_attn_all

    def _L0_ffn_setup():
        import jax, jax.numpy as jnp
        import numpy as np
        B, T, C, H, E, TOPK, DR = (2, 512, 192, 768, 8, 2, 24)

        def _normalize(v, axis=-1, eps=1e-12):
            return v / jnp.maximum(jnp.linalg.norm(v, axis=axis, keepdims=True), eps)
        key = jax.random.key(seed)
        ks = jax.random.split(key, 16)
        std = 0.02
        n = lambda k, shape, s=std: (s * jax.random.normal(k, shape)).astype(jnp.float32)
        emb = jax.random.normal(ks[3], (E, DR), dtype=jnp.float32)
        emb = emb / (jnp.linalg.norm(emb, axis=-1, keepdims=True) + 1e-08)
        return {'x': jax.random.normal(ks[0], (B, T, C), dtype=jnp.float32), 'router_w': n(ks[1], (E, C)), 'probe_w': n(ks[2], (DR, C)), 'router_emb': emb, 'fatigue': jnp.zeros((E,), jnp.float32), 'energy': jnp.ones((E,), jnp.float32), 'w_fast1': n(ks[4], (E, C, H)), 'w_slow1': n(ks[5], (E, C, H)), 'h_fast1': n(ks[6], (E, C, H), 0.005), 'm_gate1': jax.random.uniform(ks[7], (E,), dtype=jnp.float32), 'b1': jnp.zeros((E, H), jnp.float32), 'w_fast2': n(ks[8], (E, H, C)), 'w_slow2': n(ks[9], (E, H, C)), 'h_fast2': n(ks[10], (E, H, C), 0.005), 'm_gate2': jax.random.uniform(ks[11], (E,), dtype=jnp.float32), 'b2': jnp.zeros((E, C), jnp.float32)}
    _L0_ffn_all = _L0_ffn_setup()
    _L0_ffn_in = {k: v for k, v in _L0_ffn_all.items() if k in ('router_w', 'probe_w', 'router_emb', 'fatigue', 'energy', 'w_fast1', 'w_slow1', 'h_fast1', 'm_gate1', 'b1', 'w_fast2', 'w_slow2', 'h_fast2', 'm_gate2', 'b2')}
    del _L0_ffn_all
    return {'x': x, 'txt': txt, 'L0_tok_W': _L0_tok_in['W'], 'L0_tok_b': _L0_tok_in['b'], 'L0_tok_cls_token': _L0_tok_in['cls_token'], 'L0_attn_w_qkv': _L0_attn_in['w_qkv'], 'L0_attn_b_qkv': _L0_attn_in['b_qkv'], 'L0_attn_w_out': _L0_attn_in['w_out'], 'L0_attn_b_out': _L0_attn_in['b_out'], 'L0_ffn_router_w': _L0_ffn_in['router_w'], 'L0_ffn_probe_w': _L0_ffn_in['probe_w'], 'L0_ffn_router_emb': _L0_ffn_in['router_emb'], 'L0_ffn_fatigue': _L0_ffn_in['fatigue'], 'L0_ffn_energy': _L0_ffn_in['energy'], 'L0_ffn_w_fast1': _L0_ffn_in['w_fast1'], 'L0_ffn_w_slow1': _L0_ffn_in['w_slow1'], 'L0_ffn_h_fast1': _L0_ffn_in['h_fast1'], 'L0_ffn_m_gate1': _L0_ffn_in['m_gate1'], 'L0_ffn_b1': _L0_ffn_in['b1'], 'L0_ffn_w_fast2': _L0_ffn_in['w_fast2'], 'L0_ffn_w_slow2': _L0_ffn_in['w_slow2'], 'L0_ffn_h_fast2': _L0_ffn_in['h_fast2'], 'L0_ffn_m_gate2': _L0_ffn_in['m_gate2'], 'L0_ffn_b2': _L0_ffn_in['b2']}

def reference(x, txt, L0_tok_W, L0_tok_b, L0_tok_cls_token, L0_attn_w_qkv, L0_attn_b_qkv, L0_attn_w_out, L0_attn_b_out, L0_ffn_router_w, L0_ffn_probe_w, L0_ffn_router_emb, L0_ffn_fatigue, L0_ffn_energy, L0_ffn_w_fast1, L0_ffn_w_slow1, L0_ffn_h_fast1, L0_ffn_m_gate1, L0_ffn_b1, L0_ffn_w_fast2, L0_ffn_w_slow2, L0_ffn_h_fast2, L0_ffn_m_gate2, L0_ffn_b2):
    import jax
    import jax.numpy as jnp

    def _L0_tok_ref(x, W, b, cls_token):
        import jax, jax.numpy as jnp
        import numpy as np
        P = 16

        def _patchify(x):
            B, C, H, Wd = x.shape
            Hp, Wp = (H // P, Wd // P)
            x = x.reshape(B, C, Hp, P, Wp, P)
            x = x.transpose(0, 2, 4, 1, 3, 5)
            return x.reshape(B, Hp * Wp, C * P * P)
        B = x.shape[0]
        patches = _patchify(x)
        emb = jnp.einsum('blk,ke->ble', patches, W) + b
        cls = jnp.broadcast_to(cls_token, (B, 1, cls_token.shape[-1]))
        out = jnp.concatenate([cls, emb], axis=1)
        return out

    def _L0_attn_ref(x_q, w_qkv, b_qkv, w_out, b_out):
        import jax, jax.numpy as jnp
        import numpy as np
        EMBED_DIM = 192
        NUM_HEADS = 12
        HEAD_DIM = EMBED_DIM // NUM_HEADS
        SCALING = HEAD_DIM ** (-0.5)
        B, N = (4, 512)
        b_sz, n, _ = x_q.shape
        qkv = jnp.einsum('bne,fe->bnf', x_q, w_qkv) + b_qkv
        qkv = qkv.reshape(b_sz, n, 3, NUM_HEADS, HEAD_DIM).transpose(0, 3, 2, 1, 4)
        q, k, v = (qkv[:, :, 0], qkv[:, :, 1], qkv[:, :, 2])
        q = q * SCALING
        attn = jnp.einsum('bhqd,bhkd->bhqk', q, k) + 1.0
        attn = jax.nn.softmax(attn, axis=-1)
        out = jnp.einsum('bhqk,bhkd->bhqd', attn, v)
        out = out.transpose(0, 2, 1, 3).reshape(b_sz, n, EMBED_DIM)
        return jnp.einsum('bne,fe->bnf', out, w_out) + b_out

    def _L0_ffn_ref(x, router_w, probe_w, router_emb, fatigue, energy, w_fast1, w_slow1, h_fast1, m_gate1, b1, w_fast2, w_slow2, h_fast2, m_gate2, b2):
        import jax, jax.numpy as jnp
        import numpy as np
        B, T, C, H, E, TOPK, DR = (2, 512, 192, 768, 8, 2, 24)

        def _normalize(v, axis=-1, eps=1e-12):
            return v / jnp.maximum(jnp.linalg.norm(v, axis=axis, keepdims=True), eps)
        Bd, Td, Cd = x.shape
        logits = jnp.einsum('btc,ec->bte', x, router_w)
        tok_proxy = x.mean(axis=-1, keepdims=True)
        router_gain = jnp.linalg.norm(router_emb, axis=-1)
        base_bias = 0.02 * tok_proxy
        gain_bias = 0.02 * tok_proxy * router_gain
        tok_unit = _normalize(jnp.einsum('btc,dc->btd', x, probe_w))
        align_bias = 0.02 * jnp.einsum('btd,ed->bte', tok_unit, _normalize(router_emb))
        logits = logits + base_bias + gain_bias + align_bias + 0.1 * energy - 0.1 * fatigue
        g, idx = jax.lax.top_k(logits, TOPK)
        gates = jax.nn.softmax(g, axis=-1)
        N = Bd * Td
        gates_full = jnp.zeros((N, E), x.dtype).at[jnp.arange(N)[:, None], idx.reshape(N, TOPK)].set(gates.reshape(N, TOPK))
        flat_x = x.reshape(N, Cd)

        def body(acc, p):
            wf1, ws1, hf1, mg1, bb1, wf2, ws2, hf2, mg2, bb2, ge = p
            W1 = wf1 + mg1 * ws1 + hf1
            h = jnp.square(jnp.maximum(flat_x @ W1 + bb1, 0.0))
            W2 = wf2 + mg2 * ws2 + hf2
            y = h @ W2 + bb2
            return (acc + ge[:, None] * y, None)
        out, _ = jax.lax.scan(body, jnp.zeros((N, Cd), x.dtype), (w_fast1, w_slow1, h_fast1, m_gate1, b1, w_fast2, w_slow2, h_fast2, m_gate2, b2, gates_full.T))
        return out.reshape(Bd, Td, Cd)
    h = _L0_tok_ref(x, L0_tok_W, L0_tok_b, L0_tok_cls_token)
    h = jnp.concatenate([h, txt], axis=1)
    h = h + _L0_attn_ref(_layernorm(h, axis=-1), L0_attn_w_qkv, L0_attn_b_qkv, L0_attn_w_out, L0_attn_b_out)
    h = h + _L0_ffn_ref(_layernorm(h, axis=-1), L0_ffn_router_w, L0_ffn_probe_w, L0_ffn_router_emb, L0_ffn_fatigue, L0_ffn_energy, L0_ffn_w_fast1, L0_ffn_w_slow1, L0_ffn_h_fast1, L0_ffn_m_gate1, L0_ffn_b1, L0_ffn_w_fast2, L0_ffn_w_slow2, L0_ffn_h_fast2, L0_ffn_m_gate2, L0_ffn_b2)
    return h

_drawn_inputs = setup_inputs


def setup_inputs(seed=0):
    import zlib

    import numpy as np

    out = dict(_drawn_inputs(seed))
    spreads = {'L0_tok_b': (0.0, 0.1),
     'L0_ffn_fatigue': (0.0, 0.454),
     'L0_ffn_energy': (1.0, 0.6),
     'L0_ffn_b1': (0.0, 0.368),
     'L0_ffn_b2': (0.0, 0.1)}
    factors = {'L0_tok_cls_token': 3.471,
     'L0_ffn_probe_w': 5.423,
     'L0_ffn_router_emb': 5.803,
     'L0_ffn_h_fast1': 3.829,
     'L0_ffn_m_gate1': 3.138,
     'L0_ffn_h_fast2': 4.478,
     'L0_ffn_m_gate2': 3.697}
    for name, (base, spread) in spreads.items():
        noise = np.random.default_rng([zlib.crc32(name.encode()), seed]).standard_normal(out[name].shape)
        drawn = base * np.exp(spread * noise) if base else spread * noise
        out[name] = jnp.asarray(drawn.astype(out[name].dtype))
    for name, factor in factors.items():
        out[name] = (out[name] * factor).astype(out[name].dtype)
    return out
```

```python
from contextlib import ExitStack

import numpy as np

import concourse.bass as bass
from concourse import mybir

F32 = mybir.dt.float32
F32R = mybir.dt.float32r
I32 = mybir.dt.int32
U32 = mybir.dt.uint32
ALU = mybir.AluOpType
ACT = mybir.ActivationFunctionType
AX = mybir.AxisListType

B = 16
PS = 16
GRID = 7
NPATCH = GRID * GRID
TXT = 128
T = 1 + NPATCH + TXT
HT = T // 2
N = B * T
C = 192
CA, CT = 128, 64
NH, HD = 12, 16
PAIRS = NH // 2
UNITS = 2 * PAIRS
UR = 4
KC = 3 * PS * PS // 128
E, H, TOPK, DR = 8, 768, 2, 24
HC = H // 128
CAP = N + 128
BLOCKS = (TOPK * N + E * 127) // 128
ROWS = E * CAP + 8 * 128
WCOLS = 2 * H + HC * C
ROW = C + 2
RC = 2 * E + DR
SCALE = HD ** -0.5
NTOK = B * GRID

K_ID, K_TRI = 0, 128
K_ONE = K_TRI + HT
K_DESC = K_ONE + 128
K_BASE = K_DESC + 4 * E
K_TOK = K_BASE + 4 * E
K_JJ = K_TOK + 4
K_KK = K_JJ + BLOCKS
K_CUM = K_KK + 23
K_COLS = K_CUM + E * E


def shape_constants():
    c = np.zeros((128, K_COLS), np.float32)
    c[:, K_ID:K_ID + 128] = np.eye(128)
    c[:HT, K_TRI:K_TRI + HT] = np.triu(np.ones((HT, HT)), 1)
    c[:, K_ONE:K_ONE + 128] = 1
    c[:, K_DESC:K_DESC + 4 * E] = np.tile(E - np.arange(E), 4)
    c[:, K_BASE:K_BASE + 4 * E] = np.tile(CAP * np.arange(E), 4)
    p = np.arange(128)
    for i in range(4):
        c[:, K_TOK + i] = (i // 2) * T + (i % 2) * HT + p
    c[:, K_JJ:K_JJ + BLOCKS] = np.arange(BLOCKS)
    c[:, K_KK:K_KK + 23] = 128 * np.arange(23)
    c[:, K_CUM:K_CUM + E * E] = np.tril(np.ones((E, E))).ravel()
    sel = np.zeros((2, PAIRS, 2, T), np.float32)
    sel[0, :, 0], sel[1, :, 1] = 1, 1
    empty = np.zeros((128, ROW), np.float32)
    empty[:, C + 1] = (N + p).astype(np.uint32).view(np.float32)
    return {"shape_consts": c, "head_select": sel, "empty_slots": empty}


def build_program(nc, x, txt, tok_w, tok_b, cls, w_qkv, b_qkv, w_out, b_out, router_w, probe_w, router_emb,
                  fatigue, energy, w_fast1, w_slow1, h_fast1, m_gate1, b1, w_fast2, w_slow2, h_fast2,
                  m_gate2, b2, shape_consts, head_select, empty_slots, out):
    ctx = ExitStack()
    with ctx:
        def sb(name, shape, dt=F32):
            return ctx.enter_context(nc.sbuf_tensor(name, shape, dt))

        def pb(name, shape, dt=F32):
            return ctx.enter_context(nc.psum_tensor(name, shape, dt))

        def sem(name):
            return ctx.enter_context(nc.semaphore(name))

        def sems(name, n):
            return [sem(f"{name}{i}") for i in range(n)]

        h_dram = nc.dram_tensor("h_tokens", [N, C], F32, kind="Internal").ap()
        qk_dram = [nc.dram_tensor(f"qk_split{i}", [2, 3, 2 * HD, PAIRS * T], F32, kind="Internal").ap() for i in range(2)]
        m_dram = [nc.dram_tensor(f"neg_max{i}", [2 * NH, HT], F32, kind="Internal").ap() for i in range(2)]
        emb_dram = nc.dram_tensor("patch_rows", [B * GRID, GRID, C], F32, kind="Internal").ap()
        slots_dram = nc.dram_tensor("slots", [ROWS, ROW], F32, kind="Internal").ap()

        kon = sb("kon", [128, K_COLS])
        ident = kon[:, K_ID:K_ID + 128]
        empty = sb("empty", [128, ROW])
        experts = sb("experts", [128, E, WCOLS])
        stage_s = sb("stage_s", [128, WCOLS])
        stage_h = sb("stage_h", [128, WCOLS])
        mg = sb("mg", [128, 2, E])
        b2_bc = sb("b2_bc", [128, E, C])
        wqkv_hi = sb("wqkv_hi", [128, 3 * C], F32R)
        wqkv_lo = sb("wqkv_lo", [128, 3 * C], F32R)
        wqkv_t1 = sb("wqkv_t1", [CT, 3 * C], F32R)
        wqkv_t2 = sb("wqkv_t2", [128, 3 * C], F32R)
        wout = sb("wout", [128, 3, C])
        wroute = sb("wroute", [128, 2, RC])
        bqk = sb("bqk", [128, 3])
        bv_bc = sb("bv_bc", [HT, 2, C])
        bias_e = sb("bias_e", [HT, 4, E])
        powers = sb("powers", [HT, 4])
        hA = [sb(f"hA{i}", [HT, 2, C]) for i in range(2)]
        hR = [sb(f"hR{i}", [HT, 2, C]) for i in range(2)]
        st1 = [sb(f"st1_{i}", [HT, 2, 6]) for i in range(2)]
        mv1 = [sb(f"mv1_{i}", [HT, 2, 2]) for i in range(2)]
        rs1 = [sb(f"rs1_{i}", [HT, 2, 2]) for i in range(2)]
        st2 = [sb(f"st2_{i}", [HT, 2, 6]) for i in range(2)]
        mv2 = [sb(f"mv2_{i}", [HT, 2, 2]) for i in range(2)]
        rs2 = [sb(f"rs2_{i}", [HT, 2, 2]) for i in range(2)]
        xn = sb("xn", [HT, 2, 256])
        xa_hi = sb("xa_hi", [128, T], F32R)
        xa_lo = sb("xa_lo", [128, T], F32R)
        xt = sb("xt", [128, T], F32R)
        qk_hi = sb("qk_hi", [128, 3, T], F32R)
        qk_lo = sb("qk_lo", [128, 3, T], F32R)
        qpack = [sb(f"qpack{i}", [98, PAIRS, T], F32R) for i in range(2)]
        kdiag = [sb(f"kdiag{i}", [98, PAIRS, 2, T], F32R) for i in range(2)]
        vaug = [sb(f"vaug{i}", [HT, 2, NH, 32]) for i in range(2)]
        mx = sb("mx", [HT, 2, PAIRS, 2])
        mT = sb("mT", [2 * NH, HT], F32R)
        probs = sb("probs", [HT, 2, 2, T])
        work = sb("work", [128, 3, 3 * T])
        o_raw, o_sum, o_nrm = (work[:, i, :].rearrange("p (g t) -> p g t", g=3) for i in range(3))
        xn2 = sb("xn2", [HT, 2, 2, C])
        xn2T = sb("xn2T", [128, 2, T])
        rt = sb("rt", [HT, 4, RC])
        rsq = sb("rsq", [HT, 4, DR])
        rss = sb("rss", [HT, 4])
        rnm = sb("rnm", [HT, 4])
        rinv = sb("rinv", [HT, 4])
        lg = sb("lg", [HT, 4, E])
        lg2 = sb("lg2", [HT, 4, E])
        top = sb("top", [HT, 2, 4])
        cand = sb("cand", [HT, 4, E])
        cmx = sb("cmx", [HT, 4])
        hot = sb("hot", [HT, 2, 4, E])
        cum = sb("cum", [HT, 5, E])
        dlt = sb("dlt", [HT, 4])
        edl = sb("edl", [HT, 4])
        gates = sb("gates", [HT, 2, 4])
        rank = sb("rank", [HT, 4, E])
        rsel = sb("rsel", [HT, 2, 4, E])
        rowf = sb("rowf", [HT, 2, 4])
        rowi = sb("rowi", [HT, 2, 4], U32)
        tokf = sb("tokf", [HT, 4])
        slot_rows = sb("slot_rows", [HT, 4, 2, ROW])
        cnt = sb("cnt", [1, E])
        tcmp = sb("tcmp", [1, E, 23])
        nblk = sb("nblk", [1, E])
        tcum = sb("tcum", [1, E, E])
        ends = sb("ends", [1, E])
        tge = sb("tge", [1, BLOCKS, E])
        twt = sb("twt", [1, E])
        trow = sb("trow", [1, BLOCKS, E])
        tabf = sb("tabf", [1, 2 * BLOCKS + E])
        tabi = sb("tabi", [1, 2 * BLOCKS + E], I32)
        xs = [sb(f"xs{i}", [128, ROW]) for i in range(4)]
        sxa = [sb(f"sxa{i}", [128, 128]) for i in range(2)]
        sxt = [sb(f"sxt{i}", [CT + 1, 128]) for i in range(2)]
        relu = [stage_s[:, 0:H], stage_s[:, H:2 * H]]
        hid = [stage_h[:, 0:H], stage_h[:, H:2 * H]]
        flat = work[:].rearrange("p a t -> p (a t)")
        hidT = flat[:, 0:H].rearrange("p (k t) -> p k t", k=HC)
        ysum = [flat[:, H + i * C:H + (i + 1) * C] for i in range(2)]
        ygate = [flat[:, H + (2 + i) * C:H + (3 + i) * C] for i in range(2)]

        pS = [pb(f"pS{i}", [128, 512]) for i in range(2)]
        pT = [pb(f"pT{i}", [128, 512]) for i in range(2)]
        pX = pb("pX", [128, 512])
        pQ = pb("pQ", [128, 512])
        pR = pb("pR", [128, 512])
        pV = pb("pV", [128, 512])

        def p_rank(): return pV[0:HT, 464:464 + 4 * E]

        s_kon, s_x, s_tw, s_wq, s_wo, s_sm = (sem(n) for n in ("s_kon", "s_x", "s_tw", "s_wq", "s_wo", "s_sm"))
        s_emb_st, s_hd, s_pad0, s_zero, s_dummy = (sem(n) for n in ("s_emb_st", "s_hd", "s_pad0", "s_zero", "s_dummy"))
        s_wl = sem("expert_loaded")
        v_pre, a_pre, t_pre, g_pre = sem("v_pre"), sem("a_pre"), sem("t_pre"), sem("g_pre")
        hA_in, hR_in = sems("hA_in", 2), sems("hR_in", 2)
        qk_out, qk_in, m_out, m_in = sems("qk_out", 2), sems("qk_in", 2), sems("m_out", 2), sems("m_in", 2)
        h2_out = sems("h2_out", 2)
        (ln1_st, ln1_mv, ln1_pe, ln1_pow, xn_ok, ln2_st, ln2_mv, ln2_pe, ln2_pow, xn2_ok) = (sem(n) for n in (
            "ln1_st", "ln1_mv", "ln1_pe", "ln1_pow", "xn_ok", "ln2_st", "ln2_mv", "ln2_pe", "ln2_pow", "xn2_ok"))
        (xT_ps, xT_hi, xT_lo, v_ps, v_ok, qk_ps, qk_hi_ok, qk_lo_ok, mT_ps, mT_ok, o_cp, o_sh, o_rc, o_ok,
         y_ps, h2_ok) = (sem(n) for n in (
             "xT_ps", "xT_hi", "xT_lo", "v_ps", "v_ok", "qk_ps", "qk_hi_ok", "qk_lo_ok", "mT_ps", "mT_ok",
             "o_cp", "o_sh", "o_rc", "o_ok", "y_ps", "h2_ok"))
        s_ps, mx_ok, st_ps, ex_ok, pv_ok = (sems(n, UR) for n in ("s_ps", "mx_ok", "st_ps", "ex_ok", "pv_ok"))
        x2T_ps, x2T_ok, rt_ps, rt_cp, rt_sq, rt_ss, rt_pow = (sem(n) for n in (
            "x2T_ps", "x2T_ok", "rt_ps", "rt_cp", "rt_sq", "rt_ss", "rt_pow"))
        rl = sems("route", 24)
        (dl_ok, ed_ok, hot_ok, rank_ps, row_ok, sc_done, wprep) = (sem(n) for n in (
            "dl_ok", "ed_ok", "hot_ok", "rank_ps", "row_ok", "sc_done", "wprep"))
        wstep, settled = sem("wstep"), sem("settled")
        cnt_ps, tab_ok, tch, pad_done = (sem(n) for n in ("cnt_ps", "tab_ok", "tch", "pad_done"))
        (sx_ps, sx_ok, u_ps, relu_ok, hid_ok, hT_ps, hT_a, hT_v, y2_ps, ys_ok, yg_ok, add_done) = (
            sem(n) for n in ("sx_ps", "sx_ok", "u_ps", "relu_ok", "hid_ok", "hT_ps", "hT_a",
                             "hT_v", "y2_ps", "ys_ok", "yg_ok", "add_done"))
        xs_in = sems("xs_in", 4)

        FIRST, LAST = -1, 20
        LOOP0, LOOP1 = 3, 7

        def settle(eng):
            eng.sem_inc(settled, 1)

        def run_steps(eng, step):
            for s in range(FIRST, 2 * LOOP0):
                step(s // 2, s % 2, s)
            with eng.Fori(LOOP0, LOOP1) as t:
                step(t, 0, None)
                step(t, 1, None)
            for s in range(2 * LOOP1, LAST + 1):
                step(s // 2, s % 2, s)

        def batch(q, par, off, s):
            if s is not None and not 0 <= s + off < B:
                return None
            return q + (par + off) // 2, (par + off) % 2

        def n(b, back=0):
            return 2 * b[0] + b[1] + 1 - back

        def un(b, u, back=0):
            return UNITS // UR * (n(b, back) - 1) + u // UR + 1

        def first(b, k=1):
            return isinstance(b[0], int) and 2 * b[0] + b[1] < k

        w1 = [w_fast1, w_slow1, h_fast1]
        w2 = [w_fast2, w_slow2, h_fast2]
        xp = experts[0:NTOK, 4, 0:2688]
        xp3 = experts[0:NTOK, 4:6, :].rearrange("p a w -> p (a w)")[:, 0:3 * PS * PS * GRID]
        xq3 = experts[0:NTOK, 6:8, :].rearrange("p a w -> p (a w)")[:, 0:3 * PS * PS * GRID]
        tokw = experts[:, 3, 0:KC * C].rearrange("p (k n) -> p k n", k=KC)
        pT_sb = experts[:, 2, 0:KC * NTOK * 2].rearrange("p (r k n) -> p r k n", r=2, k=KC)
        emb = experts[0:NTOK, 1, 0:GRID * C].rearrange("p (w n) -> p w n", w=GRID)
        tokb = experts[0:NTOK, 1, GRID * C:GRID * C + C]
        wqk_in = stage_s[:, 0:3 * 256].rearrange("p (g c) -> p g c", g=3)
        wv_in = stage_s[0:96, 3 * 256:5 * 256].rearrange("p (g c) -> p g c", g=2)
        wo_in = stage_s[0:96, 1536:1536 + 2 * 384].rearrange("p (e w) -> p e w", e=2)
        r_in = stage_h[0:E, 0:C]
        pr_in = stage_h[0:DR, C:2 * C]
        em_in = stage_h[0:E, 2 * C:2 * C + DR]
        r_sc = stage_h[0:E, 512:560]
        nT_sb = stage_h[0:DR, 560:568]
        fe_in = stage_h[0:HT, 576:592]
        small_loads = 16
        PRE_EMB = 2 * GRID
        PRE_WQ0 = PRE_EMB + 2
        PRE_SS = PRE_WQ0 + 4
        PRE_EMBN = PRE_SS + 5
        PRE_NT = PRE_EMBN + 1
        PRE_V = PRE_NT + 4
        PRE_STAGE, PRE_T, PRE_G = 10, 2 * GRID + 5, 3
        block = ctx.enter_context(nc.Block())

        @block.sync
        def _(sp):
            for b in range(B):
                sp.dma_start(xp3[b * GRID:(b + 1) * GRID, :].rearrange("p (c w) -> p c w", c=3),
                             x[b].rearrange("c (h i) w -> h c (i w)", i=PS)).then_inc(s_x, 16)
            sp.dma_start(kon[:], shape_consts).then_inc(s_kon, 16)
            sp.dma_start(tokw, tok_w.rearrange("(k p) n -> p k n", p=128)).then_inc(s_tw, 16)
            sp.dma_start(tokb, tok_b.rearrange("(a n) -> a n", a=1).to_broadcast([NTOK, C])).then_inc(s_tw, 16)
            for qk in range(2):
                for pp in range(2):
                    src = w_qkv[(2 * qk + pp) * 96:(2 * qk + pp + 1) * 96, :].rearrange("(i x) c -> x i c", i=3)
                    rows = slice(64 * qk + pp, 64 * qk + 64, 2)
                    sp.dma_start(wqk_in[rows, :, 0:C], src).then_inc(s_wq, 16)
                    sp.dma_start(wqk_in[rows, :, C:256], src[:, :, CA:C]).then_inc(s_wq, 16)
            wv_rows = w_qkv[2 * C:3 * C, :].rearrange("(g p) c -> p g c", p=96)
            sp.dma_start(wv_in[:, :, 0:C], wv_rows).then_inc(s_wq, 16)
            sp.dma_start(wv_in[:, :, C:256], wv_rows[:, :, CA:C]).then_inc(s_wq, 16)
            hd3 = h_dram.rearrange("(b t) c -> b t c", t=T)
            sp.dma_start(hd3[:, 0, :], cls[0].to_broadcast([B, C])).then_inc(s_hd, 16)
            sp.dma_start(hd3[:, 1 + NPATCH:T, :], txt).then_inc(s_hd, 16)
            sp.wait_ge(g_pre, 1)
            for eh in range(2):
                for g in range(3):
                    dst = wo_in[:, eh, g * 128:(g + 1) * 128].rearrange("p (j d) -> p j d", d=32)[:, :, 0:HD]
                    src = w_out[eh * 96:(eh + 1) * 96, g * 64:(g + 1) * 64].rearrange("p (j d) -> p j d", d=HD)
                    sp.dma_start(dst, src).then_inc(s_wo, 16)
                sp.dma_start(wo_in[:, eh, HD:HD + 1], b_out.rearrange("(e p a) -> e p a", p=96, a=1)[eh],
                             allow_slow_non_contiguous=True).then_inc(s_wo, 16)
            sp.dma_start(r_in, router_w).then_inc(s_sm, 16)
            sp.dma_start(pr_in, probe_w).then_inc(s_sm, 16)
            sp.dma_start(em_in, router_emb).then_inc(s_sm, 16)
            sp.dma_start(fe_in[:, 0:E], energy.rearrange("(a n) -> a n", a=1).to_broadcast([HT, E])).then_inc(s_sm, 16)
            sp.dma_start(fe_in[:, E:2 * E], fatigue.rearrange("(a n) -> a n", a=1).to_broadcast([HT, E])).then_inc(s_sm, 16)
            sp.dma_start(mg[:, 0, :], m_gate1.rearrange("(a n) -> a n", a=1).to_broadcast([128, E])).then_inc(s_sm, 16)
            sp.dma_start(mg[:, 1, :], m_gate2.rearrange("(a n) -> a n", a=1).to_broadcast([128, E])).then_inc(s_sm, 16)
            sp.dma_start(b2_bc[:], b2.rearrange("(a e) n -> a (e n)", a=1).to_broadcast([128, E * C]).rearrange(
                "p (e n) -> p e n", e=E)).then_inc(s_sm, 16)
            for qk in range(2):
                for pp in range(2):
                    src = b_qkv[(2 * qk + pp) * 96:(2 * qk + pp + 1) * 96].rearrange("(i x a) -> x i a", i=3, a=1)
                    sp.dma_start(bqk[64 * qk + pp:64 * qk + 64:2].unsqueeze(2), src,
                                 allow_slow_non_contiguous=True).then_inc(s_sm, 16)
            for a in range(2):
                sp.dma_start(bv_bc[:, a, :], b_qkv[2 * C:3 * C].rearrange("(a n) -> a n", a=1).to_broadcast([HT, C])).then_inc(s_sm, 16)
            sp.dma_start(empty[:], empty_slots).then_inc(s_sm, 16)
            sp.dma_start(tokf[:], shape_consts[0:HT, K_TOK:K_TOK + 4]).then_inc(s_sm, 16)
            sp.wait_ge(s_sm, 16 * small_loads)
            for k in range(8):
                r0 = E * CAP + 128 * k
                sp.dma_start(slots_dram[r0:r0 + 128, :], empty[:]).then_inc(s_dummy, 16)
            sp.dma_start(out[N:N + 128, :], empty[:, 0:C]).then_inc(s_dummy, 16)
            sp.wait_ge(v_pre, PRE_EMB)
            hdp = hd3[:, 1:1 + NPATCH, :].rearrange("b (h w) c -> b h w c", h=GRID)
            sp.dma_start(emb_dram, emb).then_inc(s_emb_st, 16)
            sp.wait_ge(s_emb_st, 16)
            sp.dma_start(hd3[:, 1:1 + NPATCH, :], emb_dram.rearrange("(b h) w c -> b (h w) c", h=GRID)).then_inc(s_hd, 16)
            sp.wait_ge(s_hd, 48)

            def load_hA(b):
                if not first(b, 2):
                    sp.wait_ge(xn_ok, n(b, 2))
                sp.dma_start(hA[b[1]][:], h_dram[bass.ds((2 * b[0] + b[1]) * T, T), :].rearrange(
                    "(a p) c -> p a c", a=2)).then_inc(hA_in[b[1]], 16)

            def load_experts(e):
                for i, (dst, wA, wB) in enumerate(zip((experts[:, e, :], stage_s, stage_h), w1, w2)):
                    ee = bass.ds(e, 1)
                    A = wA[ee].rearrange("a k h -> (a k) h")
                    Z = wB[ee].rearrange("a (k p) c -> p (a k) c", p=128)
                    sp.dma_start(dst[:, 0:H], A[0:CA, :]).then_inc(s_wl, 16)
                    sp.dma_start(dst[0:CT, H:2 * H], A[CA:C, :]).then_inc(s_wl, 16)
                    sp.dma_start(dst[:, 2 * H:].rearrange("p (k c) -> p k c", k=HC), Z).then_inc(s_wl, 16)
                sp.dma_start(experts[CT:CT + 1, e, H:2 * H], b1[bass.ds(e, 1), :]).then_inc(s_wl, 16)

            def step(q, par, s):
                a2, f, m, bk = (batch(q, par, o, s) for o in (2, 0, -1, -2))
                r = batch(q, par, -1, s)
                if s == FIRST:
                    load_hA((0, 0))
                if r:
                    if not first(r, 2):
                        sp.wait_ge(xn2_ok, n(r, 2))
                        settle(sp)
                        sp.wait_ge(h2_out[r[1]], 16 * r[0])
                    sp.dma_start(hR[r[1]][:], h_dram[bass.ds((2 * r[0] + r[1]) * T, T), :].rearrange(
                        "(a p) c -> p a c", a=2)).then_inc(hR_in[r[1]], 16)
                if a2:
                    load_hA(a2)
                if par == 1 and (s is None or -1 <= s < 15):
                    e = q + 1
                    if s is None or s > 0:
                        sp.wait_ge(wprep, e)
                    else:
                        sp.wait_ge(a_pre, PRE_STAGE)
                        sp.wait_ge(t_pre, PRE_T)
                        sp.wait_ge(v_pre, PRE_V)
                        sp.wait_ge(g_pre, PRE_G)
                    load_experts(e)
                if m:
                    sp.wait_ge(mT_ok, n(m))
                    sp.dma_start(m_dram[m[1]], mT[:].bitcast(F32)).then_inc(m_out[m[1]], 16)
                if f:
                    d = qk_dram[f[1]]
                    sp.wait_ge(qk_hi_ok, 3 * n(f))
                    settle(sp)
                    if not first(f, 2):
                        sp.wait_ge(qk_in[f[1]], 64 * f[0])
                        settle(sp)
                        sp.wait_ge(qk_out[f[1]], 96 * f[0])
                    qk_rows = lambda tile, i: tile[64 * i:64 * i + 64].rearrange("x c t -> x (c t)").bitcast(F32)
                    d_rows = lambda i, g: d[i, g].rearrange("x (w y) -> (x w) y", w=2)
                    for i, g in ((0, 0), (0, 2), (1, 0), (1, 1)):
                        sp.dma_start(d_rows(i, g), qk_rows(qk_hi, i)).then_inc(qk_out[f[1]], 16)
                    sp.wait_ge(qk_lo_ok, 3 * n(f))
                    for i, g in ((0, 1), (1, 2)):
                        sp.dma_start(d_rows(i, g), qk_rows(qk_lo, i)).then_inc(qk_out[f[1]], 16)
                if bk:
                    sp.wait_ge(h2_ok, n(bk))
                    sp.dma_start(out[bass.ds((2 * bk[0] + bk[1]) * T, T), :].rearrange("(a p) c -> p a c", a=2),
                                 hR[bk[1]][:]).then_inc(h2_out[bk[1]], 16)

            run_steps(sp, step)
            sp.wait_ge(tab_ok, 1)
            sp.wait_ge(sc_done, 16 * TOPK * 2 * B)
            for e in range(E):
                row = sp.value_load(tabi[0:1, 2 * BLOCKS + e:2 * BLOCKS + e + 1], min_val=0, max_val=E * CAP)
                sp.dma_start(slots_dram[bass.ds(row, 128), :], empty[:]).then_inc(pad_done, 16)
                sp.wait_ge(pad_done, 16 * (e + 1))

            def load_tile(j, r, guard):
                row = sp.value_load(tabi[0:1, bass.ds(j, 1)], min_val=0, max_val=ROWS - 128)
                if guard:
                    sp.wait_ge(add_done, 16 * (j - 3))
                sp.dma_start(xs[r][:], slots_dram[bass.ds(row, 128), :]).then_inc(xs_in[r], 16)
            for r in range(4):
                load_tile(r, r, False)
            with sp.Fori(1, BLOCKS // 4) as t:
                for r in range(4):
                    load_tile(4 * t + r, r, True)
            for p in range(2):
                sp.wait_ge(h2_out[p], 16 * B // 2)

        @block.tensor
        def _(pe):
            mm = nc.tensor.matmul
            tr = nc.tensor.transpose
            pe.wait_ge(s_kon, 16)
            pe.wait_ge(s_tw, 32)
            pe.wait_ge(a_pre, 3)
            for w in range(GRID):
                base = w * KC * 128
                if w:
                    pe.wait_ge(v_pre, 2 * w)
                for k in range(KC):
                    bank = pS[0] if k < 3 else pS[1]
                    last = tr(bank[:, (k % 3) * NTOK:(k % 3 + 1) * NTOK], xq3[:, base + k * 128:base + (k + 1) * 128],
                              ident[0:NTOK, 0:NTOK])
                last.then_inc(t_pre, 1)
                pe.wait_ge(v_pre, 2 * w + 1)
                for k in range(KC):
                    last = mm(pT[w % 2][0:NTOK, 0:C], pT_sb[:, w % 2, k, :], tokw[:, k, :], start=(k == 0), stop=(k == KC - 1))
                last.then_inc(t_pre, 1)
            pe.wait_ge(a_pre, 4)
            for g in range(3):
                tr(pS[0][:, g * 128:(g + 1) * 128], wqk_in[:, g, 0:128], ident)
                last = tr(pS[1][:, g * 128:(g + 1) * 128], wqk_in[:, g, 128:256], ident)
            last.then_inc(t_pre, 1)
            pe.wait_ge(v_pre, PRE_WQ0)
            for g in range(2):
                tr(pS[0][:, g * 96:(g + 1) * 96], wv_in[:, g, 0:128], ident[0:96, 0:96])
                last = tr(pS[1][:, g * 96:(g + 1) * 96], wv_in[:, g, 128:256], ident[0:96, 0:96])
            last.then_inc(t_pre, 1)
            pe.wait_ge(s_wo, 16 * 8)
            for eh in range(2):
                for g in range(3):
                    last = tr(pQ[:, g * 96:(g + 1) * 96] if eh == 0 else pR[:, g * 96:(g + 1) * 96],
                              wo_in[:, eh, g * 128:(g + 1) * 128], ident[0:96, 0:96])
            last.then_inc(t_pre, 1)
            pe.wait_ge(v_pre, PRE_EMBN)
            tr(pX[0:DR, 448:448 + E], em_in, ident[0:E, 0:E]).then_inc(t_pre, 1)
            pe.wait_ge(v_pre, PRE_NT)
            for c, (c0, w) in enumerate(((0, CA), (CA, CT))):
                tr(pV[0:w, c * 64:c * 64 + E], r_in[:, c0:c0 + w], ident[0:E, 0:E])
                tr(pV[0:w, c * 64 + 16:c * 64 + 16 + DR], pr_in[:, c0:c0 + w], ident[0:DR, 0:DR])
                last = mm(pV[0:w, c * 64 + 8:c * 64 + 16], pr_in[:, c0:c0 + w], nT_sb, start=True, stop=True)
            last.then_inc(t_pre, 1)

            def step(q, par, s):
                f, m, bk, r1 = (batch(q, par, o, s) for o in (0, -1, -2, -3))
                r2 = par == 1 and (s is None or 0 <= (s - 5) // 2 < B // 2)
                pair = q - 2

                def values(u):
                    p, a = u // 2, u % 2
                    pe.wait_ge(ex_ok[(u) % UR], un(bk, u))
                    if u == 0:
                        pe.wait_ge(v_ok, n(bk))
                        if s is None or s - 1 < B:
                            pe.wait_ge(qk_hi_ok, 3 * (n(bk) + 1))
                            pe.wait_ge(qk_lo_ok, 3 * (n(bk) + 1))
                        else:
                            pe.wait_ge(o_cp, 2 * n(bk, 1))
                    for hh in range(2):
                        h = 2 * p + hh
                        g, j = h // 4, h % 4
                        dst = (pQ[:, g * T:(g + 1) * T] if g < 2 else pR[:, 0:T])[32 * j:32 * j + 32]
                        last = mm(dst, vaug[bk[1]][:, a, h, :], probs[:, u % 2, hh, :], start=(a == 0), stop=(a == 1))
                    last.then_inc(pv_ok[u % UR], 1)

                for u in range(UNITS):
                    p, a = u // 2, u % 2
                    if m:
                        if u == 0:
                            pe.wait_ge(qk_in[m[1]], 64 * m[0] + 64)
                            if not first(m):
                                pe.wait_ge(mT_ok, n(m, 1))
                            else:
                                pe.wait_ge(v_pre, PRE_V)
                        elif u == 1:
                            if not first(m):
                                pe.wait_ge(mx_ok[(UNITS - 1) % UR], un(m, UNITS - 1, 1))
                        else:
                            pe.wait_ge(mx_ok[(u - 2) % UR], un(m, u - 2))
                        mm(pS[u % 2][0:HT, 0:2 * T], qpack[m[1]][0:96, p, a * HT:(a + 1) * HT], kdiag[m[1]][0:96, p, :, :],
                           start=True, stop=True).then_inc(s_ps[u % UR], 1)
                    if bk:
                        if u == 0:
                            pe.wait_ge(m_in[bk[1]], 16 * bk[0] + 16)
                        if u < 2:
                            if not first(bk):
                                pe.wait_ge(ex_ok[(UNITS - 2 + u) % UR], un(bk, UNITS - 2 + u, 1))
                        else:
                            pe.wait_ge(ex_ok[(u - 2) % UR], un(bk, u - 2))
                        for hh in range(2):
                            last = mm(pT[u % 2][0:HT, hh * T:(hh + 1) * T], kdiag[bk[1]][0:98, p, hh, a * HT:(a + 1) * HT],
                                      qpack[bk[1]][0:98, p, :], start=True, stop=True)
                        last.then_inc(st_ps[u % UR], 1)
                        if u:
                            values(u - 1)
                    if u == 3 and r1:
                        pe.wait_ge(xn2_ok, n(r1))
                        if f:
                            if not first(f):
                                pe.wait_ge(xT_lo, n(f, 1))
                                pe.wait_ge(xT_hi, n(f, 1))
                        for a_ in range(2):
                            tr(pX[:, a_ * HT:(a_ + 1) * HT], xn2[:, r1[1], a_, 0:CA], ident[0:HT, 0:HT])
                            last = tr(pX[0:CT, T + a_ * HT:T + (a_ + 1) * HT], xn2[:, r1[1], a_, CA:C], ident[0:HT, 0:HT])
                        last.then_inc(x2T_ps, 1)
                    if u == 6 and r1:
                        pe.wait_ge(x2T_ok, n(r1))
                        pe.wait_ge(h2_ok, n(r1))
                        for a_ in range(2):
                            dst = pV[0:HT, 384 + a_ * RC:384 + (a_ + 1) * RC]
                            mm(dst, xn2T[:, 0, a_ * HT:(a_ + 1) * HT], wroute[:, 0, :], start=True, stop=False)
                            last = mm(dst, xn2T[0:CT, 1, a_ * HT:(a_ + 1) * HT], wroute[0:CT, 1, :], start=False, stop=True)
                        last.then_inc(rt_ps, 1)
                    if u == 9 and f:
                        pe.wait_ge(xn_ok, n(f))
                        if r1:
                            pe.wait_ge(x2T_ok, n(r1))
                        for a_ in range(2):
                            tr(pX[:, a_ * HT:(a_ + 1) * HT], xn[:, a_, 0:CA], ident[0:HT, 0:HT])
                            last = tr(pX[:, T + a_ * HT:T + (a_ + 1) * HT], xn[:, a_, CA:256 - 0], ident[0:HT, 0:HT])
                        last.then_inc(xT_ps, 1)
                if r2:
                    pe.wait_ge(rl[17], 4 * (pair + 1))
                    pe.wait_ge(rt_cp, n(r1) if r1 else B)
                    mm(p_rank(), kon[0:HT, K_TRI:K_TRI + HT], hot[:, 0, :, :], start=True, stop=False)
                    mm(p_rank(), kon[0:HT, K_TRI:K_TRI + HT], hot[:, 1, :, :], start=False, stop=False)
                    mm(p_rank(), kon[0:HT, K_ONE:K_ONE + HT], cum[:, 0:4, :], start=False, stop=True).then_inc(rank_ps, 1)
                if bk:
                    values(UNITS - 1)
                if m:
                    pe.wait_ge(mx_ok[(UNITS - 1) % UR], un(m, UNITS - 1))
                    pe.wait_ge(mx_ok[(UNITS - 2) % UR], un(m, UNITS - 2))
                    tr(pS[0][0:2 * NH, 0:HT], mx[:].rearrange("p h k a -> p (h k a)"), ident[0:HT, 0:HT]).then_inc(mT_ps, 1)
                if f:
                    pe.wait_ge(xT_hi, n(f))
                    pe.wait_ge(xT_lo, n(f))
                    if r1:
                        pe.wait_ge(rt_cp, n(r1))
                    if r2:
                        pe.wait_ge(rl[15], pair + 1)
                    if first(f):
                        pe.wait_ge(v_pre, PRE_V)
                    else:
                        pe.wait_ge(v_ok, n(f, 1))
                    for a_ in range(2):
                        t = slice(a_ * HT, (a_ + 1) * HT)
                        o = pV[0:HT, a_ * C:(a_ + 1) * C]
                        mm(o, xa_hi[:, t], wqkv_hi[:, 2 * C:], start=True, stop=False)
                        mm(o, xa_hi[:, t], wqkv_lo[:, 2 * C:], start=False, stop=False)
                        mm(o, xa_lo[:, t], wqkv_hi[:, 2 * C:], start=False, stop=False)
                        mm(o, xt[0:CT, t], wqkv_t1[:, 2 * C:], start=False, stop=False)
                        last = mm(o, xt[:, t], wqkv_t2[:, 2 * C:], start=False, stop=True)
                    last.then_inc(v_ps, 1)
                    if bk:
                        pe.wait_ge(o_cp, 2 * n(bk))
                    elif not first(f):
                        pe.wait_ge(qk_hi_ok, 3 * n(f, 1))
                        pe.wait_ge(qk_lo_ok, 3 * n(f, 1))
                    for i in range(3):
                        w = slice(i * 128, (i + 1) * 128)
                        o = pQ[:, i * T:(i + 1) * T] if i < 2 else pR[:, 0:T]
                        mm(o, wqkv_hi[:, w], xa_hi[:], start=True, stop=False)
                        mm(o, wqkv_lo[:, w], xa_hi[:], start=False, stop=False)
                        mm(o, wqkv_hi[:, w], xa_lo[:], start=False, stop=False)
                        mm(o, wqkv_t1[:, w], xt[0:CT, :], start=False, stop=False)
                        last = mm(o, wqkv_t2[:, w], xt[:], start=False, stop=True)
                    last.then_inc(qk_ps, 1)
                if bk:
                    pe.wait_ge(o_ok, n(bk))
                    if f:
                        pe.wait_ge(v_ok, n(f))
                    elif r1:
                        pe.wait_ge(rt_cp, n(r1))
                    if not f and r2:
                        pe.wait_ge(rl[15], pair + 1)
                    for a_ in range(2):
                        for g in range(3):
                            last = mm(pV[0:HT, a_ * C:(a_ + 1) * C], o_nrm[:, g, a_ * HT:(a_ + 1) * HT], wout[:, g, :],
                                      start=(g == 0), stop=(g == 2))
                    last.then_inc(y_ps, 1)

            run_steps(pe, step)
            pe.wait_ge(rl[15], B // 2)
            pe.wait_ge(rl[17], 4 * (B // 2))
            pe.wait_ge(h2_ok, B)
            mm(pV[:, 0:E], kon[0:HT, K_ONE:K_ONE + 128], cum[:, 4, :], start=True, stop=True).then_inc(cnt_ps, 1)

            U = [pS, pT]

            def transpose_slots(j, r, t, guard):
                pe.wait_ge(xs_in[r], 16 * t + 16)
                if guard:
                    pe.wait_ge(sx_ok, 2 * j)
                tr(pX[:, 0:128], xs[r][:, 0:CA], ident)
                tr(pX[0:CT, 128:256], xs[r][:, CA:C], ident).then_inc(sx_ps, 1)

            def up(j, par, guard, ew):
                pe.wait_ge(sx_ok, 2 * j + 2)
                if guard:
                    pe.wait_ge(relu_ok, 2 * (j - 1))
                for i, (c0, w) in enumerate(((0, 512), (512, 256))):
                    o = U[i][par][:, 0:w]
                    mm(o, sxa[par][:], experts[:, bass.ds(ew, 1), c0:c0 + w].rearrange("p a w -> p (a w)"), start=True, stop=False)
                    last = mm(o, sxt[par][:], experts[0:CT + 1, bass.ds(ew, 1), H + c0:H + c0 + w].rearrange("p a w -> p (a w)"),
                              start=False, stop=True)
                last.then_inc(u_ps, 1)

            def transpose_hidden(j, par, guard):
                pe.wait_ge(hid_ok, j + 1)
                if guard:
                    pe.wait_ge(hT_a, j)
                    pe.wait_ge(hT_v, j)
                for k in range(HC):
                    o = pQ if k < 3 else pR
                    last = tr(o[:, (k % 3) * 128:(k % 3 + 1) * 128], hid[par][:, k * 128:(k + 1) * 128], ident)
                last.then_inc(hT_ps, 1)

            def down(j, guard, ew):
                pe.wait_ge(hT_a, j + 1)
                pe.wait_ge(hT_v, j + 1)
                if guard:
                    pe.wait_ge(ys_ok, j)
                for k in range(HC):
                    last = mm(pV[:, 0:C], hidT[:, k, :],
                              experts[:, bass.ds(ew, 1), 2 * H + k * C:2 * H + (k + 1) * C].rearrange("p a w -> p (a w)"),
                              start=(k == 0), stop=(k == HC - 1))
                last.then_inc(y2_ps, 1)

            def expert_of(j):
                return pe.value_load(tabi[0:1, bass.ds(BLOCKS + j, 1)], min_val=0, max_val=E - 1)

            pe.wait_ge(tab_ok, 1)
            transpose_slots(0, 0, 0, False)
            e0 = expert_of(0)
            up(0, 0, False, e0)

            def ffn(t, r, guard, ahead=True):
                j, par = 4 * t + r, r % 2
                transpose_hidden(j, par, guard)
                if ahead:
                    e_next = expert_of(j + 1)
                    transpose_slots(j + 1, (r + 1) % 4, t + (r + 1) // 4, True)
                    up(j + 1, 1 - par, guard, e_next)
                down(j, guard, expert_of(j))

            for r in range(4):
                ffn(0, r, r > 0)
            with pe.Fori(1, BLOCKS // 4 - 1) as t:
                for r in range(4):
                    ffn(t, r, True)
            for r in range(4):
                ffn(BLOCKS // 4 - 1, r, True, r < 3)

        @block.scalar
        def _(act):
            sc = nc.scalar
            for c in range(3):
                act.wait_ge(s_x, 16 * B)
                src = xp3[:, c * 1792:(c + 1) * 1792].rearrange("p (i w j) -> p w i j", i=PS, w=GRID)
                dst = xq3.rearrange("p (w c i j) -> p w c i j", w=GRID, c=3, i=PS)
                if c < 3:
                    sc.copy(dst[:, :, c], src).then_inc(a_pre, 1)
            act.wait_ge(s_wq, 16 * 10)
            sc.mul(wqk_in[0:64], wqk_in[0:64], SCALE).then_inc(a_pre, 1)
            for rnd in range(2):
                act.wait_ge(t_pre, 2 * GRID + 1 + rnd)
                w = slice(0, 2 * C) if rnd == 0 else slice(2 * C, 3 * C)
                cols = w.stop - w.start
                sc.copy(wqkv_hi[:, w], pS[0][:, 0:cols]).then_inc(a_pre, 1)
                sc.copy(wqkv_t2[:, w], pS[1][:, 0:cols]).then_inc(a_pre, 1)
            act.wait_ge(t_pre, 2 * GRID + 3)
            sc.copy(wout[:, :, 0:96], pQ[:, 0:288].rearrange("p (g e) -> p g e", g=3)).then_inc(a_pre, 1)
            sc.copy(wout[:, :, 96:192], pR[:, 0:288].rearrange("p (g e) -> p g e", g=3)).then_inc(a_pre, 1)

            def step(q, par, s):
                f, bk, r1 = (batch(q, par, o, s) for o in (0, -2, -3))
                r2 = par == 1 and (s is None or 0 <= (s - 5) // 2 < B // 2)
                for u in range(UNITS):
                    if bk:
                        act.wait_ge(st_ps[(u) % UR], un(bk, u))
                        if u < 2:
                            if not first(bk):
                                act.wait_ge(pv_ok[(UNITS - 2 + u) % UR], un(bk, UNITS - 2 + u, 1))
                        else:
                            act.wait_ge(pv_ok[(u - 2) % UR], un(bk, u - 2))
                        sc.activation(probs[:, u % 2].rearrange("p h t -> p (h t)"), pT[u % 2][0:HT, 0:2 * T],
                                      ACT.Exp).then_inc(ex_ok[u % UR], 1)
                    if u == 4 and r1:
                        act.wait_ge(x2T_ps, n(r1))
                        if not first(r1):
                            act.wait_ge(rt_ps, n(r1, 1))
                        sc.copy(xn2T[:, 0, :], pX[:, 0:T])
                        sc.copy(xn2T[0:CT, 1, :], pX[0:CT, T:2 * T]).then_inc(x2T_ok, 1)
                    if u == 7 and r2:
                        act.wait_ge(dl_ok, q - 1)
                        sc.activation(edl[:], dlt[:], ACT.Exp).then_inc(ed_ok, 1)
                    if u == 10 and f:
                        act.wait_ge(xT_ps, n(f))
                        if not first(f):
                            act.wait_ge(qk_ps, n(f, 1))
                            act.wait_ge(xT_lo, n(f, 1))
                        sc.copy(xa_hi[:], pX[:, 0:T])
                        sc.copy(xt[:], pX[:, T:2 * T]).then_inc(xT_hi, 1)
                if bk:
                    act.wait_ge(pv_ok[(UNITS - 1) % UR], un(bk, UNITS - 1))
                    if not first(bk):
                        act.wait_ge(o_ok, n(bk, 1))
                    sc.copy(o_raw[:, 0:2, :], pQ[:, 0:2 * T].rearrange("p (g t) -> p g t", g=2)).then_inc(o_cp, 1)
                    sc.copy(o_raw[:, 2, :], pR[:, 0:T]).then_inc(o_cp, 1)
                if f:
                    act.wait_ge(qk_ps, n(f))
                    if not first(f):
                        pf = f[1] ^ 1
                        act.wait_ge(qk_out[pf], 96 * (f[0] - (1 if f[1] == 0 else 0)) + 96)
                    for i in range(3):
                        src = pQ[:, i * T:(i + 1) * T] if i < 2 else pR[:, 0:T]
                        sc.activation(qk_hi[:, i, :], src, ACT.Identity, bias=bqk[:, i:i + 1]).then_inc(qk_hi_ok, 1)

            act.wait_ge(v_pre, PRE_V)
            run_steps(act, step)

            def tile(j, par, guard):
                act.wait_ge(sx_ps, j + 1)
                if guard:
                    act.wait_ge(u_ps, j - 1)
                sc.copy(sxa[par][:], pX[:, 0:128]).then_inc(sx_ok, 1)
                sc.copy(sxt[par][0:CT, :], pX[0:CT, 128:256]).then_inc(sx_ok, 1)

            def relu_tile(j, par, guard):
                act.wait_ge(u_ps, j + 1)
                if guard:
                    act.wait_ge(hid_ok, j - 1)
                sc.activation(relu[par][:, 0:512], pS[par][:], ACT.Relu).then_inc(relu_ok, 1)
                sc.activation(relu[par][:, 512:768], pT[par][:, 0:256], ACT.Relu).then_inc(relu_ok, 1)

            def hidT_half(j, guard):
                act.wait_ge(hT_ps, j + 1)
                if guard:
                    act.wait_ge(y2_ps, j)
                sc.copy(hidT[:, 0:3, :], pQ[:, 0:384].rearrange("p (k t) -> p k t", k=3)).then_inc(hT_a, 1)

            act.wait_ge(tab_ok, 1)
            tile(0, 0, False)
            relu_tile(0, 0, False)

            def ffn(t, r, guard, ahead=True):
                j, par = 4 * t + r, r % 2
                hidT_half(j, guard)
                if ahead:
                    tile(j + 1, 1 - par, guard)
                    relu_tile(j + 1, 1 - par, guard)

            for r in range(4):
                ffn(0, r, r > 0)
            with act.Fori(1, BLOCKS // 4 - 1) as t:
                for r in range(4):
                    ffn(t, r, True)
            for r in range(4):
                ffn(BLOCKS // 4 - 1, r, True, r < 3)

        @block.vector
        def _(dve):
            v = nc.vector
            pre = [0]

            def p(ins):
                pre[0] += 1
                ins.then_inc(v_pre, 1)
                return pre[0]

            def pw(ins):
                dve.wait_ge(v_pre, p(ins))

            for w in range(GRID):
                dve.wait_ge(t_pre, 2 * w + 1)
                v.tensor_copy(pT_sb[:, w % 2, 0:3, :].rearrange("p k n -> p (k n)"), pS[0][:, 0:3 * NTOK])
                p(v.tensor_copy(pT_sb[:, w % 2, 3:6, :].rearrange("p k n -> p (k n)"), pS[1][:, 0:3 * NTOK]))
                dve.wait_ge(t_pre, 2 * w + 2)
                p(v.tensor_tensor(emb[:, w, :], pT[w % 2][0:NTOK, 0:C], tokb, ALU.add))
            assert pre[0] == PRE_EMB
            for rnd in range(2):
                dve.wait_ge(a_pre, 4 + 2 * rnd + 2)
                w = slice(0, 2 * C) if rnd == 0 else slice(2 * C, 3 * C)
                cols = w.stop - w.start
                v.tensor_tensor(wqkv_lo[:, w], pS[0][:, 0:cols], wqkv_hi[:, w].bitcast(F32), ALU.subtract)
                pw(v.tensor_copy(wqkv_t1[:, w], wqkv_t2[0:CT, w].bitcast(F32)))
                p(v.tensor_tensor(wqkv_t2[0:CT, w], pS[1][0:CT, 0:cols], wqkv_t1[:, w].bitcast(F32), ALU.subtract))
            assert pre[0] == PRE_WQ0 + 2
            dve.wait_ge(s_sm, 16 * small_loads)
            pw(v.tensor_tensor(r_sc[:, 24:48], em_in, em_in, ALU.mult))
            pw(v.tensor_reduce(r_sc[:, 0:1], r_sc[:, 24:48], AX.X, ALU.add))
            dve.wait_ge(g_pre, PRE_G)
            pw(v.tensor_scalar(r_sc[:, 2:3], r_sc[:, 1:2], 0.02 / C, 0.02 / C, ALU.mult, ALU.add))
            pw(v.tensor_scalar(r_sc[:, 3:4], r_sc[:, 1:2], 1e-12, None, ALU.max))
            pw(v.reciprocal(r_sc[:, 4:5], r_sc[:, 3:4]))
            pw(v.tensor_scalar(em_in, em_in, r_sc[:, 4:5], 0.02, ALU.mult, ALU.mult))
            pw(v.tensor_scalar(r_in, r_in, r_sc[:, 2:3], None, ALU.add))
            assert pre[0] == PRE_EMBN, pre[0]
            dve.wait_ge(t_pre, 2 * GRID + 4)
            p(v.tensor_copy(nT_sb, pX[0:DR, 448:448 + E]))
            assert pre[0] == PRE_NT
            pw(v.tensor_scalar(fe_in, fe_in, 0.1, None, ALU.mult))
            pw(v.tensor_tensor(fe_in[:, 0:E], fe_in[:, 0:E], fe_in[:, E:2 * E], ALU.subtract))
            pw(v.tensor_copy(bias_e[:], fe_in[:, 0:E].unsqueeze(1).to_broadcast([HT, 4, E])))
            v.tensor_scalar(bqk[0:64, :], bqk[0:64, :], SCALE, None, ALU.mult)
            v.memset(cum[:, 4, :], 0.0)
            v.memset(sxt[0][CT:CT + 1, :], 1.0)
            v.memset(sxt[1][CT:CT + 1, :], 1.0)
            for i in range(2):
                v.memset(vaug[i][:], 1.0)
            dve.wait_ge(t_pre, 2 * GRID + 5)
            v.tensor_copy(wroute[:, 0, :], pV[:, 0:RC])
            pw(v.tensor_copy(wroute[0:CT, 1, :], pV[0:CT, 64:64 + RC]))
            assert pre[0] == PRE_V, pre[0]

            def norm_stats(src, st, mv, st_sem, mv_sem, b):
                v.bn_stats(st[b[1]][:, 0, :], src[:, 0, :])
                v.bn_stats(st[b[1]][:, 1, :], src[:, 1, :]).then_inc(st_sem, 1)
                dve.wait_ge(st_sem, n(b))
                settle(dve)
                v.bn_aggr(mv[b[1]][:, 0, :], st[b[1]][:, 0, :])
                v.bn_aggr(mv[b[1]][:, 1, :], st[b[1]][:, 1, :]).then_inc(mv_sem, 1)

            def step(q, par, s):
                pr, f, m, bk, r1 = (batch(q, par, o, s) for o in (1, 0, -1, -2, -3))
                r2 = par == 1 and (s is None or 0 <= (s - 5) // 2 < B // 2)
                k = q - 1
                flat = lambda t: t.rearrange("p a e -> p (a e)")

                if r2:
                    dve.wait_ge(xn2_ok, 2 * k)
                    if s is None or s > 5:
                        dve.wait_ge(sc_done, 128 * (k - 1))
                    for c in range(2):
                        last = v.tensor_copy(slot_rows[:, :, c, 0:C], xn2[:].rearrange("p b a c -> p (b a) c"))
                    dve.wait_ge(rt_pow, 2 * k)
                    v.tensor_scalar(rinv[:], rnm[:], 1e-12, None, ALU.max).then_inc(rl[0], 1)
                    dve.wait_ge(rl[0], k)
                    v.reciprocal(rnm[:], rinv[:]).then_inc(rl[1], 1)
                    dve.wait_ge(rl[1], k)
                    v.tensor_tensor(lg2[:], rt[:, :, E:2 * E], rnm[:].unsqueeze(2).to_broadcast([HT, 4, E]), ALU.mult).then_inc(rl[2], 1)
                    dve.wait_ge(rl[2], k)
                    v.tensor_tensor(lg2[:], lg2[:], rt[:, :, 0:E], ALU.add).then_inc(rl[3], 1)
                    dve.wait_ge(rl[3], k)
                    v.tensor_tensor(lg[:], lg2[:], bias_e[:], ALU.add).then_inc(rl[4], 1)
                    dve.wait_ge(rl[4], k)
                    src = lg
                    for c in range(2):
                        o = 5 + 5 * c
                        v.tensor_reduce(top[:, c, :], src[:], AX.X, ALU.max).then_inc(rl[o], 1)
                        dve.wait_ge(rl[o], k)
                        v.tensor_tensor(cand[:], src[:], top[:, c, :].unsqueeze(2).to_broadcast([HT, 4, E]), ALU.is_equal).then_inc(rl[o + 1], 1)
                        dve.wait_ge(rl[o + 1], k)
                        v.tensor_tensor(cand[:], cand[:], kon[0:HT, K_DESC:K_DESC + 4 * E].rearrange("p (a e) -> p a e", a=4), ALU.mult).then_inc(rl[o + 2], 1)
                        dve.wait_ge(rl[o + 2], k)
                        v.tensor_reduce(cmx[:], cand[:], AX.X, ALU.max).then_inc(rl[o + 3], 1)
                        dve.wait_ge(rl[o + 3], k)
                        ins = v.tensor_tensor(hot[:, c, :, :], cand[:], cmx[:].unsqueeze(2).to_broadcast([HT, 4, E]), ALU.is_equal)
                        if c == 0:
                            ins.then_inc(rl[o + 4], 1)
                            dve.wait_ge(rl[o + 4], k)
                            v.scalar_tensor_tensor(flat(lg2[:]), flat(hot[:, 0, :, :]), -1e30, flat(lg[:]), ALU.mult, ALU.add).then_inc(rl[23], 1)
                            dve.wait_ge(rl[23], k)
                            src = lg2
                        else:
                            ins.then_inc(rl[o + 4], 1)
                            dve.wait_ge(rl[o + 4], k)
                    v.tensor_tensor(dlt[:], top[:, 1, :], top[:, 0, :], ALU.subtract).then_inc(dl_ok, 1)
                    v.tensor_tensor(flat(cand[:]), flat(hot[:, 0, :, :]), flat(hot[:, 1, :, :]), ALU.add)
                    v.tensor_copy(cum[:, 0, :], cum[:, 4, :]).then_inc(rl[16], 1)
                    dve.wait_ge(rl[16], k)
                    for i in range(4):
                        v.tensor_tensor(cum[:, i + 1, :], cum[:, i, :], cand[:, i, :], ALU.add).then_inc(rl[17], 1)
                        dve.wait_ge(rl[17], 4 * (k - 1) + i + 1)
                if r1:
                    dve.wait_ge(ln2_pow, n(r1))
                    if not first(r1, 2):
                        dve.wait_ge(x2T_ps, n(r1, 2))
                    for a in range(2):
                        last = v.tensor_scalar(xn2[:, r1[1], a, :], hR[r1[1]][:, a, :], mv2[r1[1]][:, a, 0:1],
                                               rs2[r1[1]][:, a, 1:2], ALU.subtract, ALU.mult)
                    last.then_inc(xn2_ok, 1)
                if pr:
                    dve.wait_ge(hA_in[pr[1]], 16 * pr[0] + 16)
                    if not first(pr, 2):
                        dve.wait_ge(ln1_pow, n(pr, 2))
                    norm_stats(hA[pr[1]], st1, mv1, ln1_st, ln1_mv, pr)
                for u in range(UNITS):
                    if m:
                        pp, a = u // 2, u % 2
                        dve.wait_ge(s_ps[(u) % UR], un(m, u))
                        if u == 0 and not first(m):
                            dve.wait_ge(mT_ps, n(m, 1))
                        v.tensor_reduce(mx[:, :, pp, a], pS[u % 2][0:HT, 0:2 * T].rearrange("p (h t) -> p h t", h=2),
                                        AX.X, ALU.max).then_inc(mx_ok[u % UR], 1)
                    if u == 3 and f:
                        dve.wait_ge(ln1_pow, n(f))
                        if not first(f):
                            dve.wait_ge(xT_ps, n(f, 1))
                        for a in range(2):
                            v.tensor_scalar(xn[:, a, 0:C], hA[f[1]][:, a, :], mv1[f[1]][:, a, 0:1],
                                            rs1[f[1]][:, a, 1:2], ALU.subtract, ALU.mult)
                            last = v.tensor_scalar(xn[:, a, C:256], hA[f[1]][:, a, CA:C], mv1[f[1]][:, a, 0:1],
                                                   rs1[f[1]][:, a, 1:2], ALU.subtract, ALU.mult)
                        last.then_inc(xn_ok, 1)
                    if u == 8 and r1:
                        dve.wait_ge(rt_ps, n(r1))
                        sl = slice(2 * r1[1], 2 * r1[1] + 2)
                        v.tensor_copy(rt[:, sl, :], pV[0:HT, 384:384 + 2 * RC].rearrange("p (a r) -> p a r", a=2)).then_inc(rt_cp, 1)
                        dve.wait_ge(rt_cp, n(r1))
                        v.tensor_tensor(rsq[:, sl, :], rt[:, sl, 2 * E:], rt[:, sl, 2 * E:], ALU.mult).then_inc(rt_sq, 1)
                        dve.wait_ge(rt_sq, n(r1))
                        if not first(r1, 2):
                            dve.wait_ge(rt_pow, n(r1, 2))
                        v.tensor_reduce(rss[:, sl], rsq[:, sl, :], AX.X, ALU.add).then_inc(rt_ss, 1)
                    if u == 9 and r2:
                        dve.wait_ge(ed_ok, k)
                        v.tensor_scalar(rinv[:], edl[:], 1.0, None, ALU.add).then_inc(rl[18], 1)
                        dve.wait_ge(rl[18], k)
                        v.reciprocal(gates[:, 0, :], rinv[:]).then_inc(rl[19], 1)
                        dve.wait_ge(rl[19], k)
                        v.tensor_tensor(gates[:, 1, :], gates[:, 0, :], edl[:], ALU.mult).then_inc(rl[20], 1)
                        dve.wait_ge(rl[20], k)
                if r2:
                    dve.wait_ge(rank_ps, k)
                    v.tensor_tensor(rank[:].rearrange("p a e -> p (a e)"), p_rank(), kon[0:HT, K_BASE:K_BASE + 4 * E], ALU.add).then_inc(rl[15], 1)
                    dve.wait_ge(rl[15], k)
                    for c in range(2):
                        last = v.tensor_tensor(rsel[:, c, :, :], hot[:, c, :, :], rank[:], ALU.mult)
                    last.then_inc(rl[21], 1)
                    dve.wait_ge(rl[21], k)
                    v.tensor_reduce(rowf[:].rearrange("p c a -> p (c a)"), rsel[:].rearrange("p c a e -> p (c a) e"), AX.X, ALU.add).then_inc(rl[22], 1)
                    dve.wait_ge(rl[22], k)
                    v.tensor_copy(rowi[:], rowf[:])
                    for c in range(2):
                        v.tensor_copy(slot_rows[:, :, c, C:C + 1], gates[:, c, :].unsqueeze(2))
                        last = v.tensor_copy(slot_rows[:, :, c, C + 1:C + 2].bitcast(U32), tokf[:].unsqueeze(2))
                    last.then_inc(row_ok, 1)
                    dve.wait_ge(row_ok, k)
                    v.tensor_scalar(tokf[:], tokf[:], float(2 * T), None, ALU.add)
                if m:
                    dve.wait_ge(mT_ps, n(m))
                    if not first(m):
                        pm = m[1] ^ 1
                        dve.wait_ge(m_out[pm], 16 * (m[0] - (1 if m[1] == 0 else 0)) + 16)
                    v.tensor_scalar(mT[:], pS[0][0:2 * NH, 0:HT], -1.0, None, ALU.mult).then_inc(mT_ok, 1)
                if f:
                    dve.wait_ge(xT_hi, n(f))
                    v.tensor_tensor(xa_lo[:], pX[:, 0:T], xa_hi[:].bitcast(F32), ALU.subtract)
                    v.tensor_tensor(xt[CT:128, :], pX[CT:128, T:2 * T], xt[CT:128, :].bitcast(F32), ALU.subtract).then_inc(xT_lo, 1)
                if bk:
                    dve.wait_ge(o_cp, 2 * n(bk))
                    fl = lambda t: t.rearrange("p g t -> p (g t)")
                    settle(dve)
                    v.stream_shuffle(fl(o_sum), fl(o_raw), [16] * 32).then_inc(o_sh, 1)
                    dve.wait_ge(o_sh, n(bk))
                    if not first(bk):
                        dve.wait_ge(y_ps, n(bk, 1))
                    v.reciprocal(fl(o_nrm), fl(o_sum)).then_inc(o_rc, 1)
                    dve.wait_ge(o_rc, n(bk))
                    v.tensor_tensor(fl(o_nrm), fl(o_nrm), fl(o_raw), ALU.mult).then_inc(o_ok, 1)
                if f:
                    dve.wait_ge(v_ps, n(f))
                    if not first(f, 2):
                        dve.wait_ge(pv_ok[(UNITS - 1) % UR], un(f, UNITS - 1, 2))
                    v.tensor_tensor(vaug[f[1]][:].rearrange("p a h d -> p (a h) d")[:, :, 0:HD],
                                    pV[0:HT, 0:2 * C].rearrange("p (h d) -> p h d", d=HD),
                                    bv_bc[:].rearrange("p a (h d) -> p (a h) d", d=HD), ALU.add).then_inc(v_ok, 1)
                    for i in range(3):
                        dve.wait_ge(qk_hi_ok, 3 * n(f, 1) + (2 if i < 2 else 3))
                        if i == 0 and not first(f):
                            pf = f[1] ^ 1
                            dve.wait_ge(qk_out[pf], 96 * (f[0] - (1 if f[1] == 0 else 0)) + 96)
                        src = pQ[:, i * T:(i + 1) * T] if i < 2 else pR[:, 0:T]
                        v.scalar_tensor_tensor(qk_lo[:, i, :], src, bqk[:, i:i + 1], qk_hi[:, i, :].bitcast(F32),
                                               ALU.add, ALU.subtract).then_inc(qk_lo_ok, 1)
                if bk:
                    dve.wait_ge(y_ps, n(bk))
                    dve.wait_ge(hR_in[bk[1]], 16 * bk[0] + 16)
                    v.tensor_tensor(hR[bk[1]][:].rearrange("p a c -> p (a c)"), pV[0:HT, 0:2 * C],
                                    hR[bk[1]][:].rearrange("p a c -> p (a c)"), ALU.add).then_inc(h2_ok, 1)
                    dve.wait_ge(h2_ok, n(bk))
                    norm_stats(hR[bk[1]], st2, mv2, ln2_st, ln2_mv, bk)
                if par == 0 and (s is None or 0 <= s < 16):
                    dve.wait_ge(s_wl, 160 * (q + 1))
                    if s == 0:
                        dve.wait_ge(s_sm, 16 * small_loads)
                    we = experts[:, bass.ds(q, 1), :].rearrange("p a w -> p (a w)")
                    parts = ((slice(0, 128), slice(0, H), 0), (slice(0, CT), slice(H, 2 * H), 0),
                             (slice(0, 128), slice(2 * H, WCOLS), 1))
                    for rows, cols, g in parts:
                        v.scalar_tensor_tensor(we[rows, cols], stage_s[rows, cols], mg[rows, g, bass.ds(q, 1)],
                                               we[rows, cols], ALU.mult, ALU.add).then_inc(wstep, 1)
                    dve.wait_ge(wstep, 3 * (q + 1))
                    for rows, cols, g in parts:
                        last = v.tensor_tensor(we[rows, cols], we[rows, cols], stage_h[rows, cols], ALU.add)
                    last.then_inc(wprep, 1)

            run_steps(dve, step)

            links = [0]

            def link(ins):
                links[0] += 1
                ins.then_inc(tch, 1)
                dve.wait_ge(tch, links[0])
            dve.wait_ge(cnt_ps, 1)
            link(v.tensor_copy(cnt[:], pV[0:1, 0:E]))
            kk = kon[0:1, K_KK:K_KK + 23].unsqueeze(1).to_broadcast([1, E, 23])
            link(v.tensor_tensor(tcmp[:], cnt[:].unsqueeze(2).to_broadcast([1, E, 23]), kk, ALU.is_gt))
            link(v.tensor_reduce(nblk[:], tcmp[:], AX.X, ALU.add))
            link(v.tensor_tensor(tcum[:], kon[0:1, K_CUM:K_CUM + E * E].rearrange("p (a b) -> p a b", a=E),
                                 nblk[:].unsqueeze(1).to_broadcast([1, E, E]), ALU.mult))
            link(v.tensor_reduce(ends[:], tcum[:], AX.X, ALU.add))
            jj = kon[0:1, K_JJ:K_JJ + BLOCKS]
            link(v.tensor_tensor(tge[:], jj.unsqueeze(2).to_broadcast([1, BLOCKS, E]),
                                 ends[:].unsqueeze(1).to_broadcast([1, BLOCKS, E]), ALU.is_ge))
            link(v.tensor_reduce(tabf[:, BLOCKS:2 * BLOCKS], tge[:], AX.X, ALU.add))
            link(v.tensor_scalar(tabf[:, BLOCKS:2 * BLOCKS], tabf[:, BLOCKS:2 * BLOCKS], float(E - 1), None, ALU.min))
            link(v.tensor_scalar(twt[:], nblk[:], -128.0, float(CAP), ALU.mult, ALU.add))
            link(v.tensor_tensor(trow[:], tge[:], twt[:].unsqueeze(1).to_broadcast([1, BLOCKS, E]), ALU.mult))
            link(v.tensor_reduce(tabf[:, 0:BLOCKS], trow[:], AX.X, ALU.add))
            link(v.scalar_tensor_tensor(tabf[:, 0:BLOCKS], jj, 128.0, tabf[:, 0:BLOCKS], ALU.mult, ALU.add))
            link(v.tensor_tensor(tabf[:, 2 * BLOCKS:], cnt[:], kon[0:1, K_BASE:K_BASE + E], ALU.add))
            v.tensor_copy(tabi[:], tabf[:]).then_inc(tab_ok, 1)
            dve.wait_ge(tab_ok, 1)

            def square(j, par, guard):
                dve.wait_ge(relu_ok, 2 * j + 2)
                if guard:
                    dve.wait_ge(hT_ps, j - 1)
                v.tensor_tensor(hid[par], relu[par], relu[par], ALU.mult).then_inc(hid_ok, 1)

            def hidT_half(j, guard):
                dve.wait_ge(hT_ps, j + 1)
                if guard:
                    dve.wait_ge(y2_ps, j)
                v.tensor_copy(hidT[:, 3:6, :], pR[:, 0:384].rearrange("p (k t) -> p k t", k=3)).then_inc(hT_v, 1)

            def output(j, r, par, guard, e):
                dve.wait_ge(y2_ps, j + 1)
                v.tensor_tensor(ysum[par], pV[:, 0:C], b2_bc[:, bass.ds(e, 1), :].rearrange("p a c -> p (a c)"),
                                ALU.add).then_inc(ys_ok, 1)
                dve.wait_ge(ys_ok, j + 1)
                if guard:
                    dve.wait_ge(add_done, 16 * (j - 1))
                v.tensor_scalar(ygate[par], ysum[par], xs[r][:, C:C + 1], None, ALU.mult).then_inc(yg_ok, 1)

            def ffn(t, r, guard, ahead=True):
                j, par = 4 * t + r, r % 2
                hidT_half(j, guard)
                if ahead:
                    square(j + 1, 1 - par, guard)
                e = dve.value_load(tabi[0:1, bass.ds(BLOCKS + j, 1)], min_val=0, max_val=E - 1)
                output(j, r, par, guard, e)

            square(0, 0, False)
            for r in range(4):
                ffn(0, r, r > 0)
            with dve.Fori(1, BLOCKS // 4 - 1) as t:
                for r in range(4):
                    ffn(t, r, True)
            for r in range(4):
                ffn(BLOCKS // 4 - 1, r, True, r < 3)

        @block.gpsimd
        def _(pool):
            g = nc.gpsimd
            g.memset(wo_in, 0.0).then_inc(g_pre, 1)
            g.memset(kdiag[0][:].bitcast(F32), 0.0)
            g.memset(kdiag[1][:].bitcast(F32), 0.0)
            g.memset(powers[:, 0:2], -0.5)
            g.memset(powers[:, 2:4], 0.5).then_inc(g_pre, 1)
            pool.wait_ge(g_pre, 2)
            pool.wait_ge(v_pre, PRE_SS)
            g.tensor_tensor(r_sc[:, 1:2], r_sc[:, 0:1], powers[0:E, 2:3], ALU.pow).then_inc(g_pre, 1)

            def rsqrt(mv, rs, mv_sem, pe_sem, pow_sem, b):
                pool.wait_ge(mv_sem, n(b))
                settle(pool)
                g.tensor_scalar(rs[b[1]][:, :, 0:1], mv[b[1]][:, :, 1:2], 1e-5, None, ALU.add).then_inc(pe_sem, 1)
                pool.wait_ge(pe_sem, n(b))
                g.tensor_tensor(rs[b[1]][:, :, 1], rs[b[1]][:, :, 0], powers[:, 0:2], ALU.pow).then_inc(pow_sem, 1)

            def scatter(k, p):
                for i in range(4):
                    a, c = 2 * p + i // 2, i % 2
                    if not (isinstance(k, int) and k + p + i == 0):
                        pool.wait_ge(sc_done, 128 * k + 64 * p + 16 * i)
                    settle(pool)
                    g.indirect_dma_start(slots_dram, bass.IndirectOffsetOnAxis(ap=rowi[:, c, a:a + 1], axis=0),
                                         slot_rows[:, a, c, :], None).then_inc(sc_done, 16)

            def step(q, par, s):
                pr, f, m, bk, r1 = (batch(q, par, o, s) for o in (1, 0, -1, -2, -3))
                if pr:
                    if not first(pr, 2):
                        pool.wait_ge(xn_ok, n(pr, 2))
                    rsqrt(mv1, rs1, ln1_mv, ln1_pe, ln1_pow, pr)
                if par == 0 and (s is None or s >= 6):
                    scatter(q - 3, 1)
                if r1:
                    pool.wait_ge(rt_ss, n(r1))
                    if r1[1] == 0 and not first(r1, 2):
                        pool.wait_ge(rl[1], r1[0])
                    sl = slice(2 * r1[1], 2 * r1[1] + 2)
                    g.tensor_tensor(rnm[:, sl], rss[:, sl], powers[:, 2:4], ALU.pow).then_inc(rt_pow, 1)
                if bk:
                    if not first(bk, 2):
                        pool.wait_ge(xn2_ok, n(bk, 2))
                    rsqrt(mv2, rs2, ln2_mv, ln2_pe, ln2_pow, bk)
                if m:
                    pool.wait_ge(m_out[m[1]], 16 * m[0] + 16)
                    settle(pool)
                    pool.dma_start(qpack[m[1]][96:98].rearrange("h p t -> h (p t)"),
                                   m_dram[m[1]].rearrange("(h r) t -> h (r t)", h=2)).then_inc(m_in[m[1]], 16)
                if f:
                    pool.wait_ge(qk_out[f[1]], 96 * f[0] + 96)
                    if not first(f, 2):
                        pool.wait_ge(st_ps[(UNITS - 1) % UR], un(f, UNITS - 1, 2))
                    settle(pool)
                    d = qk_dram[f[1]]
                    for a in range(2):
                        rows = slice(16 * a, 16 * a + 16)
                        kd = kdiag[f[1]][48 * a:48 * a + 48, :, a, :]
                        pool.dma_start(kd, d[1, :, rows, :].rearrange("g x (p t) -> g x p t", p=PAIRS)).then_inc(qk_in[f[1]], 16)
                        pool.dma_start(qpack[f[1]][48 * a:48 * a + 48].rearrange("r p t -> r (p t)"),
                                       d[0, :, rows, :]).then_inc(qk_in[f[1]], 16)
                if par == 1 and (s is None or s >= 5):
                    pool.wait_ge(row_ok, q - 1)
                    scatter(q - 2, 0)

            for i in range(2):
                pool.dma_start(kdiag[i][96:98], head_select).then_inc(s_zero, 16)
            pool.wait_ge(s_dummy, 16 * 9)
            pool.wait_ge(s_zero, 32)
            run_steps(pool, step)
            pool.wait_ge(sc_done, 16 * 4 * B)
            for p_ in range(2):
                pool.wait_ge(h2_out[p_], 8 * B)

            def add(j, r, guard):
                pool.wait_ge(yg_ok, j + 1)
                if guard:
                    pool.wait_ge(add_done, 16 * j)
                settle(pool)
                g.indirect_dma_start(out, bass.IndirectOffsetOnAxis(ap=xs[r][:, C + 1:C + 2].bitcast(U32), axis=0),
                                     ygate[r % 2], None, compute_op=ALU.add).then_inc(add_done, 16)
            for r in range(4):
                add(r, r, r > 0)
            with pool.Fori(1, BLOCKS // 4) as t:
                for r in range(4):
                    add(4 * t + r, r, True)
            pool.wait_ge(add_done, 16 * BLOCKS)



_INS = ["x", "txt", "L0_tok_W", "L0_tok_b", "L0_tok_cls_token", "L0_attn_w_qkv", "L0_attn_b_qkv", "L0_attn_w_out",
        "L0_attn_b_out", "L0_ffn_router_w", "L0_ffn_probe_w", "L0_ffn_router_emb", "L0_ffn_fatigue", "L0_ffn_energy",
        "L0_ffn_w_fast1", "L0_ffn_w_slow1", "L0_ffn_h_fast1", "L0_ffn_m_gate1", "L0_ffn_b1", "L0_ffn_w_fast2",
        "L0_ffn_w_slow2", "L0_ffn_h_fast2", "L0_ffn_m_gate2", "L0_ffn_b2"]


def kernel(**inputs):
    import concourse.bacc as bacc
    from concourse.bass_utils import run_bass_kernel_spmd

    nc = bacc.Bacc("TRN2", target_bir_lowering=False, num_devices=1)
    arrays = {f"in_{k}": np.ascontiguousarray(inputs[k]) for k in _INS}
    arrays.update({f"const_{k}": a for k, a in shape_constants().items()})
    args = [nc.dram_tensor(k, a.shape, mybir.dt.from_np(a.dtype), kind="ExternalInput").ap() for k, a in arrays.items()]
    out = nc.dram_tensor("out_rows", [N + 128, C], F32, kind="ExternalOutput").ap()
    build_program(nc, *args, out)
    r = run_bass_kernel_spmd(nc, [arrays], core_ids=[0])
    return r.results[0]["out_rows"][:N].reshape(B, T, C)
```

```python
from contextlib import ExitStack

import numpy as np

import concourse.bass as bass
from concourse import mybir

F32 = mybir.dt.float32
F32R = mybir.dt.float32r
I32 = mybir.dt.int32
U32 = mybir.dt.uint32
ALU = mybir.AluOpType
ACT = mybir.ActivationFunctionType
AX = mybir.AxisListType

B = 16
PS = 16
GRID = 7
NPATCH = GRID * GRID
TXT = 128
T = 1 + NPATCH + TXT
HT = T // 2
N = B * T
C = 192
CA, CT = 128, 64
NH, HD = 12, 16
PAIRS = NH // 2
UNITS = 2 * PAIRS
UR = 4
KC = 3 * PS * PS // 128
E, H, TOPK, DR = 8, 768, 2, 24
HC = H // 128
CAP = N + 128
BLOCKS = (TOPK * N + E * 127) // 128
ROWS = E * CAP + 8 * 128
WCOLS = 2 * H + HC * C
ROW = C + 2
OW = -(-3 * T // 32) * 32
RC = 2 * E + DR
SCALE = HD ** -0.5
NTOK = B * GRID

K_ID, K_TRI = 0, 128
K_ONE = K_TRI + HT
K_DESC = K_ONE + 128
K_BASE = K_DESC + 4 * E
K_TOK = K_BASE + 4 * E
K_JJ = K_TOK + 4
K_KK = K_JJ + BLOCKS
K_CUM = K_KK + 23
K_COLS = K_CUM + E * E


def shape_constants():
    c = np.zeros((128, K_COLS), np.float32)
    c[:, K_ID:K_ID + 128] = np.eye(128)
    c[:HT, K_TRI:K_TRI + HT] = np.triu(np.ones((HT, HT)), 1)
    c[:, K_ONE:K_ONE + 128] = 1
    c[:, K_DESC:K_DESC + 4 * E] = np.tile(E - np.arange(E), 4)
    c[:, K_BASE:K_BASE + 4 * E] = np.tile(CAP * np.arange(E), 4)
    p = np.arange(128)
    for i in range(4):
        c[:, K_TOK + i] = (i // 2) * T + (i % 2) * HT + p
    c[:, K_JJ:K_JJ + BLOCKS] = np.arange(BLOCKS)
    c[:, K_KK:K_KK + 23] = 128 * np.arange(23)
    c[:, K_CUM:K_CUM + E * E] = np.tril(np.ones((E, E))).ravel()
    sel = np.zeros((2, PAIRS, 2, T), np.float32)
    sel[0, :, 0], sel[1, :, 1] = 1, 1
    empty = np.zeros((128, ROW), np.float32)
    empty[:, C + 1] = (N + p).astype(np.uint32).view(np.float32)
    return {"shape_consts": c, "head_select": sel, "empty_slots": empty}


def build_program(nc, x, txt, tok_w, tok_b, cls, w_qkv, b_qkv, w_out, b_out, router_w, probe_w, router_emb,
                  fatigue, energy, w_fast1, w_slow1, h_fast1, m_gate1, b1, w_fast2, w_slow2, h_fast2,
                  m_gate2, b2, shape_consts, head_select, empty_slots, out):
    ctx = ExitStack()
    with ctx:
        def sb(name, shape, dt=F32):
            return ctx.enter_context(nc.sbuf_tensor(name, shape, dt))

        def pb(name, shape, dt=F32):
            return ctx.enter_context(nc.psum_tensor(name, shape, dt))

        def sem(name):
            return ctx.enter_context(nc.semaphore(name))

        def sems(name, n):
            return [sem(f"{name}{i}") for i in range(n)]

        h_dram = nc.dram_tensor("h_tokens", [N, C], F32, kind="Internal").ap()
        qk_dram = [nc.dram_tensor(f"qk_split{i}", [2, 3, 2 * HD, PAIRS * T], F32, kind="Internal").ap() for i in range(2)]
        m_dram = [nc.dram_tensor(f"neg_max{i}", [2 * NH, HT], F32, kind="Internal").ap() for i in range(2)]
        emb_dram = nc.dram_tensor("patch_rows", [B * GRID, GRID, C], F32, kind="Internal").ap()
        slots_dram = nc.dram_tensor("slots", [ROWS, ROW], F32, kind="Internal").ap()

        kon = sb("kon", [128, K_COLS])
        ident = kon[:, K_ID:K_ID + 128]
        empty = sb("empty", [128, ROW])
        experts = sb("experts", [128, E, WCOLS])
        stage_s = sb("stage_s", [128, WCOLS])
        stage_h = sb("stage_h", [128, WCOLS])
        mg = sb("mg", [128, 2, E])
        b2_bc = sb("b2_bc", [128, E, C])
        wqkv_hi = sb("wqkv_hi", [128, 3 * C], F32R)
        wqkv_lo = sb("wqkv_lo", [128, 3 * C], F32R)
        wqkv_t1 = sb("wqkv_t1", [CT, 3 * C], F32R)
        wqkv_t2 = sb("wqkv_t2", [128, 3 * C], F32R)
        wout = sb("wout", [128, 3, C])
        wroute = sb("wroute", [128, 2, RC])
        bqk = sb("bqk", [128, 3])
        bv_bc = sb("bv_bc", [HT, 2, C])
        bias_e = sb("bias_e", [HT, 4, E])
        powers = sb("powers", [HT, 4])
        hA = [sb(f"hA{i}", [HT, 2, C]) for i in range(2)]
        hR = [sb(f"hR{i}", [HT, 2, C]) for i in range(2)]
        st1 = [sb(f"st1_{i}", [HT, 2, 6]) for i in range(2)]
        mv1 = [sb(f"mv1_{i}", [HT, 2, 2]) for i in range(2)]
        rs1 = [sb(f"rs1_{i}", [HT, 2, 2]) for i in range(2)]
        st2 = [sb(f"st2_{i}", [HT, 2, 6]) for i in range(2)]
        mv2 = [sb(f"mv2_{i}", [HT, 2, 2]) for i in range(2)]
        rs2 = [sb(f"rs2_{i}", [HT, 2, 2]) for i in range(2)]
        xn = sb("xn", [HT, 2, 256])
        xa_hi = sb("xa_hi", [128, T], F32R)
        xa_lo = sb("xa_lo", [128, T], F32R)
        xt = sb("xt", [128, T], F32R)
        qk_hi = sb("qk_hi", [128, 3, T], F32R)
        qk_lo = sb("qk_lo", [128, 3, T], F32R)
        qpack = [sb(f"qpack{i}", [98, PAIRS, T], F32R) for i in range(2)]
        kdiag = [sb(f"kdiag{i}", [98, PAIRS, 2, T], F32R) for i in range(2)]
        vaug = [sb(f"vaug{i}", [HT, 2, NH, 32]) for i in range(2)]
        vtmp = sb("vtmp", [HT, 2 * C])
        mx = sb("mx", [HT, 2, PAIRS, 2])
        mT = sb("mT", [2 * NH, HT], F32R)
        probs = sb("probs", [HT, 2, 2, T])
        work = sb("work", [128, 3, OW])
        o_raw, o_tr, o_out = (work[:, i, :] for i in range(3))
        o_nrm = o_out[:, 0:3 * T].rearrange("p (g t) -> p g t", g=3)
        osum = sb("osum", [128, OW // 32])
        xn2 = sb("xn2", [HT, 2, 2, C])
        xn2T = sb("xn2T", [128, 2, T])
        rt = sb("rt", [HT, 4, RC])
        rsq = sb("rsq", [HT, 4, DR])
        rss = sb("rss", [HT, 4])
        rnm = sb("rnm", [HT, 4])
        rinv = sb("rinv", [HT, 4])
        lg = sb("lg", [HT, 4, E])
        lg2 = sb("lg2", [HT, 4, E])
        top = sb("top", [HT, 2, 4])
        cand = sb("cand", [HT, 4, E])
        cmx = sb("cmx", [HT, 4])
        hot = sb("hot", [HT, 2, 4, E])
        cum = sb("cum", [HT, 5, E])
        dlt = sb("dlt", [HT, 4])
        edl = sb("edl", [HT, 4])
        gates = sb("gates", [HT, 2, 4])
        rank = sb("rank", [HT, 4, E])
        rsel = sb("rsel", [HT, 2, 4, E])
        rowf = sb("rowf", [HT, 2, 4])
        rowi = sb("rowi", [HT, 2, 4], U32)
        tokf = sb("tokf", [HT, 4])
        slot_rows = sb("slot_rows", [HT, 4, 2, ROW])
        cnt = sb("cnt", [1, E])
        tcmp = sb("tcmp", [1, E, 23])
        nblk = sb("nblk", [1, E])
        tcum = sb("tcum", [1, E, E])
        ends = sb("ends", [1, E])
        tge = sb("tge", [1, BLOCKS, E])
        twt = sb("twt", [1, E])
        trow = sb("trow", [1, BLOCKS, E])
        tabf = sb("tabf", [1, 2 * BLOCKS + E])
        tabi = sb("tabi", [1, 2 * BLOCKS + E], I32)
        xs = [sb(f"xs{i}", [128, ROW]) for i in range(4)]
        sxa = [sb(f"sxa{i}", [128, 128]) for i in range(2)]
        sxt = [sb(f"sxt{i}", [CT + 1, 128]) for i in range(2)]
        relu = [stage_s[:, 0:H], stage_s[:, H:2 * H]]
        hid = [stage_h[:, 0:H], stage_h[:, H:2 * H]]
        flat = work[:].rearrange("p a t -> p (a t)")
        hidT = flat[:, 0:H].rearrange("p (k t) -> p k t", k=HC)
        ysum = [flat[:, H + i * C:H + (i + 1) * C] for i in range(2)]
        ygate = [flat[:, H + (2 + i) * C:H + (3 + i) * C] for i in range(2)]

        pS = [pb(f"pS{i}", [128, 512]) for i in range(2)]
        pT = [pb(f"pT{i}", [128, 512]) for i in range(2)]
        pX = pb("pX", [128, 512])
        pQ = pb("pQ", [128, 512])
        pR = pb("pR", [128, 512])
        pV = pb("pV", [128, 512])

        def p_rank(): return pV[0:HT, 464:464 + 4 * E]

        s_kon, s_x, s_tw, s_wq, s_wo, s_sm = (sem(n) for n in ("s_kon", "s_x", "s_tw", "s_wq", "s_wo", "s_sm"))
        s_emb_st, s_hd, s_zero, s_dummy = (sem(n) for n in ("s_emb_st", "s_hd", "s_zero", "s_dummy"))
        fast_in, slow_in, hebb_in = (sem(n) for n in ("fast_in", "slow_in", "hebb_in"))
        v_pre, a_pre, t_pre, g_pre = sem("v_pre"), sem("a_pre"), sem("t_pre"), sem("g_pre")
        hA_in, hR_in = sems("hA_in", 2), sems("hR_in", 2)
        qk_out, qk_in, m_out, m_in = sems("qk_out", 2), sems("qk_in", 2), sems("m_out", 2), sems("m_in", 2)
        h2_out = sems("h2_out", 2)
        (ln1_st, ln1_mv, ln1_pe, ln1_pow, xn_ok, ln2_st, ln2_mv, ln2_pe, ln2_pow, xn2_ok) = (sem(n) for n in (
            "ln1_st", "ln1_mv", "ln1_pe", "ln1_pow", "xn_ok", "ln2_st", "ln2_mv", "ln2_pe", "ln2_pow", "xn2_ok"))
        (xT_ps, xT_hi, xT_lo, v_ps, v_ok, va_ok, qk_ps, qk_hi_ok, qk_lo_ok, mT_ps, mT_ok, o_cp, o_tr_ok, o_rc, o_mul, o_ok,
         y_ps, h2_ok) = (sem(n) for n in (
             "xT_ps", "xT_hi", "xT_lo", "v_ps", "v_ok", "va_ok", "qk_ps", "qk_hi_ok", "qk_lo_ok", "mT_ps", "mT_ok",
             "o_cp", "o_tr_ok", "o_rc", "o_mul", "o_ok", "y_ps", "h2_ok"))
        s_ps, mx_ok, st_ps, ex_ok, pv_ok = (sems(n, UR) for n in ("s_ps", "mx_ok", "st_ps", "ex_ok", "pv_ok"))
        x2T_ps, x2T_ok, rt_ps, rt_cp, rt_sq, rt_ss, rt_pow = (sem(n) for n in (
            "x2T_ps", "x2T_ok", "rt_ps", "rt_cp", "rt_sq", "rt_ss", "rt_pow"))
        rl = sems("route", 24)
        (dl_ok, ed_ok, rank_ps, row_ok, sc_done, wprep) = (sem(n) for n in (
            "dl_ok", "ed_ok", "rank_ps", "row_ok", "sc_done", "wprep"))
        slot_cp, settled = sem("slot_cp"), sem("settled")
        cnt_ps, tab_ok, tch, pad_done = (sem(n) for n in ("cnt_ps", "tab_ok", "tch", "pad_done"))
        (sx_ps, sx_ok, u_ps, relu_ok, hid_ok, hT_ps, hT_a, hT_v, y2_ps, ys_ok, yg_ok, add_done) = (
            sem(n) for n in ("sx_ps", "sx_ok", "u_ps", "relu_ok", "hid_ok", "hT_ps", "hT_a",
                             "hT_v", "y2_ps", "ys_ok", "yg_ok", "add_done"))
        xs_in = sems("xs_in", 4)

        FIRST, LAST = -1, 22
        LOOP0, LOOP1 = 4, 7

        S0 = 3

        def settle(eng):
            eng.sem_inc(settled, 1)

        def run_steps(eng, step):
            for s in range(FIRST, 2 * LOOP0):
                step(s // 2, s % 2, s)
            with eng.Fori(LOOP0, LOOP1) as t:
                step(t, 0, None)
                step(t, 1, None)
            for s in range(2 * LOOP1, LAST + 1):
                step(s // 2, s % 2, s)

        def batch(q, par, off, s):
            if s is not None and not 0 <= s + off < B:
                return None
            return q + (par + off) // 2, (par + off) % 2

        def n(b, back=0):
            return 2 * b[0] + b[1] + 1 - back

        def un(b, u, back=0):
            return UNITS // UR * (n(b, back) - 1) + u // UR + 1

        def first(b, k=1):
            return isinstance(b[0], int) and 2 * b[0] + b[1] < k

        def expert_loads(dst, wA, wB, e):
            ee = bass.ds(e, 1)
            A = wA[ee].rearrange("a k h -> (a k) h")
            return ((dst[:, 0:H], A[0:CA, :]), (dst[0:CT, H:2 * H], A[CA:C, :]),
                    (dst[:, 2 * H:].rearrange("p (k c) -> p k c", k=HC), wB[ee].rearrange("a (k p) c -> p (a k) c", p=128)))

        def expert(e):
            return experts[:, bass.ds(e, 1), :].rearrange("p a w -> p (a w)")

        xp = experts[0:NTOK, 4, 0:2688]
        xp3 = experts[0:NTOK, 4:6, :].rearrange("p a w -> p (a w)")[:, 0:3 * PS * PS * GRID]
        xq3 = experts[0:NTOK, 6:8, :].rearrange("p a w -> p (a w)")[:, 0:3 * PS * PS * GRID]
        tokw = experts[:, 3, 0:KC * C].rearrange("p (k n) -> p k n", k=KC)
        pT_sb = experts[:, 2, 0:KC * NTOK * 2].rearrange("p (r k n) -> p r k n", r=2, k=KC)
        emb = experts[0:NTOK, 1, 0:GRID * C].rearrange("p (w n) -> p w n", w=GRID)
        tokb = experts[0:NTOK, 1, GRID * C:GRID * C + C]
        wqk_in = stage_s[:, 0:3 * 256].rearrange("p (g c) -> p g c", g=3)
        wv_in = stage_s[0:96, 3 * 256:5 * 256].rearrange("p (g c) -> p g c", g=2)
        wo_in = stage_s[0:96, 1536:1536 + 2 * 384].rearrange("p (e w) -> p e w", e=2)
        r_in = stage_h[0:E, 0:C]
        pr_in = stage_h[0:DR, C:2 * C]
        em_in = stage_h[0:E, 2 * C:2 * C + DR]
        r_sc = stage_h[0:E, 512:560]
        nT_sb = stage_h[0:DR, 560:568]
        fe_in = stage_h[0:HT, 576:592]
        small_loads = 16
        PRE_EMB = 2 * GRID
        PRE_WQ0 = PRE_EMB + 2
        PRE_SS = PRE_WQ0 + 4
        PRE_EMBN = PRE_SS + 5
        PRE_NT = PRE_EMBN + 1
        PRE_V = PRE_NT + 4
        PRE_STAGE, PRE_T, PRE_G = 10, 2 * GRID + 5, 3
        block = ctx.enter_context(nc.Block())

        @block.sync
        def _(sp):
            for b in range(B):
                sp.dma_start(xp3[b * GRID:(b + 1) * GRID, :].rearrange("p (c w) -> p c w", c=3),
                             x[b].rearrange("c (h i) w -> h c (i w)", i=PS)).then_inc(s_x, 16)
            sp.dma_start(kon[:], shape_consts).then_inc(s_kon, 16)
            sp.dma_start(tokw, tok_w.rearrange("(k p) n -> p k n", p=128)).then_inc(s_tw, 16)
            sp.dma_start(tokb, tok_b.rearrange("(a n) -> a n", a=1).to_broadcast([NTOK, C])).then_inc(s_tw, 16)
            for qk in range(2):
                for pp in range(2):
                    src = w_qkv[(2 * qk + pp) * 96:(2 * qk + pp + 1) * 96, :].rearrange("(i x) c -> x i c", i=3)
                    rows = slice(64 * qk + pp, 64 * qk + 64, 2)
                    sp.dma_start(wqk_in[rows, :, 0:C], src).then_inc(s_wq, 16)
                    sp.dma_start(wqk_in[rows, :, C:256], src[:, :, CA:C]).then_inc(s_wq, 16)
            wv_rows = w_qkv[2 * C:3 * C, :].rearrange("(g p) c -> p g c", p=96)
            sp.dma_start(wv_in[:, :, 0:C], wv_rows).then_inc(s_wq, 16)
            sp.dma_start(wv_in[:, :, C:256], wv_rows[:, :, CA:C]).then_inc(s_wq, 16)
            hd3 = h_dram.rearrange("(b t) c -> b t c", t=T)
            sp.dma_start(hd3[:, 0, :], cls[0].to_broadcast([B, C])).then_inc(s_hd, 16)
            sp.dma_start(hd3[:, 1 + NPATCH:T, :], txt).then_inc(s_hd, 16)
            sp.wait_ge(g_pre, 1)
            for eh in range(2):
                for g in range(3):
                    dst = wo_in[:, eh, g * 128:(g + 1) * 128].rearrange("p (j d) -> p j d", d=32)[:, :, 0:HD]
                    src = w_out[eh * 96:(eh + 1) * 96, g * 64:(g + 1) * 64].rearrange("p (j d) -> p j d", d=HD)
                    sp.dma_start(dst, src).then_inc(s_wo, 16)
                sp.dma_start(wo_in[:, eh, HD:HD + 1], b_out.rearrange("(e p a) -> e p a", p=96, a=1)[eh],
                             allow_slow_non_contiguous=True).then_inc(s_wo, 16)
            sp.dma_start(r_in, router_w).then_inc(s_sm, 16)
            sp.dma_start(pr_in, probe_w).then_inc(s_sm, 16)
            sp.dma_start(em_in, router_emb).then_inc(s_sm, 16)
            sp.dma_start(fe_in[:, 0:E], energy.rearrange("(a n) -> a n", a=1).to_broadcast([HT, E])).then_inc(s_sm, 16)
            sp.dma_start(fe_in[:, E:2 * E], fatigue.rearrange("(a n) -> a n", a=1).to_broadcast([HT, E])).then_inc(s_sm, 16)
            sp.dma_start(mg[:, 0, :], m_gate1.rearrange("(a n) -> a n", a=1).to_broadcast([128, E])).then_inc(s_sm, 16)
            sp.dma_start(mg[:, 1, :], m_gate2.rearrange("(a n) -> a n", a=1).to_broadcast([128, E])).then_inc(s_sm, 16)
            sp.dma_start(b2_bc[:], b2.rearrange("(a e) n -> a (e n)", a=1).to_broadcast([128, E * C]).rearrange(
                "p (e n) -> p e n", e=E)).then_inc(s_sm, 16)
            for qk in range(2):
                for pp in range(2):
                    src = b_qkv[(2 * qk + pp) * 96:(2 * qk + pp + 1) * 96].rearrange("(i x a) -> x i a", i=3, a=1)
                    sp.dma_start(bqk[64 * qk + pp:64 * qk + 64:2].unsqueeze(2), src,
                                 allow_slow_non_contiguous=True).then_inc(s_sm, 16)
            for a in range(2):
                sp.dma_start(bv_bc[:, a, :], b_qkv[2 * C:3 * C].rearrange("(a n) -> a n", a=1).to_broadcast([HT, C])).then_inc(s_sm, 16)
            sp.dma_start(empty[:], empty_slots).then_inc(s_sm, 16)
            sp.dma_start(tokf[:], shape_consts[0:HT, K_TOK:K_TOK + 4]).then_inc(s_sm, 16)
            sp.wait_ge(s_sm, 16 * small_loads)
            for k in range(8):
                r0 = E * CAP + 128 * k
                sp.dma_start(slots_dram[r0:r0 + 128, :], empty[:]).then_inc(s_dummy, 16)
            sp.dma_start(out[N:N + 128, :], empty[:, 0:C]).then_inc(s_dummy, 16)
            sp.wait_ge(v_pre, PRE_EMB)
            hdp = hd3[:, 1:1 + NPATCH, :].rearrange("b (h w) c -> b h w c", h=GRID)
            sp.dma_start(emb_dram, emb).then_inc(s_emb_st, 16)
            sp.wait_ge(s_emb_st, 16)
            sp.dma_start(hd3[:, 1:1 + NPATCH, :], emb_dram.rearrange("(b h) w c -> b (h w) c", h=GRID)).then_inc(s_hd, 16)
            sp.wait_ge(s_hd, 48)

            def load_hA(b):
                if not first(b, 2):
                    sp.wait_ge(xn_ok, n(b, 2))
                sp.dma_start(hA[b[1]][:], h_dram[bass.ds((2 * b[0] + b[1]) * T, T), :].rearrange(
                    "(a p) c -> p a c", a=2)).then_inc(hA_in[b[1]], 16)

            def load_experts(e):
                for dst, src in expert_loads(expert(e), w_fast1, w_fast2, e):
                    sp.dma_start(dst, src).then_inc(fast_in, 16)
                sp.dma_start(experts[CT:CT + 1, bass.ds(e, 1), H:2 * H].rearrange("p a w -> p (a w)"),
                             b1[bass.ds(e, 1), :]).then_inc(fast_in, 16)
                for dst, src in expert_loads(stage_s, w_slow1, w_slow2, e):
                    sp.dma_start(dst, src).then_inc(slow_in, 16)

            def step(q, par, s):
                a2, f, m, bk, r1 = (batch(q, par, o, s) for o in (2, 0, -2, -3, -4))
                if s == FIRST:
                    load_hA((0, 0))
                if a2:
                    load_hA(a2)
                if bk:
                    if not first(bk, 2):
                        sp.wait_ge(xn2_ok, n(bk, 2))
                        settle(sp)
                        sp.wait_ge(h2_out[bk[1]], 16 * bk[0])
                    sp.dma_start(hR[bk[1]][:], h_dram[bass.ds((2 * bk[0] + bk[1]) * T, T), :].rearrange(
                        "(a p) c -> p a c", a=2)).then_inc(hR_in[bk[1]], 16)
                if r1:
                    sp.wait_ge(h2_ok, n(r1))
                    sp.dma_start(out[bass.ds((2 * r1[0] + r1[1]) * T, T), :].rearrange("(a p) c -> p a c", a=2),
                                 hR[r1[1]][:]).then_inc(h2_out[r1[1]], 16)
                if par == 0 and (s is None or 0 <= s < 2 * E):
                    e = q
                    if s is None or s > 0:
                        sp.wait_ge(wprep, e)
                    else:
                        sp.wait_ge(a_pre, PRE_STAGE)
                        sp.wait_ge(t_pre, PRE_T)
                        sp.wait_ge(v_pre, PRE_V)
                        sp.wait_ge(g_pre, PRE_G)
                    load_experts(e)
                if m:
                    sp.wait_ge(mT_ok, n(m))
                    sp.dma_start(m_dram[m[1]], mT[:].bitcast(F32)).then_inc(m_out[m[1]], 16)
                if f:
                    d = qk_dram[f[1]]
                    sp.wait_ge(qk_hi_ok, 3 * n(f))
                    settle(sp)
                    if not first(f, 2):
                        sp.wait_ge(qk_in[f[1]], 64 * f[0])
                        settle(sp)
                        sp.wait_ge(qk_out[f[1]], 96 * f[0])
                    qk_rows = lambda tile, i: tile[64 * i:64 * i + 64].rearrange("x c t -> x (c t)").bitcast(F32)
                    d_rows = lambda i, g: d[i, g].rearrange("x (w y) -> (x w) y", w=2)
                    for i, g in ((0, 0), (0, 2), (1, 0), (1, 1)):
                        sp.dma_start(d_rows(i, g), qk_rows(qk_hi, i)).then_inc(qk_out[f[1]], 16)
                    sp.wait_ge(qk_lo_ok, 3 * n(f))
                    for i, g in ((0, 1), (1, 2)):
                        sp.dma_start(d_rows(i, g), qk_rows(qk_lo, i)).then_inc(qk_out[f[1]], 16)
            run_steps(sp, step)
            sp.wait_ge(tab_ok, 1)
            for e in range(E):
                row = sp.value_load(tabi[0:1, 2 * BLOCKS + e:2 * BLOCKS + e + 1], min_val=0, max_val=E * CAP)
                sp.dma_start(slots_dram[bass.ds(row, 128), :], empty[:]).then_inc(pad_done, 16)
            sp.wait_ge(pad_done, 16 * E)
            sp.wait_ge(sc_done, 16 * TOPK * 2 * B)

            def load_tile(j, r, guard):
                row = sp.value_load(tabi[0:1, bass.ds(j, 1)], min_val=0, max_val=ROWS - 128)
                if guard:
                    sp.wait_ge(add_done, 16 * (j - 3))
                sp.dma_start(xs[r][:], slots_dram[bass.ds(row, 128), :]).then_inc(xs_in[r], 16)
            for r in range(4):
                load_tile(r, r, False)
            with sp.Fori(1, BLOCKS // 4) as t:
                for r in range(4):
                    load_tile(4 * t + r, r, True)
            for p in range(2):
                sp.wait_ge(h2_out[p], 16 * B // 2)

        @block.tensor
        def _(pe):
            mm = nc.tensor.matmul
            tr = nc.tensor.transpose
            pe.wait_ge(s_kon, 16)
            pe.wait_ge(s_tw, 32)
            pe.wait_ge(a_pre, 3)
            for w in range(GRID):
                base = w * KC * 128
                if w:
                    pe.wait_ge(v_pre, 2 * w)
                for k in range(KC):
                    bank = pS[0] if k < 3 else pS[1]
                    last = tr(bank[:, (k % 3) * NTOK:(k % 3 + 1) * NTOK], xq3[:, base + k * 128:base + (k + 1) * 128],
                              ident[0:NTOK, 0:NTOK])
                last.then_inc(t_pre, 1)
                pe.wait_ge(v_pre, 2 * w + 1)
                for k in range(KC):
                    last = mm(pT[w % 2][0:NTOK, 0:C], pT_sb[:, w % 2, k, :], tokw[:, k, :], start=(k == 0), stop=(k == KC - 1))
                last.then_inc(t_pre, 1)
            pe.wait_ge(a_pre, 4)
            for g in range(3):
                tr(pS[0][:, g * 128:(g + 1) * 128], wqk_in[:, g, 0:128], ident)
                last = tr(pS[1][:, g * 128:(g + 1) * 128], wqk_in[:, g, 128:256], ident)
            last.then_inc(t_pre, 1)
            pe.wait_ge(v_pre, PRE_WQ0)
            for g in range(2):
                tr(pS[0][:, g * 96:(g + 1) * 96], wv_in[:, g, 0:128], ident[0:96, 0:96])
                last = tr(pS[1][:, g * 96:(g + 1) * 96], wv_in[:, g, 128:256], ident[0:96, 0:96])
            last.then_inc(t_pre, 1)
            pe.wait_ge(s_wo, 16 * 8)
            for eh in range(2):
                for g in range(3):
                    last = tr(pQ[:, g * 96:(g + 1) * 96] if eh == 0 else pR[:, g * 96:(g + 1) * 96],
                              wo_in[:, eh, g * 128:(g + 1) * 128], ident[0:96, 0:96])
            last.then_inc(t_pre, 1)
            pe.wait_ge(v_pre, PRE_EMBN)
            tr(pX[0:DR, 448:448 + E], em_in, ident[0:E, 0:E]).then_inc(t_pre, 1)
            pe.wait_ge(v_pre, PRE_NT)
            for c, (c0, w) in enumerate(((0, CA), (CA, CT))):
                tr(pV[0:w, c * 64:c * 64 + E], r_in[:, c0:c0 + w], ident[0:E, 0:E])
                tr(pV[0:w, c * 64 + 16:c * 64 + 16 + DR], pr_in[:, c0:c0 + w], ident[0:DR, 0:DR])
                last = mm(pV[0:w, c * 64 + 8:c * 64 + 16], pr_in[:, c0:c0 + w], nT_sb, start=True, stop=True)
            last.then_inc(t_pre, 1)

            def step(q, par, s):
                f, g, m, bk, r1 = (batch(q, par, o, s) for o in (0, -1, -2, -3, -4))
                ranks = par == 0 and (s is None or 6 <= s < 6 + B)

                def scores(u):
                    p, a = u // 2, u % 2
                    if u == 0:
                        pe.wait_ge(qk_in[m[1]], 64 * m[0] + 64)
                    if u < 2:
                        if g:
                            pe.wait_ge(qk_hi_ok, 3 * n(g))
                            pe.wait_ge(qk_lo_ok, 3 * n(g))
                        else:
                            pe.wait_ge(mT_ok, n(m, 1))
                            pe.wait_ge(mx_ok[(UNITS - 1) % UR], un(m, UNITS - 1, 1))
                    else:
                        pe.wait_ge(mx_ok[(u - 2) % UR], un(m, u - 2))
                    mm(pS[u % 2][0:HT, 0:2 * T], qpack[m[1]][0:96, p, a * HT:(a + 1) * HT], kdiag[m[1]][0:96, p, :, :],
                       start=True, stop=True).then_inc(s_ps[u % UR], 1)

                def values(u):
                    p, a = u // 2, u % 2
                    pe.wait_ge(ex_ok[u % UR], un(bk, u))
                    if u == 0:
                        pe.wait_ge(va_ok, n(bk))
                        if first(bk):
                            pe.wait_ge(a_pre, PRE_STAGE)
                        else:
                            pe.wait_ge(o_cp, 2 * n(bk, 1))
                    for hh in range(2):
                        h = 2 * p + hh
                        gg, j = h // 4, h % 4
                        dst = (pQ[:, gg * T:(gg + 1) * T] if gg < 2 else pR[:, 0:T])[32 * j:32 * j + 32]
                        last = mm(dst, vaug[bk[1]][:, a, h, :], probs[:, u % 2, hh, :], start=(a == 0), stop=(a == 1))
                    last.then_inc(pv_ok[u % UR], 1)

                for u in range(UNITS):
                    p, a = u // 2, u % 2
                    if m and S0 <= u < S0 + UNITS // 2:
                        scores(2 * (u - S0))
                        scores(2 * (u - S0) + 1)
                    if bk:
                        if u == 0:
                            pe.wait_ge(m_in[bk[1]], 16 * bk[0] + 16)
                        if u < 2:
                            if not first(bk):
                                pe.wait_ge(ex_ok[(UNITS - 2 + u) % UR], un(bk, UNITS - 2 + u, 1))
                        else:
                            pe.wait_ge(ex_ok[(u - 2) % UR], un(bk, u - 2))
                        for hh in range(2):
                            last = mm(pT[u % 2][0:HT, hh * T:(hh + 1) * T], kdiag[bk[1]][0:98, p, hh, a * HT:(a + 1) * HT],
                                      qpack[bk[1]][0:98, p, :], start=True, stop=True)
                        last.then_inc(st_ps[u % UR], 1)
                        if u:
                            values(u - 1)
                    if u == 0 and f:
                        pe.wait_ge(xn_ok, n(f))
                        if r1 and not first(r1):
                            pe.wait_ge(x2T_ok, n(r1, 1))
                        elif g:
                            pe.wait_ge(xT_lo, n(g))
                        for a_ in range(2):
                            tr(pX[:, a_ * HT:(a_ + 1) * HT], xn[:, a_, 0:CA], ident[0:HT, 0:HT])
                            last = tr(pX[:, T + a_ * HT:T + (a_ + 1) * HT], xn[:, a_, CA:256], ident[0:HT, 0:HT])
                        last.then_inc(xT_ps, 1)
                    if u == 2 and r1:
                        pe.wait_ge(o_ok, n(r1))
                        if g:
                            pe.wait_ge(v_ok, n(g))
                        for a_ in range(2):
                            for gg in range(3):
                                last = mm(pV[0:HT, a_ * C:(a_ + 1) * C], o_nrm[:, gg, a_ * HT:(a_ + 1) * HT], wout[:, gg, :],
                                          start=(gg == 0), stop=(gg == 2))
                        last.then_inc(y_ps, 1)
                    if u == 6 and ranks:
                        pe.wait_ge(rl[17], 4 * (q - 2))
                        if r1:
                            pe.wait_ge(h2_ok, n(r1))
                        mm(p_rank(), kon[0:HT, K_TRI:K_TRI + HT], hot[:, 0, :, :], start=True, stop=False)
                        mm(p_rank(), kon[0:HT, K_TRI:K_TRI + HT], hot[:, 1, :, :], start=False, stop=False)
                        mm(p_rank(), kon[0:HT, K_ONE:K_ONE + HT], cum[:, 0:4, :], start=False, stop=True).then_inc(rank_ps, 1)
                    if u == 9 and m:
                        pe.wait_ge(mx_ok[(UNITS - 1) % UR], un(m, UNITS - 1))
                        pe.wait_ge(mx_ok[(UNITS - 2) % UR], un(m, UNITS - 2))
                        tr(pS[0][0:2 * NH, 0:HT], mx[:].rearrange("p h k a -> p (h k a)"), ident[0:HT, 0:HT]).then_inc(mT_ps, 1)
                    if u == 9 and r1:
                        pe.wait_ge(xn2_ok, n(r1))
                        if f:
                            pe.wait_ge(xT_lo, n(f))
                            pe.wait_ge(xT_hi, n(f))
                        for a_ in range(2):
                            tr(pX[:, a_ * HT:(a_ + 1) * HT], xn2[:, r1[1], a_, 0:CA], ident[0:HT, 0:HT])
                            last = tr(pX[0:CT, T + a_ * HT:T + (a_ + 1) * HT], xn2[:, r1[1], a_, CA:C], ident[0:HT, 0:HT])
                        last.then_inc(x2T_ps, 1)
                    if u == 11 and r1:
                        pe.wait_ge(x2T_ok, n(r1))
                        pe.wait_ge(h2_ok, n(r1))
                        if ranks:
                            pe.wait_ge(rl[15], q - 2)
                        for a_ in range(2):
                            dst = pV[0:HT, 384 + a_ * RC:384 + (a_ + 1) * RC]
                            mm(dst, xn2T[:, 0, a_ * HT:(a_ + 1) * HT], wroute[:, 0, :], start=True, stop=False)
                            last = mm(dst, xn2T[0:CT, 1, a_ * HT:(a_ + 1) * HT], wroute[0:CT, 1, :], start=False, stop=True)
                        last.then_inc(rt_ps, 1)
                if bk:
                    values(UNITS - 1)
                if f:
                    pe.wait_ge(xT_hi, n(f))
                    pe.wait_ge(xT_lo, n(f))
                    if m:
                        pe.wait_ge(mT_ok, n(m))
                    elif g:
                        pe.wait_ge(qk_hi_ok, 3 * n(g))
                        pe.wait_ge(qk_lo_ok, 3 * n(g))
                    if first(f):
                        pe.wait_ge(v_pre, PRE_V)
                    for i in range(3):
                        w = slice(i * 128, (i + 1) * 128)
                        o = pS[0][:, i * T:(i + 1) * T] if i < 2 else pS[1][:, 0:T]
                        mm(o, wqkv_hi[:, w], xa_hi[:], start=True, stop=False)
                        mm(o, wqkv_lo[:, w], xa_hi[:], start=False, stop=False)
                        mm(o, wqkv_hi[:, w], xa_lo[:], start=False, stop=False)
                        mm(o, wqkv_t1[:, w], xt[0:CT, :], start=False, stop=False)
                        last = mm(o, wqkv_t2[:, w], xt[:], start=False, stop=True)
                    last.then_inc(qk_ps, 1)
                    if r1:
                        pe.wait_ge(rt_cp, n(r1))
                    if g:
                        pe.wait_ge(v_ok, n(g))
                    for a_ in range(2):
                        t = slice(a_ * HT, (a_ + 1) * HT)
                        o = pV[0:HT, a_ * C:(a_ + 1) * C]
                        mm(o, xa_hi[:, t], wqkv_hi[:, 2 * C:], start=True, stop=False)
                        mm(o, xa_hi[:, t], wqkv_lo[:, 2 * C:], start=False, stop=False)
                        mm(o, xa_lo[:, t], wqkv_hi[:, 2 * C:], start=False, stop=False)
                        mm(o, xt[0:CT, t], wqkv_t1[:, 2 * C:], start=False, stop=False)
                        last = mm(o, xt[:, t], wqkv_t2[:, 2 * C:], start=False, stop=True)
                    last.then_inc(v_ps, 1)

            run_steps(pe, step)
            pe.wait_ge(rl[15], B // 2)
            pe.wait_ge(rl[17], 4 * (B // 2))
            pe.wait_ge(h2_ok, B)
            mm(pV[:, 0:E], kon[0:HT, K_ONE:K_ONE + 128], cum[:, 4, :], start=True, stop=True).then_inc(cnt_ps, 1)

            U = [pS, pT]

            def transpose_slots(j, r, t, guard):
                pe.wait_ge(xs_in[r], 16 * t + 16)
                if guard:
                    pe.wait_ge(sx_ok, 2 * j)
                tr(pX[:, 0:128], xs[r][:, 0:CA], ident)
                tr(pX[0:CT, 128:256], xs[r][:, CA:C], ident).then_inc(sx_ps, 1)

            def up(j, par, guard, ew):
                pe.wait_ge(sx_ok, 2 * j + 2)
                if guard:
                    pe.wait_ge(relu_ok, 2 * (j - 1))
                for i, (c0, w) in enumerate(((0, 512), (512, 256))):
                    o = U[i][par][:, 0:w]
                    mm(o, sxa[par][:], experts[:, bass.ds(ew, 1), c0:c0 + w].rearrange("p a w -> p (a w)"), start=True, stop=False)
                    last = mm(o, sxt[par][:], experts[0:CT + 1, bass.ds(ew, 1), H + c0:H + c0 + w].rearrange("p a w -> p (a w)"),
                              start=False, stop=True)
                last.then_inc(u_ps, 1)

            def transpose_hidden(j, par, guard):
                if guard:
                    pe.wait_ge(hT_a, j)
                    pe.wait_ge(hT_v, j)
                for k in range(HC):
                    if k == 0:
                        pe.wait_ge(hid_ok, 2 * j + 1)
                    if k == 4:
                        pe.wait_ge(hid_ok, 2 * j + 2)
                    o = pQ if k < 3 else pR
                    last = tr(o[:, (k % 3) * 128:(k % 3 + 1) * 128], hid[par][:, k * 128:(k + 1) * 128], ident)
                last.then_inc(hT_ps, 1)

            def down(j, guard, ew):
                pe.wait_ge(hT_a, j + 1)
                pe.wait_ge(hT_v, j + 1)
                if guard:
                    pe.wait_ge(ys_ok, j)
                for k in range(HC):
                    last = mm(pV[:, 0:C], hidT[:, k, :],
                              experts[:, bass.ds(ew, 1), 2 * H + k * C:2 * H + (k + 1) * C].rearrange("p a w -> p (a w)"),
                              start=(k == 0), stop=(k == HC - 1))
                last.then_inc(y2_ps, 1)

            def expert_of(j):
                return pe.value_load(tabi[0:1, bass.ds(BLOCKS + j, 1)], min_val=0, max_val=E - 1)

            pe.wait_ge(tab_ok, 1)
            transpose_slots(0, 0, 0, False)
            up(0, 0, False, expert_of(0))
            transpose_slots(1, 1, 0, True)

            def ffn(t, r, guard, ahead=2):
                j, par = 4 * t + r, r % 2
                e_next, e = expert_of(j + 1) if ahead else None, expert_of(j)
                transpose_hidden(j, par, guard)
                if ahead:
                    up(j + 1, 1 - par, guard, e_next)
                if ahead > 1:
                    transpose_slots(j + 2, (r + 2) % 4, t + (r + 2) // 4, True)
                down(j, guard, e)

            for r in range(4):
                ffn(0, r, r > 0)
            with pe.Fori(1, BLOCKS // 4 - 1) as t:
                for r in range(4):
                    ffn(t, r, True)
            for r in range(4):
                ffn(BLOCKS // 4 - 1, r, True, min(2, 3 - r))

        @block.scalar
        def _(act):
            sc = nc.scalar
            for c in range(3):
                act.wait_ge(s_x, 16 * B)
                src = xp3[:, c * 1792:(c + 1) * 1792].rearrange("p (i w j) -> p w i j", i=PS, w=GRID)
                dst = xq3.rearrange("p (w c i j) -> p w c i j", w=GRID, c=3, i=PS)
                if c < 3:
                    sc.copy(dst[:, :, c], src).then_inc(a_pre, 1)
            act.wait_ge(s_wq, 16 * 10)
            sc.mul(wqk_in[0:64], wqk_in[0:64], SCALE).then_inc(a_pre, 1)
            for rnd in range(2):
                act.wait_ge(t_pre, 2 * GRID + 1 + rnd)
                w = slice(0, 2 * C) if rnd == 0 else slice(2 * C, 3 * C)
                cols = w.stop - w.start
                sc.copy(wqkv_hi[:, w], pS[0][:, 0:cols]).then_inc(a_pre, 1)
                sc.copy(wqkv_t2[:, w], pS[1][:, 0:cols]).then_inc(a_pre, 1)
            act.wait_ge(t_pre, 2 * GRID + 3)
            sc.copy(wout[:, :, 0:96], pQ[:, 0:288].rearrange("p (g e) -> p g e", g=3)).then_inc(a_pre, 1)
            sc.copy(wout[:, :, 96:192], pR[:, 0:288].rearrange("p (g e) -> p g e", g=3)).then_inc(a_pre, 1)

            def step(q, par, s):
                f, g, bk, r1 = (batch(q, par, o, s) for o in (0, -1, -3, -4))
                r2 = par == 0 and (s is None or 6 <= s < 6 + B)
                for u in range(UNITS):
                    if bk:
                        act.wait_ge(st_ps[u % UR], un(bk, u))
                        if u < 2:
                            if not first(bk):
                                act.wait_ge(pv_ok[(UNITS - 2 + u) % UR], un(bk, UNITS - 2 + u, 1))
                        else:
                            act.wait_ge(pv_ok[(u - 2) % UR], un(bk, u - 2))
                        sc.activation(probs[:, u % 2].rearrange("p h t -> p (h t)"), pT[u % 2][0:HT, 0:2 * T],
                                      ACT.Exp).then_inc(ex_ok[u % UR], 1)
                    if u == 1 and f:
                        act.wait_ge(xT_ps, n(f))
                        if not first(f):
                            act.wait_ge(qk_ps, n(f, 1))
                            act.wait_ge(v_ps, n(f, 1))
                            act.wait_ge(xT_lo, n(f, 1))
                        sc.copy(xa_hi[:], pX[:, 0:T])
                        sc.copy(xt[:], pX[:, T:2 * T]).then_inc(xT_hi, 1)
                    if u == 10 and r1:
                        act.wait_ge(x2T_ps, n(r1))
                        if not first(r1):
                            act.wait_ge(rt_ps, n(r1, 1))
                        sc.copy(xn2T[:, 0, :], pX[:, 0:T])
                        sc.copy(xn2T[0:CT, 1, :], pX[0:CT, T:2 * T]).then_inc(x2T_ok, 1)
                    if u == 7 and r2:
                        act.wait_ge(dl_ok, q - 2)
                        sc.activation(edl[:], dlt[:], ACT.Exp).then_inc(ed_ok, 1)
                if bk:
                    act.wait_ge(pv_ok[(UNITS - 1) % UR], un(bk, UNITS - 1))
                    if not first(bk):
                        act.wait_ge(o_tr_ok, n(bk, 1))
                    sc.copy(o_raw[:, 0:2 * T], pQ[:, 0:2 * T]).then_inc(o_cp, 1)
                    sc.copy(o_raw[:, 2 * T:3 * T], pR[:, 0:T]).then_inc(o_cp, 1)
                if f:
                    act.wait_ge(qk_ps, n(f))
                    if not first(f):
                        pf = f[1] ^ 1
                        act.wait_ge(qk_out[pf], 96 * (f[0] - (1 if f[1] == 0 else 0)) + 96)
                    for i in range(3):
                        src = pS[0][:, i * T:(i + 1) * T] if i < 2 else pS[1][:, 0:T]
                        sc.activation(qk_hi[:, i, :], src, ACT.Identity, bias=bqk[:, i:i + 1]).then_inc(qk_hi_ok, 1)
                if g:
                    act.wait_ge(v_ok, n(g))
                    sc.copy(vaug[g[1]][:].rearrange("p a h d -> p (a h) d")[:, :, 0:HD],
                            vtmp[:].rearrange("p (h d) -> p h d", d=HD)).then_inc(va_ok, 1)

            act.wait_ge(v_pre, PRE_V)
            run_steps(act, step)

            def tile(j, par, guard):
                act.wait_ge(sx_ps, j + 1)
                if guard:
                    act.wait_ge(u_ps, j - 1)
                sc.copy(sxa[par][:], pX[:, 0:128]).then_inc(sx_ok, 1)
                sc.copy(sxt[par][0:CT, :], pX[0:CT, 128:256]).then_inc(sx_ok, 1)

            def relu_tile(j, par, guard):
                act.wait_ge(u_ps, j + 1)
                if guard:
                    act.wait_ge(hid_ok, 2 * (j - 1))
                sc.activation(relu[par][:, 0:512], pS[par][:], ACT.Relu).then_inc(relu_ok, 1)
                sc.activation(relu[par][:, 512:768], pT[par][:, 0:256], ACT.Relu).then_inc(relu_ok, 1)

            def hidT_half(j, guard):
                act.wait_ge(hT_ps, j + 1)
                if guard:
                    act.wait_ge(y2_ps, j)
                sc.copy(hidT[:, 0:3, :], pQ[:, 0:384].rearrange("p (k t) -> p k t", k=3)).then_inc(hT_a, 1)

            act.wait_ge(tab_ok, 1)
            tile(0, 0, False)
            relu_tile(0, 0, False)
            tile(1, 1, False)

            def ffn(t, r, guard, ahead=2):
                j, par = 4 * t + r, r % 2
                hidT_half(j, guard)
                if ahead > 1:
                    tile(j + 2, par, True)
                if ahead:
                    relu_tile(j + 1, 1 - par, guard)

            for r in range(4):
                ffn(0, r, r > 0)
            with act.Fori(1, BLOCKS // 4 - 1) as t:
                for r in range(4):
                    ffn(t, r, True)
            for r in range(4):
                ffn(BLOCKS // 4 - 1, r, True, min(2, 3 - r))

        @block.vector
        def _(dve):
            v = nc.vector
            pre = [0]

            def p(ins):
                pre[0] += 1
                ins.then_inc(v_pre, 1)
                return pre[0]

            def pw(ins):
                dve.wait_ge(v_pre, p(ins))

            for w in range(GRID):
                dve.wait_ge(t_pre, 2 * w + 1)
                v.tensor_copy(pT_sb[:, w % 2, 0:3, :].rearrange("p k n -> p (k n)"), pS[0][:, 0:3 * NTOK])
                p(v.tensor_copy(pT_sb[:, w % 2, 3:6, :].rearrange("p k n -> p (k n)"), pS[1][:, 0:3 * NTOK]))
                dve.wait_ge(t_pre, 2 * w + 2)
                p(v.tensor_tensor(emb[:, w, :], pT[w % 2][0:NTOK, 0:C], tokb, ALU.add))
            assert pre[0] == PRE_EMB
            for rnd in range(2):
                dve.wait_ge(a_pre, 4 + 2 * rnd + 2)
                w = slice(0, 2 * C) if rnd == 0 else slice(2 * C, 3 * C)
                cols = w.stop - w.start
                v.tensor_tensor(wqkv_lo[:, w], pS[0][:, 0:cols], wqkv_hi[:, w].bitcast(F32), ALU.subtract)
                pw(v.tensor_copy(wqkv_t1[:, w], wqkv_t2[0:CT, w].bitcast(F32)))
                p(v.tensor_tensor(wqkv_t2[0:CT, w], pS[1][0:CT, 0:cols], wqkv_t1[:, w].bitcast(F32), ALU.subtract))
            assert pre[0] == PRE_WQ0 + 2
            dve.wait_ge(s_sm, 16 * small_loads)
            pw(v.tensor_tensor(r_sc[:, 24:48], em_in, em_in, ALU.mult))
            pw(v.tensor_reduce(r_sc[:, 0:1], r_sc[:, 24:48], AX.X, ALU.add))
            dve.wait_ge(g_pre, PRE_G)
            pw(v.tensor_scalar(r_sc[:, 2:3], r_sc[:, 1:2], 0.02 / C, 0.02 / C, ALU.mult, ALU.add))
            pw(v.tensor_scalar(r_sc[:, 3:4], r_sc[:, 1:2], 1e-12, None, ALU.max))
            pw(v.reciprocal(r_sc[:, 4:5], r_sc[:, 3:4]))
            pw(v.tensor_scalar(em_in, em_in, r_sc[:, 4:5], 0.02, ALU.mult, ALU.mult))
            pw(v.tensor_scalar(r_in, r_in, r_sc[:, 2:3], None, ALU.add))
            assert pre[0] == PRE_EMBN, pre[0]
            dve.wait_ge(t_pre, 2 * GRID + 4)
            p(v.tensor_copy(nT_sb, pX[0:DR, 448:448 + E]))
            assert pre[0] == PRE_NT
            pw(v.tensor_scalar(fe_in, fe_in, 0.1, None, ALU.mult))
            pw(v.tensor_tensor(fe_in[:, 0:E], fe_in[:, 0:E], fe_in[:, E:2 * E], ALU.subtract))
            pw(v.tensor_copy(bias_e[:], fe_in[:, 0:E].unsqueeze(1).to_broadcast([HT, 4, E])))
            v.tensor_scalar(bqk[0:64, :], bqk[0:64, :], SCALE, None, ALU.mult)
            v.memset(cum[:, 4, :], 0.0)
            v.memset(sxt[0][CT:CT + 1, :], 1.0)
            v.memset(sxt[1][CT:CT + 1, :], 1.0)
            for i in range(2):
                v.memset(vaug[i][:], 1.0)
            v.memset(o_raw, 1.0)
            dve.wait_ge(t_pre, 2 * GRID + 5)
            v.tensor_copy(wroute[:, 0, :], pV[:, 0:RC])
            pw(v.tensor_copy(wroute[0:CT, 1, :], pV[0:CT, 64:64 + RC]))
            assert pre[0] == PRE_V, pre[0]

            def norm_stats(src, st, mv, st_sem, mv_sem, b):
                v.bn_stats(st[b[1]][:, 0, :], src[:, 0, :])
                v.bn_stats(st[b[1]][:, 1, :], src[:, 1, :]).then_inc(st_sem, 1)
                dve.wait_ge(st_sem, n(b))
                settle(dve)
                v.bn_aggr(mv[b[1]][:, 0, :], st[b[1]][:, 0, :])
                v.bn_aggr(mv[b[1]][:, 1, :], st[b[1]][:, 1, :]).then_inc(mv_sem, 1)

            def step(q, par, s):
                pr, f, g, m, bk, r1 = (batch(q, par, o, s) for o in (1, 0, -1, -2, -3, -4))
                r2 = par == 0 and (s is None or 6 <= s < 6 + B)
                weights = par == 1 and (s is None or 0 <= s < 2 * E)
                k = q - 2
                flat = lambda t: t.rearrange("p a e -> p (a e)")

                if g:
                    dve.wait_ge(v_ps, n(g))
                    if not first(g):
                        dve.wait_ge(va_ok, n(g, 1))
                    v.tensor_tensor(vtmp[:], pV[0:HT, 0:2 * C], bv_bc[:].rearrange("p a c -> p (a c)"), ALU.add).then_inc(v_ok, 1)
                if f:
                    dve.wait_ge(xT_hi, n(f))
                    v.tensor_tensor(xa_lo[:], pX[:, 0:T], xa_hi[:].bitcast(F32), ALU.subtract)
                    v.tensor_tensor(xt[CT:128, :], pX[CT:128, T:2 * T], xt[CT:128, :].bitcast(F32), ALU.subtract).then_inc(xT_lo, 1)
                if pr:
                    dve.wait_ge(hA_in[pr[1]], 16 * pr[0] + 16)
                    if not first(pr, 2):
                        dve.wait_ge(ln1_pow, n(pr, 2))
                    norm_stats(hA[pr[1]], st1, mv1, ln1_st, ln1_mv, pr)
                if r2:
                    dve.wait_ge(rt_pow, 2 * k)
                    v.tensor_scalar(rinv[:], rnm[:], 1e-12, None, ALU.max).then_inc(rl[0], 1)
                    dve.wait_ge(rl[0], k)
                    v.reciprocal(rnm[:], rinv[:]).then_inc(rl[1], 1)
                    dve.wait_ge(rl[1], k)
                    v.tensor_tensor(lg2[:], rt[:, :, E:2 * E], rnm[:].unsqueeze(2).to_broadcast([HT, 4, E]), ALU.mult).then_inc(rl[2], 1)
                    dve.wait_ge(rl[2], k)
                    v.tensor_tensor(lg2[:], lg2[:], rt[:, :, 0:E], ALU.add).then_inc(rl[3], 1)
                    dve.wait_ge(rl[3], k)
                    v.tensor_tensor(lg[:], lg2[:], bias_e[:], ALU.add).then_inc(rl[4], 1)
                    dve.wait_ge(rl[4], k)
                    src = lg
                    for c in range(2):
                        o = 5 + 5 * c
                        v.tensor_reduce(top[:, c, :], src[:], AX.X, ALU.max).then_inc(rl[o], 1)
                        dve.wait_ge(rl[o], k)
                        v.tensor_tensor(cand[:], src[:], top[:, c, :].unsqueeze(2).to_broadcast([HT, 4, E]), ALU.is_equal).then_inc(rl[o + 1], 1)
                        dve.wait_ge(rl[o + 1], k)
                        v.tensor_tensor(cand[:], cand[:], kon[0:HT, K_DESC:K_DESC + 4 * E].rearrange("p (a e) -> p a e", a=4), ALU.mult).then_inc(rl[o + 2], 1)
                        dve.wait_ge(rl[o + 2], k)
                        v.tensor_reduce(cmx[:], cand[:], AX.X, ALU.max).then_inc(rl[o + 3], 1)
                        dve.wait_ge(rl[o + 3], k)
                        v.tensor_tensor(hot[:, c, :, :], cand[:], cmx[:].unsqueeze(2).to_broadcast([HT, 4, E]), ALU.is_equal).then_inc(rl[o + 4], 1)
                        dve.wait_ge(rl[o + 4], k)
                        if c == 0:
                            v.scalar_tensor_tensor(flat(lg2[:]), flat(hot[:, 0, :, :]), -1e30, flat(lg[:]), ALU.mult, ALU.add).then_inc(rl[23], 1)
                            dve.wait_ge(rl[23], k)
                            src = lg2
                    v.tensor_tensor(dlt[:], top[:, 1, :], top[:, 0, :], ALU.subtract).then_inc(dl_ok, 1)
                    v.tensor_tensor(flat(cand[:]), flat(hot[:, 0, :, :]), flat(hot[:, 1, :, :]), ALU.add)
                    v.tensor_copy(cum[:, 0, :], cum[:, 4, :]).then_inc(rl[16], 1)
                    dve.wait_ge(rl[16], k)
                    for i in range(4):
                        v.tensor_tensor(cum[:, i + 1, :], cum[:, i, :], cand[:, i, :], ALU.add).then_inc(rl[17], 1)
                        dve.wait_ge(rl[17], 4 * (k - 1) + i + 1)
                for u in range(UNITS):
                    if m:
                        pp, a = u // 2, u % 2
                        dve.wait_ge(s_ps[u % UR], un(m, u))
                        if u == 0 and not first(m):
                            dve.wait_ge(mT_ps, n(m, 1))
                        v.tensor_reduce(mx[:, :, pp, a], pS[u % 2][0:HT, 0:2 * T].rearrange("p (h t) -> p h t", h=2),
                                        AX.X, ALU.max).then_inc(mx_ok[u % UR], 1)
                    if u == 3 and r1:
                        dve.wait_ge(y_ps, n(r1))
                        dve.wait_ge(hR_in[r1[1]], 16 * r1[0] + 16)
                        v.tensor_tensor(hR[r1[1]][:].rearrange("p a c -> p (a c)"), pV[0:HT, 0:2 * C],
                                        hR[r1[1]][:].rearrange("p a c -> p (a c)"), ALU.add).then_inc(h2_ok, 1)
                        dve.wait_ge(h2_ok, n(r1))
                        norm_stats(hR[r1[1]], st2, mv2, ln2_st, ln2_mv, r1)
                    if u == 5 and r2:
                        if s is None or k > 1:
                            dve.wait_ge(sc_done, 128 * (k - 1))
                        for c in range(2):
                            last = v.tensor_copy(slot_rows[:, :, c, 0:C], xn2[:].rearrange("p b a c -> p (b a) c"))
                        last.then_inc(slot_cp, 1)
                    if u == 7 and r2:
                        dve.wait_ge(rank_ps, k)
                        v.tensor_tensor(rank[:].rearrange("p a e -> p (a e)"), p_rank(), kon[0:HT, K_BASE:K_BASE + 4 * E], ALU.add).then_inc(rl[15], 1)
                    if u == 9 and r1:
                        dve.wait_ge(ln2_pow, n(r1))
                        if not first(r1, 2):
                            dve.wait_ge(x2T_ps, n(r1, 2))
                        if r2:
                            dve.wait_ge(slot_cp, k)
                        for a in range(2):
                            last = v.tensor_scalar(xn2[:, r1[1], a, :], hR[r1[1]][:, a, :], mv2[r1[1]][:, a, 0:1],
                                                   rs2[r1[1]][:, a, 1:2], ALU.subtract, ALU.mult)
                        last.then_inc(xn2_ok, 1)
                if m:
                    dve.wait_ge(mT_ps, n(m))
                    if not first(m):
                        pm = m[1] ^ 1
                        dve.wait_ge(m_out[pm], 16 * (m[0] - (1 if m[1] == 0 else 0)) + 16)
                    v.tensor_scalar(mT[:], pS[0][0:2 * NH, 0:HT], -1.0, None, ALU.mult).then_inc(mT_ok, 1)
                if r1:
                    dve.wait_ge(rt_ps, n(r1))
                    sl = slice(2 * r1[1], 2 * r1[1] + 2)
                    v.tensor_copy(rt[:, sl, :], pV[0:HT, 384:384 + 2 * RC].rearrange("p (a r) -> p a r", a=2)).then_inc(rt_cp, 1)
                    dve.wait_ge(rt_cp, n(r1))
                    v.tensor_tensor(rsq[:, sl, :], rt[:, sl, 2 * E:], rt[:, sl, 2 * E:], ALU.mult).then_inc(rt_sq, 1)
                    dve.wait_ge(rt_sq, n(r1))
                    if not first(r1, 2):
                        dve.wait_ge(rt_pow, n(r1, 2))
                    v.tensor_reduce(rss[:, sl], rsq[:, sl, :], AX.X, ALU.add).then_inc(rt_ss, 1)
                if bk:
                    dve.wait_ge(o_cp, 2 * n(bk))
                    settle(dve)
                    v.transpose(o_tr, o_raw).then_inc(o_tr_ok, 1)
                    dve.wait_ge(o_tr_ok, n(bk))
                    blocks = o_tr.rearrange("p (b x) -> p b x", x=32)
                    v.reciprocal(osum[:].unsqueeze(2), blocks[:, :, HD:HD + 1]).then_inc(o_rc, 1)
                    dve.wait_ge(o_rc, n(bk))
                    v.tensor_tensor(blocks, blocks, osum[:].unsqueeze(2).to_broadcast([128, OW // 32, 32]), ALU.mult).then_inc(o_mul, 1)
                    dve.wait_ge(o_mul, n(bk))
                    settle(dve)
                    if not first(bk):
                        dve.wait_ge(y_ps, n(bk, 1))
                        settle(dve)
                    v.transpose(o_out, o_tr).then_inc(o_ok, 1)
                if f:
                    for i in range(3):
                        dve.wait_ge(qk_hi_ok, 3 * n(f, 1) + (2 if i < 2 else 3))
                        if i == 0 and not first(f):
                            pf = f[1] ^ 1
                            dve.wait_ge(qk_out[pf], 96 * (f[0] - (1 if f[1] == 0 else 0)) + 96)
                        src = pS[0][:, i * T:(i + 1) * T] if i < 2 else pS[1][:, 0:T]
                        v.scalar_tensor_tensor(qk_lo[:, i, :], src, bqk[:, i:i + 1], qk_hi[:, i, :].bitcast(F32),
                                               ALU.add, ALU.subtract).then_inc(qk_lo_ok, 1)
                if pr:
                    dve.wait_ge(ln1_pow, n(pr))
                    if not first(pr):
                        dve.wait_ge(xT_ps, n(pr, 1))
                    for a in range(2):
                        v.tensor_scalar(xn[:, a, 0:C], hA[pr[1]][:, a, :], mv1[pr[1]][:, a, 0:1],
                                        rs1[pr[1]][:, a, 1:2], ALU.subtract, ALU.mult)
                        last = v.tensor_scalar(xn[:, a, C:256], hA[pr[1]][:, a, CA:C], mv1[pr[1]][:, a, 0:1],
                                               rs1[pr[1]][:, a, 1:2], ALU.subtract, ALU.mult)
                    last.then_inc(xn_ok, 1)
                if r2:
                    dve.wait_ge(ed_ok, k)
                    v.tensor_scalar(rinv[:], edl[:], 1.0, None, ALU.add).then_inc(rl[18], 1)
                    dve.wait_ge(rl[15], k)
                    for c in range(2):
                        last = v.tensor_tensor(rsel[:, c, :, :], hot[:, c, :, :], rank[:], ALU.mult)
                    last.then_inc(rl[21], 1)
                    dve.wait_ge(rl[18], k)
                    v.reciprocal(gates[:, 0, :], rinv[:]).then_inc(rl[19], 1)
                    dve.wait_ge(rl[21], k)
                    v.tensor_reduce(rowf[:].rearrange("p c a -> p (c a)"), rsel[:].rearrange("p c a e -> p (c a) e"), AX.X, ALU.add).then_inc(rl[22], 1)
                    dve.wait_ge(rl[19], k)
                    v.tensor_tensor(gates[:, 1, :], gates[:, 0, :], edl[:], ALU.mult).then_inc(rl[20], 1)
                    dve.wait_ge(rl[22], k)
                    v.tensor_copy(rowi[:], rowf[:])
                    dve.wait_ge(rl[20], k)
                    for c in range(2):
                        v.tensor_copy(slot_rows[:, :, c, C:C + 1], gates[:, c, :].unsqueeze(2))
                        last = v.tensor_copy(slot_rows[:, :, c, C + 1:C + 2].bitcast(U32), tokf[:].unsqueeze(2))
                    last.then_inc(row_ok, 1)
                    dve.wait_ge(row_ok, k)
                    v.tensor_scalar(tokf[:], tokf[:], float(2 * T), None, ALU.add)
                if weights:
                    dve.wait_ge(hebb_in, 48 * q + 48)
                    dve.wait_ge(slow_in, 48 * q + 48)
                    if s == 1:
                        dve.wait_ge(s_sm, 16 * small_loads)
                    we = expert(q)
                    parts = ((slice(0, 128), slice(0, H), 0), (slice(0, CT), slice(H, 2 * H), 0),
                             (slice(0, 128), slice(2 * H, WCOLS), 1))
                    for i, (rows, cols, gate) in enumerate(parts):
                        last = v.scalar_tensor_tensor(we[rows, cols], stage_s[rows, cols], mg[rows, gate, bass.ds(q, 1)],
                                                      we[rows, cols], ALU.mult, ALU.add)
                    last.then_inc(wprep, 1)

            run_steps(dve, step)

            links = [0]

            def link(ins):
                links[0] += 1
                ins.then_inc(tch, 1)
                dve.wait_ge(tch, links[0])
            dve.wait_ge(cnt_ps, 1)
            link(v.tensor_copy(cnt[:], pV[0:1, 0:E]))
            kk = kon[0:1, K_KK:K_KK + 23].unsqueeze(1).to_broadcast([1, E, 23])
            link(v.tensor_tensor(tcmp[:], cnt[:].unsqueeze(2).to_broadcast([1, E, 23]), kk, ALU.is_gt))
            link(v.tensor_reduce(nblk[:], tcmp[:], AX.X, ALU.add))
            link(v.tensor_tensor(tcum[:], kon[0:1, K_CUM:K_CUM + E * E].rearrange("p (a b) -> p a b", a=E),
                                 nblk[:].unsqueeze(1).to_broadcast([1, E, E]), ALU.mult))
            link(v.tensor_reduce(ends[:], tcum[:], AX.X, ALU.add))
            jj = kon[0:1, K_JJ:K_JJ + BLOCKS]
            link(v.tensor_tensor(tge[:], jj.unsqueeze(2).to_broadcast([1, BLOCKS, E]),
                                 ends[:].unsqueeze(1).to_broadcast([1, BLOCKS, E]), ALU.is_ge))
            link(v.tensor_reduce(tabf[:, BLOCKS:2 * BLOCKS], tge[:], AX.X, ALU.add))
            link(v.tensor_scalar(tabf[:, BLOCKS:2 * BLOCKS], tabf[:, BLOCKS:2 * BLOCKS], float(E - 1), None, ALU.min))
            link(v.tensor_scalar(twt[:], nblk[:], -128.0, float(CAP), ALU.mult, ALU.add))
            link(v.tensor_tensor(trow[:], tge[:], twt[:].unsqueeze(1).to_broadcast([1, BLOCKS, E]), ALU.mult))
            link(v.tensor_reduce(tabf[:, 0:BLOCKS], trow[:], AX.X, ALU.add))
            link(v.scalar_tensor_tensor(tabf[:, 0:BLOCKS], jj, 128.0, tabf[:, 0:BLOCKS], ALU.mult, ALU.add))
            link(v.tensor_tensor(tabf[:, 2 * BLOCKS:], cnt[:], kon[0:1, K_BASE:K_BASE + E], ALU.add))
            v.tensor_copy(tabi[:], tabf[:]).then_inc(tab_ok, 1)
            dve.wait_ge(tab_ok, 1)

            def square(j, par, guard):
                for i, cols in enumerate((slice(0, 512), slice(512, H))):
                    dve.wait_ge(relu_ok, 2 * j + 1 + i)
                    if guard and i == 0:
                        dve.wait_ge(hT_ps, j - 1)
                    r_ = relu[par][:, cols]
                    v.tensor_tensor(hid[par][:, cols], r_, r_, ALU.mult).then_inc(hid_ok, 1)

            def hidT_half(j, guard):
                dve.wait_ge(hT_ps, j + 1)
                if guard:
                    dve.wait_ge(y2_ps, j)
                v.tensor_copy(hidT[:, 3:6, :], pR[:, 0:384].rearrange("p (k t) -> p k t", k=3)).then_inc(hT_v, 1)

            def output(j, r, par, guard, e):
                dve.wait_ge(y2_ps, j + 1)
                v.tensor_tensor(ysum[par], pV[:, 0:C], b2_bc[:, bass.ds(e, 1), :].rearrange("p a c -> p (a c)"),
                                ALU.add).then_inc(ys_ok, 1)
                dve.wait_ge(ys_ok, j + 1)
                if guard:
                    dve.wait_ge(add_done, 16 * (j - 1))
                v.tensor_scalar(ygate[par], ysum[par], xs[r][:, C:C + 1], None, ALU.mult).then_inc(yg_ok, 1)

            def ffn(t, r, guard, ahead=True):
                j, par = 4 * t + r, r % 2
                hidT_half(j, guard)
                if ahead:
                    square(j + 1, 1 - par, guard)
                e = dve.value_load(tabi[0:1, bass.ds(BLOCKS + j, 1)], min_val=0, max_val=E - 1)
                output(j, r, par, guard, e)

            square(0, 0, False)
            for r in range(4):
                ffn(0, r, r > 0)
            with dve.Fori(1, BLOCKS // 4 - 1) as t:
                for r in range(4):
                    ffn(t, r, True)
            for r in range(4):
                ffn(BLOCKS // 4 - 1, r, True, min(2, 3 - r))

        @block.gpsimd
        def _(pool):
            g = nc.gpsimd
            g.memset(wo_in, 0.0).then_inc(g_pre, 1)
            g.memset(kdiag[0][:].bitcast(F32), 0.0)
            g.memset(kdiag[1][:].bitcast(F32), 0.0)
            g.memset(powers[:, 0:2], -0.5)
            g.memset(powers[:, 2:4], 0.5).then_inc(g_pre, 1)
            pool.wait_ge(g_pre, 2)
            pool.wait_ge(v_pre, PRE_SS)
            g.tensor_tensor(r_sc[:, 1:2], r_sc[:, 0:1], powers[0:E, 2:3], ALU.pow).then_inc(g_pre, 1)

            def rsqrt(mv, rs, mv_sem, pe_sem, pow_sem, b):
                pool.wait_ge(mv_sem, n(b))
                settle(pool)
                g.tensor_scalar(rs[b[1]][:, :, 0:1], mv[b[1]][:, :, 1:2], 1e-5, None, ALU.add).then_inc(pe_sem, 1)
                pool.wait_ge(pe_sem, n(b))
                g.tensor_tensor(rs[b[1]][:, :, 1], rs[b[1]][:, :, 0], powers[:, 0:2], ALU.pow).then_inc(pow_sem, 1)

            def scatter(k, j):
                a, c = j // 2, j % 2
                if not (isinstance(k, int) and k + j == 0):
                    pool.wait_ge(sc_done, 128 * k + 16 * j)
                settle(pool)
                g.indirect_dma_start(slots_dram, bass.IndirectOffsetOnAxis(ap=rowi[:, c, a:a + 1], axis=0),
                                     slot_rows[:, a, c, :], None).then_inc(sc_done, 16)

            def step(q, par, s):
                pr, gg, m, bk, r1 = (batch(q, par, o, s) for o in (1, -1, -2, -3, -4))
                if par == 0 and (s is None or s >= 8):
                    scatter(q - 4, 7)
                turn = iter(range(1, 7))

                def next_scatter():
                    if par == 1 and (s is None or 7 <= s):
                        scatter(q - 3, next(turn))

                next_scatter()
                if pr:
                    if not first(pr, 2):
                        pool.wait_ge(xn_ok, n(pr, 2))
                    rsqrt(mv1, rs1, ln1_mv, ln1_pe, ln1_pow, pr)
                next_scatter()
                if par == 1 and (s is None or 0 <= s < 2 * E):
                    pool.wait_ge(fast_in, 64 * q + 64)
                    settle(pool)
                    for dst, src in expert_loads(expert(q), h_fast1, h_fast2, q):
                        pool.dma_start(dst, src, accum_op=ALU.add).then_inc(hebb_in, 16)
                next_scatter()
                if r1:
                    if not first(r1, 2):
                        pool.wait_ge(xn2_ok, n(r1, 2))
                    rsqrt(mv2, rs2, ln2_mv, ln2_pe, ln2_pow, r1)
                next_scatter()
                next_scatter()
                if m:
                    pool.wait_ge(m_out[m[1]], 16 * m[0] + 16)
                    settle(pool)
                    pool.dma_start(qpack[m[1]][96:98].rearrange("h p t -> h (p t)"),
                                   m_dram[m[1]].rearrange("(h r) t -> h (r t)", h=2)).then_inc(m_in[m[1]], 16)
                if gg:
                    pool.wait_ge(qk_out[gg[1]], 96 * gg[0] + 96)
                    if bk:
                        pool.wait_ge(st_ps[(UNITS - 1) % UR], un(bk, UNITS - 1))
                    settle(pool)
                    d = qk_dram[gg[1]]
                    for a in range(2):
                        rows = slice(16 * a, 16 * a + 16)
                        pool.dma_start(kdiag[gg[1]][48 * a:48 * a + 48, :, a, :],
                                       d[1, :, rows, :].rearrange("g x (p t) -> g x p t", p=PAIRS)).then_inc(qk_in[gg[1]], 16)
                        pool.dma_start(qpack[gg[1]][48 * a:48 * a + 48].rearrange("r p t -> r (p t)"),
                                       d[0, :, rows, :]).then_inc(qk_in[gg[1]], 16)
                if r1:
                    pool.wait_ge(rt_ss, n(r1))
                    if r1[1] == 0 and not first(r1, 2):
                        pool.wait_ge(rl[1], r1[0])
                    sl = slice(2 * r1[1], 2 * r1[1] + 2)
                    g.tensor_tensor(rnm[:, sl], rss[:, sl], powers[:, 2:4], ALU.pow).then_inc(rt_pow, 1)
                next_scatter()
                if par == 0 and (s is None or 6 <= s < 6 + B):
                    pool.wait_ge(row_ok, q - 2)
                    scatter(q - 3, 0)

            for i in range(2):
                pool.dma_start(kdiag[i][96:98], head_select).then_inc(s_zero, 16)
            pool.wait_ge(s_dummy, 16 * 9)
            pool.wait_ge(s_zero, 32)
            run_steps(pool, step)
            pool.wait_ge(sc_done, 16 * 4 * B)
            for p_ in range(2):
                pool.wait_ge(h2_out[p_], 8 * B)

            def add(j, r, guard):
                pool.wait_ge(yg_ok, j + 1)
                if guard:
                    pool.wait_ge(add_done, 16 * j)
                settle(pool)
                g.indirect_dma_start(out, bass.IndirectOffsetOnAxis(ap=xs[r][:, C + 1:C + 2].bitcast(U32), axis=0),
                                     ygate[r % 2], None, compute_op=ALU.add).then_inc(add_done, 16)
            for r in range(4):
                add(r, r, r > 0)
            with pool.Fori(1, BLOCKS // 4) as t:
                for r in range(4):
                    add(4 * t + r, r, True)
            pool.wait_ge(add_done, 16 * BLOCKS)



_INS = ["x", "txt", "L0_tok_W", "L0_tok_b", "L0_tok_cls_token", "L0_attn_w_qkv", "L0_attn_b_qkv", "L0_attn_w_out",
        "L0_attn_b_out", "L0_ffn_router_w", "L0_ffn_probe_w", "L0_ffn_router_emb", "L0_ffn_fatigue", "L0_ffn_energy",
        "L0_ffn_w_fast1", "L0_ffn_w_slow1", "L0_ffn_h_fast1", "L0_ffn_m_gate1", "L0_ffn_b1", "L0_ffn_w_fast2",
        "L0_ffn_w_slow2", "L0_ffn_h_fast2", "L0_ffn_m_gate2", "L0_ffn_b2"]


def kernel(**inputs):
    import concourse.bacc as bacc
    from concourse.bass_utils import run_bass_kernel_spmd

    nc = bacc.Bacc("TRN2", target_bir_lowering=False, num_devices=1)
    arrays = {f"in_{k}": np.ascontiguousarray(inputs[k]) for k in _INS}
    arrays.update({f"const_{k}": a for k, a in shape_constants().items()})
    args = [nc.dram_tensor(k, a.shape, mybir.dt.from_np(a.dtype), kind="ExternalInput").ap() for k, a in arrays.items()]
    out = nc.dram_tensor("out_rows", [N + 128, C], F32, kind="ExternalOutput").ap()
    build_program(nc, *args, out)
    r = run_bass_kernel_spmd(nc, [arrays], core_ids=[0])
    return r.results[0]["out_rows"][:N].reshape(B, T, C)
```

```python
from contextlib import ExitStack

import numpy as np

import concourse.bass as bass
from concourse import mybir

F32 = mybir.dt.float32
F32R = mybir.dt.float32r
I32 = mybir.dt.int32
U32 = mybir.dt.uint32
ALU = mybir.AluOpType
ACT = mybir.ActivationFunctionType
AX = mybir.AxisListType

B = 16
PS = 16
GRID = 7
NPATCH = GRID * GRID
TXT = 128
T = 1 + NPATCH + TXT
HT = T // 2
N = B * T
C = 192
CA, CT = 128, 64
NH, HD = 12, 16
PAIRS = NH // 2
UNITS = 2 * PAIRS
UR = 4
KC = 3 * PS * PS // 128
E, H, TOPK, DR = 8, 768, 2, 24
HC = H // 128
CAP = N + 128
BLOCKS = (TOPK * N + E * 127) // 128
LIST_TILES = -(-N // 128)
ROWS = E * CAP + 8 * 128
WCOLS = 2 * H + HC * C
ROW = C + 2
OW = -(-3 * T // 32) * 32
RC = 2 * E + DR
SCALE = HD ** -0.5
NTOK = B * GRID

K_ID, K_TRI = 0, 128
K_ONE = K_TRI + HT
K_DESC = K_ONE + 128
K_BASE = K_DESC + 4 * E
K_TOK = K_BASE + 4 * E
K_JJ = K_TOK + 4
K_KK = K_JJ + BLOCKS
K_CUM = K_KK + LIST_TILES
K_COLS = K_CUM + E * E


def shape_constants():
    c = np.zeros((128, K_COLS), np.float32)
    c[:, K_ID:K_ID + 128] = np.eye(128)
    c[:HT, K_TRI:K_TRI + HT] = np.triu(np.ones((HT, HT)), 1)
    c[:, K_ONE:K_ONE + 128] = 1
    c[:, K_DESC:K_DESC + 4 * E] = np.tile(E - np.arange(E), 4)
    c[:, K_BASE:K_BASE + 4 * E] = np.tile(CAP * np.arange(E), 4)
    p = np.arange(128)
    for i in range(4):
        c[:, K_TOK + i] = (i // 2) * T + (i % 2) * HT + p
    c[:, K_JJ:K_JJ + BLOCKS] = np.arange(BLOCKS)
    c[:, K_KK:K_KK + LIST_TILES] = 128 * np.arange(LIST_TILES)
    c[:, K_CUM:K_CUM + E * E] = np.tril(np.ones((E, E))).ravel()
    sel = np.zeros((2, PAIRS, 2, T), np.float32)
    sel[0, :, 0], sel[1, :, 1] = 1, 1
    empty = np.zeros((128, ROW), np.float32)
    empty[:, C + 1] = (N + p).astype(np.uint32).view(np.float32)
    return {"shape_consts": c, "head_select": sel, "empty_slots": empty}


def build_program(nc, x, txt, tok_w, tok_b, cls, w_qkv, b_qkv, w_out, b_out, router_w, probe_w, router_emb,
                  fatigue, energy, w_fast1, w_slow1, h_fast1, m_gate1, b1, w_fast2, w_slow2, h_fast2,
                  m_gate2, b2, shape_consts, head_select, empty_slots, out):
    ctx = ExitStack()
    with ctx:
        def sb(name, shape, dt=F32):
            return ctx.enter_context(nc.sbuf_tensor(name, shape, dt))

        def pb(name, shape, dt=F32):
            return ctx.enter_context(nc.psum_tensor(name, shape, dt))

        def sem(name):
            return ctx.enter_context(nc.semaphore(name))

        def sems(name, n):
            return [sem(f"{name}{i}") for i in range(n)]

        h_dram = nc.dram_tensor("h_tokens", [N, C], F32, kind="Internal").ap()
        qk_dram = [nc.dram_tensor(f"qk_split{i}", [2, 3, 2 * HD, PAIRS * T], F32, kind="Internal").ap() for i in range(2)]
        m_dram = [nc.dram_tensor(f"neg_max{i}", [2 * NH, HT], F32, kind="Internal").ap() for i in range(2)]
        emb_dram = nc.dram_tensor("patch_rows", [B * GRID, GRID, C], F32, kind="Internal").ap()
        slots_dram = nc.dram_tensor("slots", [ROWS, ROW], F32, kind="Internal").ap()

        kon = sb("kon", [128, K_COLS])
        ident = kon[:, K_ID:K_ID + 128]
        empty = sb("empty", [128, ROW])
        experts = sb("experts", [128, E, WCOLS])
        stage_s = sb("stage_s", [128, WCOLS])
        stage_h = sb("stage_h", [128, WCOLS])
        mg = sb("mg", [128, 2, E])
        b2_bc = sb("b2_bc", [128, E, C])
        wqkv_hi = sb("wqkv_hi", [128, 3 * C], F32R)
        wqkv_lo = sb("wqkv_lo", [128, 3 * C], F32R)
        wqkv_t1 = sb("wqkv_t1", [CT, 3 * C], F32R)
        wqkv_t2 = sb("wqkv_t2", [128, 3 * C], F32R)
        wout = sb("wout", [128, 3, C])
        wroute = sb("wroute", [128, 2, RC])
        bqk = sb("bqk", [128, 3])
        bv_bc = sb("bv_bc", [HT, 2, C])
        bias_e = sb("bias_e", [HT, 4, E])
        powers = sb("powers", [HT, 4])
        hA = [sb(f"hA{i}", [HT, 2, C]) for i in range(2)]
        hR = [sb(f"hR{i}", [HT, 2, C]) for i in range(2)]
        st1 = [sb(f"st1_{i}", [HT, 2, 6]) for i in range(2)]
        mv1 = [sb(f"mv1_{i}", [HT, 2, 2]) for i in range(2)]
        rs1 = [sb(f"rs1_{i}", [HT, 2, 2]) for i in range(2)]
        st2 = [sb(f"st2_{i}", [HT, 2, 6]) for i in range(2)]
        mv2 = [sb(f"mv2_{i}", [HT, 2, 2]) for i in range(2)]
        rs2 = [sb(f"rs2_{i}", [HT, 2, 2]) for i in range(2)]
        xn = sb("xn", [HT, 2, 256])
        xa_hi = sb("xa_hi", [128, T], F32R)
        xa_lo = sb("xa_lo", [128, T], F32R)
        xt = sb("xt", [128, T], F32R)
        qk_hi = sb("qk_hi", [128, 3, T], F32R)
        qk_lo = sb("qk_lo", [128, 3, T], F32R)
        qpack = [sb(f"qpack{i}", [98, PAIRS, T], F32R) for i in range(2)]
        kdiag = [sb(f"kdiag{i}", [98, PAIRS, 2, T], F32R) for i in range(2)]
        vaug = [sb(f"vaug{i}", [HT, 2, NH, 32]) for i in range(2)]
        vtmp = sb("vtmp", [HT, 2 * C])
        mx = sb("mx", [HT, 2, PAIRS, 2])
        mT = sb("mT", [2 * NH, HT], F32R)
        probs = sb("probs", [HT, 2, 2, T])
        work = sb("work", [128, 3, OW])
        o_raw, o_tr, o_out = (work[:, i, :] for i in range(3))
        o_nrm = o_out[:, 0:3 * T].rearrange("p (g t) -> p g t", g=3)
        osum = sb("osum", [128, OW // 32])
        xn2 = sb("xn2", [HT, 2, 2, C])
        xn2T = sb("xn2T", [128, 2, T])
        rt = sb("rt", [HT, 4, RC])
        rsq = sb("rsq", [HT, 4, DR])
        rss = sb("rss", [HT, 4])
        rnm = sb("rnm", [HT, 4])
        rinv = sb("rinv", [HT, 4])
        lg = sb("lg", [HT, 4, E])
        lg2 = sb("lg2", [HT, 4, E])
        top = sb("top", [HT, 2, 4])
        cand = sb("cand", [HT, 4, E])
        cmx = sb("cmx", [HT, 4])
        hot = sb("hot", [HT, 2, 4, E])
        cum = sb("cum", [HT, 5, E])
        dlt = sb("dlt", [HT, 4])
        edl = sb("edl", [HT, 4])
        gates = sb("gates", [HT, 2, 4])
        rank = sb("rank", [HT, 4, E])
        rsel = sb("rsel", [HT, 2, 4, E])
        rowf = sb("rowf", [HT, 2, 4])
        rowi = sb("rowi", [HT, 2, 4], U32)
        tokf = sb("tokf", [HT, 4])
        slot_rows = sb("slot_rows", [HT, 4, 2, ROW])
        cnt = sb("cnt", [1, E])
        tcmp = sb("tcmp", [1, E, LIST_TILES])
        nblk = sb("nblk", [1, E])
        tcum = sb("tcum", [1, E, E])
        ends = sb("ends", [1, E])
        tge = sb("tge", [1, BLOCKS, E])
        twt = sb("twt", [1, E])
        trow = sb("trow", [1, BLOCKS, E])
        tabf = sb("tabf", [1, 2 * BLOCKS + E])
        tabi = sb("tabi", [1, 2 * BLOCKS + E], I32)
        xs = [sb(f"xs{i}", [128, ROW]) for i in range(4)]
        sxa = [sb(f"sxa{i}", [128, 128]) for i in range(2)]
        sxt = [sb(f"sxt{i}", [CT + 1, 128]) for i in range(2)]
        relu = [stage_s[:, 0:H], stage_s[:, H:2 * H]]
        hid = [stage_h[:, 0:H], stage_h[:, H:2 * H]]
        flat = work[:].rearrange("p a t -> p (a t)")
        hidT = flat[:, 0:H].rearrange("p (k t) -> p k t", k=HC)
        ysum = [flat[:, H + i * C:H + (i + 1) * C] for i in range(2)]
        ygate = [flat[:, H + (2 + i) * C:H + (3 + i) * C] for i in range(2)]

        pS = [pb(f"pS{i}", [128, 512]) for i in range(2)]
        pT = [pb(f"pT{i}", [128, 512]) for i in range(2)]
        pX = pb("pX", [128, 512])
        pQ = pb("pQ", [128, 512])
        pR = pb("pR", [128, 512])
        pV = pb("pV", [128, 512])

        def p_rank(): return pV[0:HT, 464:464 + 4 * E]

        s_kon, s_tw, s_wq, s_wo, s_sm = (sem(n) for n in ("s_kon", "s_tw", "s_wq", "s_wo", "s_sm"))
        s_x = sems("s_x", 3)
        patch_tr, patch_ta, patch_tv, patch_mm, emb_ok = (sem(n) for n in (
            "patch_tr", "patch_ta", "patch_tv", "patch_mm", "emb_ok"))
        s_emb_st, s_hd, s_zero, s_dummy = (sem(n) for n in ("s_emb_st", "s_hd", "s_zero", "s_dummy"))
        fast_in, slow_in, hebb_in = (sem(n) for n in ("fast_in", "slow_in", "hebb_in"))
        v_pre, a_pre, t_pre, g_pre = sem("v_pre"), sem("a_pre"), sem("t_pre"), sem("g_pre")
        hA_in, hR_in = sems("hA_in", 2), sems("hR_in", 2)
        qk_out, qk_in, m_out, m_in = sems("qk_out", 2), sems("qk_in", 2), sems("m_out", 2), sems("m_in", 2)
        h2_out = sems("h2_out", 2)
        (ln1_st, ln1_mv, ln1_pe, ln1_pow, xn_ok, ln2_st, ln2_mv, ln2_pe, ln2_pow, xn2_ok) = (sem(n) for n in (
            "ln1_st", "ln1_mv", "ln1_pe", "ln1_pow", "xn_ok", "ln2_st", "ln2_mv", "ln2_pe", "ln2_pow", "xn2_ok"))
        (xT_ps, xT_hi, xT_lo, v_ps, v_ok, va_ok, qk_ps, qk_hi_ok, qk_lo_ok, mT_ps, mT_ok, o_cp, o_tr_ok, o_rc, o_mul, o_ok,
         y_ps, h2_ok) = (sem(n) for n in (
             "xT_ps", "xT_hi", "xT_lo", "v_ps", "v_ok", "va_ok", "qk_ps", "qk_hi_ok", "qk_lo_ok", "mT_ps", "mT_ok",
             "o_cp", "o_tr_ok", "o_rc", "o_mul", "o_ok", "y_ps", "h2_ok"))
        s_ps, mx_ok, st_ps, ex_ok, pv_ok = (sems(n, UR) for n in ("s_ps", "mx_ok", "st_ps", "ex_ok", "pv_ok"))
        x2T_ps, x2T_ok, rt_ps, rt_cp, rt_sq, rt_ss, rt_pow = (sem(n) for n in (
            "x2T_ps", "x2T_ok", "rt_ps", "rt_cp", "rt_sq", "rt_ss", "rt_pow"))
        (nm_floor, nm_inv, align_ok, lin_ok, lg_ok, lg2_ok, cum_cp, cum_ok, rank_ok, den_ok, gate0_ok, gate1_ok, rsel_ok,
         rowf_ok) = (sem(n) for n in ("nm_floor", "nm_inv", "align_ok", "lin_ok", "lg_ok", "lg2_ok", "cum_cp", "cum_ok",
                                      "rank_ok", "den_ok", "gate0_ok", "gate1_ok", "rsel_ok", "rowf_ok"))
        pick_max, pick_eq, pick_order, pick_best, hot_ok = (sems(n, 2) for n in (
            "pick_max", "pick_eq", "pick_order", "pick_best", "hot_ok"))
        (dl_ok, ed_ok, rank_ps, row_ok, sc_done, wprep) = (sem(n) for n in (
            "dl_ok", "ed_ok", "rank_ps", "row_ok", "sc_done", "wprep"))
        slot_cp, settled = sem("slot_cp"), sem("settled")
        cnt_ps, tab_ok, tch, pad_done = (sem(n) for n in ("cnt_ps", "tab_ok", "tch", "pad_done"))
        (sx_ps, sx_ok, u_ps, relu_ok, hid_ok, hT_ps, hT_a, hT_v, y2_ps, ys_ok, yg_ok, add_done) = (
            sem(n) for n in ("sx_ps", "sx_ok", "u_ps", "relu_ok", "hid_ok", "hT_ps", "hT_a",
                             "hT_v", "y2_ps", "ys_ok", "yg_ok", "add_done"))
        xs_in = sems("xs_in", 4)

        FIRST, LAST = -1, B + 6
        LOOP0, LOOP1 = 4, 7

        WARM_FILL, WARM_DRAIN = 22, 14
        S0 = 3

        def settle(eng):
            eng.sem_inc(settled, 1)

        def run_steps(eng, step):
            for s in range(FIRST, 2 * LOOP0):
                step(s // 2, s % 2, s)
            with eng.Fori(LOOP0, LOOP1) as t:
                step(t, 0, None)
                step(t, 1, None)
            for s in range(2 * LOOP1, LAST + 1):
                step(s // 2, s % 2, s)

        def batch(q, par, off, s):
            if s is not None and not 0 <= s + off < B:
                return None
            return q + (par + off) // 2, (par + off) % 2

        def n(b, back=0):
            return 2 * b[0] + b[1] + 1 - back

        def un(b, u, back=0):
            return UNITS // UR * (n(b, back) - 1) + u // UR + 1

        def first(b, k=1):
            return isinstance(b[0], int) and 2 * b[0] + b[1] < k

        def expert_loads(dst, wA, wB, e):
            ee = bass.ds(e, 1)
            A = wA[ee].rearrange("a k h -> (a k) h")
            return ((dst[:, 0:H], A[0:CA, :]), (dst[0:CT, H:2 * H], A[CA:C, :]),
                    (dst[:, 2 * H:].rearrange("p (k c) -> p k c", k=HC), wB[ee].rearrange("a (k p) c -> p (a k) c", p=128)))

        def expert(e):
            return experts[:, bass.ds(e, 1), :].rearrange("p a w -> p (a w)")

        xp3 = experts[0:NTOK, 4:6, :].rearrange("p a w -> p (a w)")[:, 0:3 * PS * PS * GRID]
        xq3 = experts[0:NTOK, 6:8, :].rearrange("p a w -> p (a w)")[:, 0:3 * PS * PS * GRID]
        tokw = experts[:, 3, 0:KC * C].rearrange("p (k n) -> p k n", k=KC)
        pT_sb = experts[:, 2, 0:KC * NTOK * 2].rearrange("p (r k n) -> p r k n", r=2, k=KC)
        emb = experts[0:NTOK, 1, 0:GRID * C].rearrange("p (w n) -> p w n", w=GRID)
        tokb = experts[0:NTOK, 1, GRID * C:GRID * C + C]
        wqk_in = stage_s[:, 0:3 * 256].rearrange("p (g c) -> p g c", g=3)
        wv_in = stage_s[0:96, 3 * 256:5 * 256].rearrange("p (g c) -> p g c", g=2)
        wo_in = stage_s[0:96, 1536:1536 + 2 * 384].rearrange("p (e w) -> p e w", e=2)
        r_in = stage_h[0:E, 0:C]
        pr_in = stage_h[0:DR, C:2 * C]
        em_in = stage_h[0:E, 2 * C:2 * C + DR]
        r_sc = stage_h[0:E, 512:560]
        nT_sb = stage_h[0:DR, 560:568]
        fe_in = stage_h[0:HT, 576:592]
        small_loads = 15
        PRE_LO = (2, 4)
        PRE_X = PRE_LO[1] + 2
        PRE_SS = PRE_X + 2
        PRE_EMBN = PRE_SS + 5
        PRE_NT = PRE_EMBN + 1
        PRE_V = PRE_NT + 4
        PRE_STAGE, PRE_T, PRE_G = 11, 5, 3

        def patch_views(c):
            src = xp3[:, c * PS * PS * GRID:(c + 1) * PS * PS * GRID].rearrange("p (i w j) -> p w i j", i=PS, w=GRID)
            return src, xq3.rearrange("p (w c i j) -> p w c i j", w=GRID, c=3, i=PS)[:, :, c]

        block = ctx.enter_context(nc.Block())

        @block.sync
        def _(sp):
            for c in range(3):
                sp.dma_start(xp3[:, c * PS * PS * GRID:(c + 1) * PS * PS * GRID],
                             x[:, c].rearrange("b (h i) w -> b h (i w)", i=PS)).then_inc(s_x[c], 16)
            sp.dma_start(tokw, tok_w.rearrange("(k p) n -> p k n", p=128)).then_inc(s_tw, 16)
            hd3 = h_dram.rearrange("(b t) c -> b t c", t=T)
            sp.dma_start(hd3[:, 0, :], cls[0].to_broadcast([B, C])).then_inc(s_hd, 16)
            sp.dma_start(hd3[:, 1 + NPATCH:T, :], txt).then_inc(s_hd, 16)
            sp.dma_start(r_in, router_w).then_inc(s_sm, 16)
            sp.dma_start(pr_in, probe_w).then_inc(s_sm, 16)
            sp.dma_start(em_in, router_emb).then_inc(s_sm, 16)
            sp.dma_start(fe_in[:, 0:E], energy.rearrange("(a n) -> a n", a=1).to_broadcast([HT, E])).then_inc(s_sm, 16)
            sp.dma_start(fe_in[:, E:2 * E], fatigue.rearrange("(a n) -> a n", a=1).to_broadcast([HT, E])).then_inc(s_sm, 16)
            sp.dma_start(mg[:, 0, :], m_gate1.rearrange("(a n) -> a n", a=1).to_broadcast([128, E])).then_inc(s_sm, 16)
            sp.dma_start(mg[:, 1, :], m_gate2.rearrange("(a n) -> a n", a=1).to_broadcast([128, E])).then_inc(s_sm, 16)
            sp.dma_start(b2_bc[:], b2.rearrange("(a e) n -> a (e n)", a=1).to_broadcast([128, E * C]).rearrange(
                "p (e n) -> p e n", e=E)).then_inc(s_sm, 16)
            for a in range(2):
                sp.dma_start(bv_bc[:, a, :], b_qkv[2 * C:3 * C].rearrange("(a n) -> a n", a=1).to_broadcast([HT, C])).then_inc(s_sm, 16)
            sp.dma_start(empty[:], empty_slots).then_inc(s_sm, 16)
            sp.wait_ge(s_sm, 16 * small_loads)
            sp.dma_start(slots_dram[E * CAP:, :].rearrange("(k p) c -> p k c", p=128),
                         empty[:].unsqueeze(1).to_broadcast([128, 8, ROW])).then_inc(s_dummy, 16)
            sp.dma_start(out[N:N + 128, :], empty[:, 0:C]).then_inc(s_dummy, 16)
            sp.wait_ge(emb_ok, GRID)
            hdp = hd3[:, 1:1 + NPATCH, :].rearrange("b (h w) c -> b h w c", h=GRID)
            sp.dma_start(emb_dram, emb).then_inc(s_emb_st, 16)
            sp.wait_ge(s_emb_st, 16)
            sp.dma_start(hd3[:, 1:1 + NPATCH, :], emb_dram.rearrange("(b h) w c -> b (h w) c", h=GRID)).then_inc(s_hd, 16)
            sp.wait_ge(s_hd, 48)

            def load_hA(b):
                if not first(b, 2):
                    sp.wait_ge(xn_ok, n(b, 2))
                sp.dma_start(hA[b[1]][:], h_dram[bass.ds((2 * b[0] + b[1]) * T, T), :].rearrange(
                    "(a p) c -> p a c", a=2)).then_inc(hA_in[b[1]], 16)

            def load_fast(e):
                for dst, src in expert_loads(expert(e), w_fast1, w_fast2, e):
                    sp.dma_start(dst, src).then_inc(fast_in, 16)
                sp.dma_start(experts[CT:CT + 1, bass.ds(e, 1), H:2 * H].rearrange("p a w -> p (a w)"),
                             b1[bass.ds(e, 1), :]).then_inc(fast_in, 16)

            def load_slow(e):
                for dst, src in expert_loads(stage_s, w_slow1, w_slow2, e):
                    sp.dma_start(dst, src).then_inc(slow_in, 16)

            def step(q, par, s):
                a2, f, m, bk, r1 = (batch(q, par, o, s) for o in (2, 0, -2, -3, -4))
                if s == FIRST:
                    load_hA((0, 0))
                if a2:
                    load_hA(a2)
                if bk:
                    if not first(bk, 2):
                        sp.wait_ge(xn2_ok, n(bk, 2))
                        settle(sp)
                        sp.wait_ge(h2_out[bk[1]], 16 * bk[0])
                    sp.dma_start(hR[bk[1]][:], h_dram[bass.ds((2 * bk[0] + bk[1]) * T, T), :].rearrange(
                        "(a p) c -> p a c", a=2)).then_inc(hR_in[bk[1]], 16)
                if r1:
                    sp.wait_ge(h2_ok, n(r1))
                    sp.dma_start(out[bass.ds((2 * r1[0] + r1[1]) * T, T), :].rearrange("(a p) c -> p a c", a=2),
                                 hR[r1[1]][:]).then_inc(h2_out[r1[1]], 16)
                if par == 0 and (s is None or 0 <= s < 2 * E):
                    load_fast(q)
                if s == 0:
                    sp.wait_ge(a_pre, PRE_STAGE)
                    sp.wait_ge(t_pre, PRE_T)
                    sp.wait_ge(v_pre, PRE_V)
                    sp.wait_ge(g_pre, PRE_G)
                    load_slow(q)
                if m:
                    sp.wait_ge(mT_ok, n(m))
                    sp.dma_start(m_dram[m[1]], mT[:].bitcast(F32)).then_inc(m_out[m[1]], 16)
                if f:
                    d = qk_dram[f[1]]
                    sp.wait_ge(qk_hi_ok, 3 * n(f))
                    settle(sp)
                    if not first(f, 2):
                        sp.wait_ge(qk_in[f[1]], 64 * f[0])
                        settle(sp)
                        sp.wait_ge(qk_out[f[1]], 96 * f[0])
                    qk_rows = lambda tile, i: tile[64 * i:64 * i + 64].rearrange("x c t -> x (c t)").bitcast(F32)
                    d_rows = lambda i, g: d[i, g].rearrange("x (w y) -> (x w) y", w=2)
                    for i, g in ((0, 0), (0, 2), (1, 0), (1, 1)):
                        sp.dma_start(d_rows(i, g), qk_rows(qk_hi, i)).then_inc(qk_out[f[1]], 16)
                    sp.wait_ge(qk_lo_ok, 3 * n(f))
                    for i, g in ((0, 1), (1, 2)):
                        sp.dma_start(d_rows(i, g), qk_rows(qk_lo, i)).then_inc(qk_out[f[1]], 16)
                if par == 0 and (s is None or 0 < s < 2 * E):
                    sp.wait_ge(wprep, q)
                    load_slow(q)

            run_steps(sp, step)
            sp.wait_ge(tab_ok, 1)
            for e in range(E):
                row = sp.value_load(tabi[0:1, 2 * BLOCKS + e:2 * BLOCKS + e + 1], min_val=0, max_val=E * CAP)
                sp.dma_start(slots_dram[bass.ds(row, 128), :], empty[:]).then_inc(pad_done, 16)
            sp.wait_ge(pad_done, 16 * E)
            sp.wait_ge(sc_done, 16 * TOPK * 2 * B)

            def load_tile(j, r, guard):
                row = sp.value_load(tabi[0:1, bass.ds(j, 1)], min_val=0, max_val=ROWS - 128)
                if guard:
                    sp.wait_ge(add_done, 16 * (j - 3))
                sp.dma_start(xs[r][:], slots_dram[bass.ds(row, 128), :]).then_inc(xs_in[r], 16)
            for r in range(4):
                load_tile(r, r, False)
            with sp.Fori(1, BLOCKS // 4) as t:
                for r in range(4):
                    load_tile(4 * t + r, r, True)
            for p in range(2):
                sp.wait_ge(h2_out[p], 16 * B // 2)

        @block.tensor
        def _(pe):
            mm = nc.tensor.matmul
            tr = nc.tensor.transpose

            def keep_warm(k, bank=pX):
                for _ in range(k):
                    mm(bank[:, 0:128], ident, ident, start=True, stop=True)

            pe.wait_ge(s_kon, 16)
            pe.wait_ge(a_pre, 3)
            for g in range(3):
                tr(pS[0][:, g * 128:(g + 1) * 128], wqk_in[:, g, 0:128], ident)
                last = tr(pS[1][:, g * 128:(g + 1) * 128], wqk_in[:, g, 128:256], ident)
            last.then_inc(t_pre, 1)
            for g in range(2):
                tr(pT[0][:, g * 96:(g + 1) * 96], wv_in[:, g, 0:128], ident[0:96, 0:96])
                last = tr(pT[1][:, g * 96:(g + 1) * 96], wv_in[:, g, 128:256], ident[0:96, 0:96])
            last.then_inc(t_pre, 1)
            pe.wait_ge(s_wo, 16 * 3)
            for eh in range(2):
                for g in range(3):
                    last = tr(pQ[:, g * 96:(g + 1) * 96] if eh == 0 else pR[:, g * 96:(g + 1) * 96],
                              wo_in[:, eh, g * 128:(g + 1) * 128], ident[0:96, 0:96])
            last.then_inc(t_pre, 1)

            def transpose_patches(w):
                banks = pS if w % 2 == 0 else (pQ, pR)
                if w > 1:
                    pe.wait_ge(patch_ta, w - 1)
                    pe.wait_ge(patch_tv, w - 1)
                for k in range(KC):
                    c0 = (w * KC + k) * 128
                    last = tr(banks[k // 3][:, (k % 3) * NTOK:(k % 3 + 1) * NTOK], xq3[:, c0:c0 + 128], ident[0:NTOK, 0:NTOK])
                last.then_inc(patch_tr, 1)

            pe.wait_ge(a_pre, PRE_STAGE)
            pe.wait_ge(v_pre, PRE_X)
            pe.wait_ge(s_tw, 32)
            transpose_patches(0)
            for w in range(GRID):
                if w + 1 < GRID:
                    transpose_patches(w + 1)
                pe.wait_ge(patch_ta, w + 1)
                pe.wait_ge(patch_tv, w + 1)
                if w > 1:
                    pe.wait_ge(emb_ok, w - 1)
                for k in range(KC):
                    last = mm(pT[w % 2][0:NTOK, 0:C], pT_sb[:, w % 2, k, :], tokw[:, k, :], start=(k == 0), stop=(k == KC - 1))
                last.then_inc(patch_mm, 1)
            pe.wait_ge(v_pre, PRE_EMBN)
            tr(pX[0:DR, 448:448 + E], em_in, ident[0:E, 0:E]).then_inc(t_pre, 1)
            pe.wait_ge(v_pre, PRE_NT)
            for c, (c0, w) in enumerate(((0, CA), (CA, CT))):
                tr(pV[0:w, c * 64:c * 64 + E], r_in[:, c0:c0 + w], ident[0:E, 0:E])
                tr(pV[0:w, c * 64 + 16:c * 64 + 16 + DR], pr_in[:, c0:c0 + w], ident[0:DR, 0:DR])
                last = mm(pV[0:w, c * 64 + 8:c * 64 + 16], pr_in[:, c0:c0 + w], nT_sb, start=True, stop=True)
            last.then_inc(t_pre, 1)

            def step(q, par, s):
                f, g, m, bk, r1 = (batch(q, par, o, s) for o in (0, -1, -2, -3, -4))
                ranks = par == 0 and (s is None or 6 <= s < 6 + B)

                def scores(u):
                    p, a = u // 2, u % 2
                    if u == 0:
                        pe.wait_ge(qk_in[m[1]], 64 * m[0] + 64)
                    if u < 2:
                        if g:
                            pe.wait_ge(qk_hi_ok, 3 * n(g))
                            pe.wait_ge(qk_lo_ok, 3 * n(g))
                        else:
                            pe.wait_ge(mT_ok, n(m, 1))
                            pe.wait_ge(mx_ok[(UNITS - 1) % UR], un(m, UNITS - 1, 1))
                    else:
                        pe.wait_ge(mx_ok[(u - 2) % UR], un(m, u - 2))
                    mm(pS[u % 2][0:HT, 0:2 * T], qpack[m[1]][0:96, p, a * HT:(a + 1) * HT], kdiag[m[1]][0:96, p, :, :],
                       start=True, stop=True).then_inc(s_ps[u % UR], 1)

                def values(u):
                    p, a = u // 2, u % 2
                    pe.wait_ge(ex_ok[u % UR], un(bk, u))
                    if u == 0:
                        pe.wait_ge(va_ok, n(bk))
                        if first(bk):
                            pe.wait_ge(a_pre, PRE_STAGE)
                        else:
                            pe.wait_ge(o_cp, 2 * n(bk, 1))
                    for hh in range(2):
                        h = 2 * p + hh
                        gg, j = h // 4, h % 4
                        dst = (pQ[:, gg * T:(gg + 1) * T] if gg < 2 else pR[:, 0:T])[32 * j:32 * j + 32]
                        last = mm(dst, vaug[bk[1]][:, a, h, :], probs[:, u % 2, hh, :], start=(a == 0), stop=(a == 1))
                    last.then_inc(pv_ok[u % UR], 1)

                for u in range(UNITS):
                    p, a = u // 2, u % 2
                    if s == 2 and u == 0:
                        keep_warm(WARM_FILL, pT[0])
                    if m and S0 <= u < S0 + UNITS // 2:
                        scores(2 * (u - S0))
                    if bk:
                        if u == 0:
                            pe.wait_ge(m_in[bk[1]], 16 * bk[0] + 16)
                        if u < 2:
                            if not first(bk):
                                pe.wait_ge(ex_ok[(UNITS - 2 + u) % UR], un(bk, UNITS - 2 + u, 1))
                        else:
                            pe.wait_ge(ex_ok[(u - 2) % UR], un(bk, u - 2))
                        for hh in range(2):
                            last = mm(pT[u % 2][0:HT, hh * T:(hh + 1) * T], kdiag[bk[1]][0:98, p, hh, a * HT:(a + 1) * HT],
                                      qpack[bk[1]][0:98, p, :], start=True, stop=True)
                        last.then_inc(st_ps[u % UR], 1)
                    if m and S0 <= u < S0 + UNITS // 2:
                        scores(2 * (u - S0) + 1)
                    if bk and u:
                        values(u - 1)
                    if s is not None and s > B and bk and u <= 8:
                        keep_warm(1)
                    if u == 0 and f:
                        pe.wait_ge(xn_ok, n(f))
                        if r1 and not first(r1):
                            pe.wait_ge(x2T_ok, n(r1, 1))
                        elif g:
                            pe.wait_ge(xT_lo, n(g))
                        for a_ in range(2):
                            tr(pX[:, a_ * HT:(a_ + 1) * HT], xn[:, a_, 0:CA], ident[0:HT, 0:HT])
                            last = tr(pX[:, T + a_ * HT:T + (a_ + 1) * HT], xn[:, a_, CA:256], ident[0:HT, 0:HT])
                        last.then_inc(xT_ps, 1)
                    if u == 2 and r1:
                        pe.wait_ge(o_ok, n(r1))
                        if g:
                            pe.wait_ge(v_ok, n(g))
                        for a_ in range(2):
                            for gg in range(3):
                                last = mm(pV[0:HT, a_ * C:(a_ + 1) * C], o_nrm[:, gg, a_ * HT:(a_ + 1) * HT], wout[:, gg, :],
                                          start=(gg == 0), stop=(gg == 2))
                        last.then_inc(y_ps, 1)
                    if u == 9 and m:
                        pe.wait_ge(mx_ok[(UNITS - 1) % UR], un(m, UNITS - 1))
                        pe.wait_ge(mx_ok[(UNITS - 2) % UR], un(m, UNITS - 2))
                        tr(pS[0][0:2 * NH, 0:HT], mx[:].rearrange("p h k a -> p (h k a)"), ident[0:HT, 0:HT]).then_inc(mT_ps, 1)
                    if u == 9 and r1:
                        pe.wait_ge(xn2_ok, n(r1))
                        if f:
                            pe.wait_ge(xT_lo, n(f))
                            pe.wait_ge(xT_hi, n(f))
                        for a_ in range(2):
                            tr(pX[:, a_ * HT:(a_ + 1) * HT], xn2[:, r1[1], a_, 0:CA], ident[0:HT, 0:HT])
                            last = tr(pX[0:CT, T + a_ * HT:T + (a_ + 1) * HT], xn2[:, r1[1], a_, CA:C], ident[0:HT, 0:HT])
                        last.then_inc(x2T_ps, 1)
                    if u == 11 and r1:
                        pe.wait_ge(x2T_ok, n(r1))
                        pe.wait_ge(h2_ok, n(r1))
                        for a_ in range(2):
                            dst = pV[0:HT, 384 + a_ * RC:384 + (a_ + 1) * RC]
                            mm(dst, xn2T[:, 0, a_ * HT:(a_ + 1) * HT], wroute[:, 0, :], start=True, stop=False)
                            last = mm(dst, xn2T[0:CT, 1, a_ * HT:(a_ + 1) * HT], wroute[0:CT, 1, :], start=False, stop=True)
                        last.then_inc(rt_ps, 1)
                    if u == 11 and ranks:
                        pe.wait_ge(cum_ok, 4 * (q - 2))
                        if r1:
                            pe.wait_ge(h2_ok, n(r1))
                        mm(p_rank(), kon[0:HT, K_TRI:K_TRI + HT], hot[:, 0, :, :], start=True, stop=False)
                        mm(p_rank(), kon[0:HT, K_TRI:K_TRI + HT], hot[:, 1, :, :], start=False, stop=False)
                        mm(p_rank(), kon[0:HT, K_ONE:K_ONE + HT], cum[:, 0:4, :], start=False, stop=True).then_inc(rank_ps, 1)
                if bk:
                    values(UNITS - 1)
                if f:
                    pe.wait_ge(xT_hi, n(f))
                    pe.wait_ge(xT_lo, n(f))
                    if m:
                        pe.wait_ge(mT_ok, n(m))
                    elif g:
                        pe.wait_ge(qk_hi_ok, 3 * n(g))
                        pe.wait_ge(qk_lo_ok, 3 * n(g))
                    if first(f):
                        pe.wait_ge(v_pre, PRE_V)
                    for i in range(3):
                        w = slice(i * 128, (i + 1) * 128)
                        o = pS[0][:, i * T:(i + 1) * T] if i < 2 else pS[1][:, 0:T]
                        mm(o, wqkv_hi[:, w], xa_hi[:], start=True, stop=False)
                        mm(o, wqkv_lo[:, w], xa_hi[:], start=False, stop=False)
                        mm(o, wqkv_hi[:, w], xa_lo[:], start=False, stop=False)
                        mm(o, wqkv_t1[:, w], xt[0:CT, :], start=False, stop=False)
                        last = mm(o, wqkv_t2[:, w], xt[:], start=False, stop=True)
                    last.then_inc(qk_ps, 1)
                    if r1:
                        pe.wait_ge(rt_cp, n(r1))
                    if ranks:
                        pe.wait_ge(rank_ok, q - 2)
                    if g:
                        pe.wait_ge(v_ok, n(g))
                    for a_ in range(2):
                        t = slice(a_ * HT, (a_ + 1) * HT)
                        o = pV[0:HT, a_ * C:(a_ + 1) * C]
                        mm(o, xa_hi[:, t], wqkv_hi[:, 2 * C:], start=True, stop=False)
                        mm(o, xa_hi[:, t], wqkv_lo[:, 2 * C:], start=False, stop=False)
                        mm(o, xa_lo[:, t], wqkv_hi[:, 2 * C:], start=False, stop=False)
                        mm(o, xt[0:CT, t], wqkv_t1[:, 2 * C:], start=False, stop=False)
                        last = mm(o, xt[:, t], wqkv_t2[:, 2 * C:], start=False, stop=True)
                    last.then_inc(v_ps, 1)

            run_steps(pe, step)
            pe.wait_ge(rank_ok, B // 2)
            pe.wait_ge(cum_ok, 4 * (B // 2))
            pe.wait_ge(h2_ok, B)
            mm(pV[:, 0:E], kon[0:HT, K_ONE:K_ONE + 128], cum[:, 4, :], start=True, stop=True).then_inc(cnt_ps, 1)

            U = [pS, pT]

            def transpose_slots(j, r, t, guard):
                pe.wait_ge(xs_in[r], 16 * t + 16)
                if guard:
                    pe.wait_ge(sx_ok, 2 * j)
                tr(pX[:, 0:128], xs[r][:, 0:CA], ident)
                tr(pX[0:CT, 128:256], xs[r][:, CA:C], ident).then_inc(sx_ps, 1)

            def up(j, par, guard, ew):
                pe.wait_ge(sx_ok, 2 * j + 2)
                if guard:
                    pe.wait_ge(relu_ok, 2 * (j - 1))
                for i, (c0, w) in enumerate(((0, 512), (512, 256))):
                    o = U[i][par][:, 0:w]
                    mm(o, sxa[par][:], experts[:, bass.ds(ew, 1), c0:c0 + w].rearrange("p a w -> p (a w)"), start=True, stop=False)
                    last = mm(o, sxt[par][:], experts[0:CT + 1, bass.ds(ew, 1), H + c0:H + c0 + w].rearrange("p a w -> p (a w)"),
                              start=False, stop=True)
                last.then_inc(u_ps, 1)

            def transpose_hidden(j, par, guard):
                if guard:
                    pe.wait_ge(hT_a, j)
                    pe.wait_ge(hT_v, j)
                for k in range(HC):
                    if k == 0:
                        pe.wait_ge(hid_ok, 2 * j + 1)
                    if k == 4:
                        pe.wait_ge(hid_ok, 2 * j + 2)
                    o = pQ if k < 3 else pR
                    last = tr(o[:, (k % 3) * 128:(k % 3 + 1) * 128], hid[par][:, k * 128:(k + 1) * 128], ident)
                last.then_inc(hT_ps, 1)

            def down(j, guard, ew):
                pe.wait_ge(hT_a, j + 1)
                pe.wait_ge(hT_v, j + 1)
                if guard:
                    pe.wait_ge(ys_ok, j)
                for k in range(HC):
                    last = mm(pV[:, 0:C], hidT[:, k, :],
                              experts[:, bass.ds(ew, 1), 2 * H + k * C:2 * H + (k + 1) * C].rearrange("p a w -> p (a w)"),
                              start=(k == 0), stop=(k == HC - 1))
                last.then_inc(y2_ps, 1)

            def expert_of(j):
                return pe.value_load(tabi[0:1, bass.ds(BLOCKS + j, 1)], min_val=0, max_val=E - 1)

            pe.wait_ge(tab_ok, 1)
            pe.wait_ge(sc_done, 16 * (TOPK * 2 * B - 1))
            keep_warm(WARM_DRAIN)
            transpose_slots(0, 0, 0, False)
            up(0, 0, False, expert_of(0))
            transpose_slots(1, 1, 0, True)

            def ffn(t, r, guard, ahead=2):
                j, par = 4 * t + r, r % 2
                e_next, e = expert_of(j + 1) if ahead else None, expert_of(j)
                transpose_hidden(j, par, guard)
                if ahead:
                    up(j + 1, 1 - par, guard, e_next)
                if ahead > 1:
                    transpose_slots(j + 2, (r + 2) % 4, t + (r + 2) // 4, True)
                down(j, guard, e)

            for r in range(4):
                ffn(0, r, r > 0)
            with pe.Fori(1, BLOCKS // 4 - 1) as t:
                for r in range(4):
                    ffn(t, r, True)
            for r in range(4):
                ffn(BLOCKS // 4 - 1, r, True, min(2, 3 - r))

        @block.scalar
        def _(act):
            sc = nc.scalar
            sc.dma_start(kon[:], shape_consts).then_inc(s_kon, 16)
            for qk in range(2):
                for pp in range(2):
                    src = w_qkv[(2 * qk + pp) * 96:(2 * qk + pp + 1) * 96, :].rearrange("(i x) c -> x i c", i=3)
                    sc.dma_start(wqk_in[64 * qk + pp:64 * qk + 64:2, :, 0:C], src).then_inc(s_wq, 16)
            sc.dma_start(wv_in[:, :, 0:C], w_qkv[2 * C:3 * C, :].rearrange("(g p) c -> p g c", p=96)).then_inc(s_wq, 16)
            sc.dma_start(tokb, tok_b.rearrange("(a n) -> a n", a=1).to_broadcast([NTOK, C])).then_inc(s_tw, 16)
            for qk in range(2):
                for pp in range(2):
                    src = b_qkv[(2 * qk + pp) * 96:(2 * qk + pp + 1) * 96].rearrange("(i x a) -> x i a", i=3, a=1)
                    sc.dma_start(bqk[64 * qk + pp:64 * qk + 64:2].unsqueeze(2), src,
                                 allow_slow_non_contiguous=True).then_inc(s_sm, 16)
            act.wait_ge(s_wq, 16 * 5)
            sc.copy(wqk_in[:, :, C:256], wqk_in[:, :, CA:C]).then_inc(a_pre, 1)
            sc.copy(wv_in[:, :, C:256], wv_in[:, :, CA:C]).then_inc(a_pre, 1)
            act.wait_ge(a_pre, 1)
            sc.mul(wqk_in[0:64], wqk_in[0:64], SCALE).then_inc(a_pre, 1)
            for rnd in range(2):
                act.wait_ge(t_pre, 1 + rnd)
                w = slice(0, 2 * C) if rnd == 0 else slice(2 * C, 3 * C)
                cols = w.stop - w.start
                banks = pS if rnd == 0 else pT
                sc.copy(wqkv_hi[:, w], banks[0][:, 0:cols]).then_inc(a_pre, 1)
                sc.copy(wqkv_t2[:, w], banks[1][:, 0:cols]).then_inc(a_pre, 1)
            act.wait_ge(t_pre, 3)
            sc.copy(wout[:, :, 0:96], pQ[:, 0:288].rearrange("p (g e) -> p g e", g=3)).then_inc(a_pre, 1)
            sc.copy(wout[:, :, 96:192], pR[:, 0:288].rearrange("p (g e) -> p g e", g=3)).then_inc(a_pre, 1)
            for c, rows in ((0, slice(0, PS)), (2, slice(0, PS // 2))):
                act.wait_ge(s_x[c], 16)
                src, dst = patch_views(c)
                sc.copy(dst[:, :, rows], src[:, :, rows]).then_inc(a_pre, 1)
            for w in range(GRID):
                act.wait_ge(patch_tr, w + 1)
                if w > 1:
                    act.wait_ge(patch_mm, w - 1)
                bank = pS[0] if w % 2 == 0 else pQ
                sc.copy(pT_sb[:, w % 2, 0:3, :].rearrange("p k n -> p (k n)"), bank[:, 0:3 * NTOK]).then_inc(patch_ta, 1)

            def step(q, par, s):
                f, g, bk, r1 = (batch(q, par, o, s) for o in (0, -1, -3, -4))
                r2 = par == 0 and (s is None or 6 <= s < 6 + B)
                for u in range(UNITS):
                    if bk:
                        act.wait_ge(st_ps[u % UR], un(bk, u))
                        if u < 2:
                            if not first(bk):
                                act.wait_ge(pv_ok[(UNITS - 2 + u) % UR], un(bk, UNITS - 2 + u, 1))
                        else:
                            act.wait_ge(pv_ok[(u - 2) % UR], un(bk, u - 2))
                        sc.activation(probs[:, u % 2].rearrange("p h t -> p (h t)"), pT[u % 2][0:HT, 0:2 * T],
                                      ACT.Exp).then_inc(ex_ok[u % UR], 1)
                    if u == 1 and f:
                        act.wait_ge(xT_ps, n(f))
                        if not first(f):
                            act.wait_ge(qk_ps, n(f, 1))
                            act.wait_ge(v_ps, n(f, 1))
                            act.wait_ge(xT_lo, n(f, 1))
                        sc.copy(xa_hi[:], pX[:, 0:T])
                        sc.copy(xt[:], pX[:, T:2 * T]).then_inc(xT_hi, 1)
                    if u == 10 and r1:
                        act.wait_ge(x2T_ps, n(r1))
                        if not first(r1):
                            act.wait_ge(rt_ps, n(r1, 1))
                        sc.copy(xn2T[:, 0, :], pX[:, 0:T])
                        sc.copy(xn2T[0:CT, 1, :], pX[0:CT, T:2 * T]).then_inc(x2T_ok, 1)
                    if u == 10 and r2:
                        act.wait_ge(dl_ok, q - 2)
                        sc.activation(edl[:], dlt[:], ACT.Exp).then_inc(ed_ok, 1)
                if bk:
                    act.wait_ge(pv_ok[(UNITS - 1) % UR], un(bk, UNITS - 1))
                    if not first(bk):
                        act.wait_ge(o_tr_ok, n(bk, 1))
                    sc.copy(o_raw[:, 0:2 * T], pQ[:, 0:2 * T]).then_inc(o_cp, 1)
                    sc.copy(o_raw[:, 2 * T:3 * T], pR[:, 0:T]).then_inc(o_cp, 1)
                if f:
                    act.wait_ge(qk_ps, n(f))
                    if not first(f):
                        pf = f[1] ^ 1
                        act.wait_ge(qk_out[pf], 96 * (f[0] - (1 if f[1] == 0 else 0)) + 96)
                    for i in range(3):
                        src = pS[0][:, i * T:(i + 1) * T] if i < 2 else pS[1][:, 0:T]
                        sc.activation(qk_hi[:, i, :], src, ACT.Identity, bias=bqk[:, i:i + 1]).then_inc(qk_hi_ok, 1)
                if g:
                    act.wait_ge(v_ok, n(g))
                    sc.copy(vaug[g[1]][:].rearrange("p a h d -> p (a h) d")[:, :, 0:HD],
                            vtmp[:].rearrange("p (h d) -> p h d", d=HD)).then_inc(va_ok, 1)

            act.wait_ge(v_pre, PRE_V)
            run_steps(act, step)

            def tile(j, par, guard):
                act.wait_ge(sx_ps, j + 1)
                if guard:
                    act.wait_ge(u_ps, j - 1)
                sc.copy(sxa[par][:], pX[:, 0:128]).then_inc(sx_ok, 1)
                sc.copy(sxt[par][0:CT, :], pX[0:CT, 128:256]).then_inc(sx_ok, 1)

            def relu_tile(j, par, guard):
                act.wait_ge(u_ps, j + 1)
                if guard:
                    act.wait_ge(hid_ok, 2 * (j - 1))
                sc.activation(relu[par][:, 0:512], pS[par][:], ACT.Relu).then_inc(relu_ok, 1)
                sc.activation(relu[par][:, 512:768], pT[par][:, 0:256], ACT.Relu).then_inc(relu_ok, 1)

            def hidT_half(j, guard):
                act.wait_ge(hT_ps, j + 1)
                if guard:
                    act.wait_ge(y2_ps, j)
                sc.copy(hidT[:, 0:3, :], pQ[:, 0:384].rearrange("p (k t) -> p k t", k=3)).then_inc(hT_a, 1)

            act.wait_ge(tab_ok, 1)
            tile(0, 0, False)
            relu_tile(0, 0, False)
            tile(1, 1, False)

            def ffn(t, r, guard, ahead=2):
                j, par = 4 * t + r, r % 2
                hidT_half(j, guard)
                if ahead > 1:
                    tile(j + 2, par, True)
                if ahead:
                    relu_tile(j + 1, 1 - par, guard)

            for r in range(4):
                ffn(0, r, r > 0)
            with act.Fori(1, BLOCKS // 4 - 1) as t:
                for r in range(4):
                    ffn(t, r, True)
            for r in range(4):
                ffn(BLOCKS // 4 - 1, r, True, min(2, 3 - r))

        @block.vector
        def _(dve):
            v = nc.vector
            pre = [0]

            def p(ins):
                pre[0] += 1
                ins.then_inc(v_pre, 1)
                return pre[0]

            def pw(ins):
                dve.wait_ge(v_pre, p(ins))

            for rnd in range(2):
                dve.wait_ge(a_pre, 5 + 2 * rnd)
                w = slice(0, 2 * C) if rnd == 0 else slice(2 * C, 3 * C)
                cols = w.stop - w.start
                banks = pS if rnd == 0 else pT
                v.tensor_tensor(wqkv_lo[:, w], banks[0][:, 0:cols], wqkv_hi[:, w].bitcast(F32), ALU.subtract)
                pw(v.tensor_copy(wqkv_t1[:, w], wqkv_t2[0:CT, w].bitcast(F32)))
                p(v.tensor_tensor(wqkv_t2[0:CT, w], banks[1][0:CT, 0:cols], wqkv_t1[:, w].bitcast(F32), ALU.subtract))
                assert pre[0] == PRE_LO[rnd]
            for c, rows in ((1, slice(0, PS)), (2, slice(PS // 2, PS))):
                dve.wait_ge(s_x[c], 16)
                src, dst = patch_views(c)
                p(v.tensor_copy(dst[:, :, rows], src[:, :, rows]))
            assert pre[0] == PRE_X
            for w in range(GRID + 1):
                if w < GRID:
                    dve.wait_ge(patch_tr, w + 1)
                    if w > 1:
                        dve.wait_ge(patch_mm, w - 1)
                    bank = pS[1] if w % 2 == 0 else pR
                    v.tensor_copy(pT_sb[:, w % 2, 3:6, :].rearrange("p k n -> p (k n)"), bank[:, 0:3 * NTOK]).then_inc(patch_tv, 1)
                if w:
                    dve.wait_ge(patch_mm, w)
                    if w == 1:
                        dve.wait_ge(s_tw, 32)
                    v.tensor_tensor(emb[:, w - 1, :], pT[(w - 1) % 2][0:NTOK, 0:C], tokb, ALU.add).then_inc(emb_ok, 1)
            dve.wait_ge(s_sm, 16 * small_loads)
            pw(v.tensor_tensor(r_sc[:, 24:48], em_in, em_in, ALU.mult))
            pw(v.tensor_reduce(r_sc[:, 0:1], r_sc[:, 24:48], AX.X, ALU.add))
            dve.wait_ge(g_pre, PRE_G)
            pw(v.tensor_scalar(r_sc[:, 2:3], r_sc[:, 1:2], 0.02 / C, 0.02 / C, ALU.mult, ALU.add))
            pw(v.tensor_scalar(r_sc[:, 3:4], r_sc[:, 1:2], 1e-12, None, ALU.max))
            pw(v.reciprocal(r_sc[:, 4:5], r_sc[:, 3:4]))
            pw(v.tensor_scalar(em_in, em_in, r_sc[:, 4:5], 0.02, ALU.mult, ALU.mult))
            pw(v.tensor_scalar(r_in, r_in, r_sc[:, 2:3], None, ALU.add))
            assert pre[0] == PRE_EMBN, pre[0]
            dve.wait_ge(t_pre, 4)
            p(v.tensor_copy(nT_sb, pX[0:DR, 448:448 + E]))
            assert pre[0] == PRE_NT
            pw(v.tensor_scalar(fe_in, fe_in, 0.1, None, ALU.mult))
            pw(v.tensor_tensor(fe_in[:, 0:E], fe_in[:, 0:E], fe_in[:, E:2 * E], ALU.subtract))
            pw(v.tensor_copy(bias_e[:], fe_in[:, 0:E].unsqueeze(1).to_broadcast([HT, 4, E])))
            v.tensor_scalar(bqk[0:64, :], bqk[0:64, :], SCALE, None, ALU.mult)
            v.memset(cum[:, 4, :], 0.0)
            dve.wait_ge(s_kon, 16)
            v.tensor_copy(tokf[:], kon[0:HT, K_TOK:K_TOK + 4])
            v.memset(sxt[0][CT:CT + 1, :], 1.0)
            v.memset(sxt[1][CT:CT + 1, :], 1.0)
            for i in range(2):
                v.memset(vaug[i][:], 1.0)
            v.memset(o_raw, 1.0)
            dve.wait_ge(t_pre, 5)
            v.tensor_copy(wroute[:, 0, :], pV[:, 0:RC])
            pw(v.tensor_copy(wroute[0:CT, 1, :], pV[0:CT, 64:64 + RC]))
            assert pre[0] == PRE_V, pre[0]

            def norm_stats(src, st, st_sem, b, a):
                ins = v.bn_stats(st[b[1]][:, a, :], src[:, a, :])
                if a == 1:
                    ins.then_inc(st_sem, 1)

            def norm_aggregate(st, mv, st_sem, mv_sem, b):
                dve.wait_ge(st_sem, n(b))
                settle(dve)
                v.bn_aggr(mv[b[1]][:, 0, :], st[b[1]][:, 0, :])
                v.bn_aggr(mv[b[1]][:, 1, :], st[b[1]][:, 1, :]).then_inc(mv_sem, 1)

            def step(q, par, s):
                pr, f, g, m, bk, r1 = (batch(q, par, o, s) for o in (1, 0, -1, -2, -3, -4))
                r2 = par == 0 and (s is None or 6 <= s < 6 + B)
                weights = par == 1 and (s is None or 0 <= s < 2 * E)
                k = q - 2
                flat = lambda t: t.rearrange("p a e -> p (a e)")

                def expert_part(i, e):
                    rows, cols = ((slice(0, 128), slice(0, H)), (slice(0, CT), slice(H, 2 * H)), (slice(0, 128), slice(2 * H, WCOLS)))[i]
                    gate = mg[rows, i // 2, bass.ds(e, 1)]
                    ins = v.scalar_tensor_tensor(expert(e)[rows, cols], stage_s[rows, cols], gate, expert(e)[rows, cols], ALU.mult, ALU.add)
                    if i == 2:
                        ins.then_inc(wprep, 1)

                def route(i):
                    src = lg if i < 10 else lg2
                    c = int(i > 10)
                    if i == 0:
                        dve.wait_ge(rt_pow, 2 * k)
                        v.tensor_scalar(rinv[:], rnm[:], 1e-12, None, ALU.max).then_inc(nm_floor, 1)
                    if i == 1:
                        dve.wait_ge(nm_floor, k)
                        v.reciprocal(rnm[:], rinv[:]).then_inc(nm_inv, 1)
                    if i == 2:
                        dve.wait_ge(nm_inv, k)
                        v.tensor_tensor(lg2[:], rt[:, :, E:2 * E], rnm[:].unsqueeze(2).to_broadcast([HT, 4, E]), ALU.mult).then_inc(align_ok, 1)
                    if i == 3:
                        dve.wait_ge(align_ok, k)
                        v.tensor_tensor(lg2[:], lg2[:], rt[:, :, 0:E], ALU.add).then_inc(lin_ok, 1)
                    if i == 4:
                        dve.wait_ge(lin_ok, k)
                        v.tensor_tensor(lg[:], lg2[:], bias_e[:], ALU.add).then_inc(lg_ok, 1)
                    if i in (5, 11):
                        dve.wait_ge(lg_ok if i == 5 else lg2_ok, k)
                        v.tensor_reduce(top[:, c, :], src[:], AX.X, ALU.max).then_inc(pick_max[c], 1)
                    if i in (6, 12):
                        dve.wait_ge(pick_max[c], k)
                        v.tensor_tensor(cand[:], src[:], top[:, c, :].unsqueeze(2).to_broadcast([HT, 4, E]), ALU.is_equal).then_inc(pick_eq[c], 1)
                    if i in (7, 13):
                        dve.wait_ge(pick_eq[c], k)
                        v.tensor_tensor(cand[:], cand[:], kon[0:HT, K_DESC:K_DESC + 4 * E].rearrange("p (a e) -> p a e", a=4), ALU.mult).then_inc(pick_order[c], 1)
                    if i in (8, 14):
                        dve.wait_ge(pick_order[c], k)
                        v.tensor_reduce(cmx[:], cand[:], AX.X, ALU.max).then_inc(pick_best[c], 1)
                    if i in (9, 15):
                        dve.wait_ge(pick_best[c], k)
                        v.tensor_tensor(hot[:, c, :, :], cand[:], cmx[:].unsqueeze(2).to_broadcast([HT, 4, E]), ALU.is_equal).then_inc(hot_ok[c], 1)
                    if i == 10:
                        dve.wait_ge(hot_ok[0], k)
                        v.scalar_tensor_tensor(flat(lg2[:]), flat(hot[:, 0, :, :]), -1e30, flat(lg[:]), ALU.mult, ALU.add).then_inc(lg2_ok, 1)
                    if i == 16:
                        v.tensor_tensor(dlt[:], top[:, 1, :], top[:, 0, :], ALU.subtract).then_inc(dl_ok, 1)
                    if i == 17:
                        dve.wait_ge(hot_ok[1], k)
                        v.tensor_tensor(flat(cand[:]), flat(hot[:, 0, :, :]), flat(hot[:, 1, :, :]), ALU.add)
                    if i == 18:
                        v.tensor_copy(cum[:, 0, :], cum[:, 4, :]).then_inc(cum_cp, 1)
                    if 19 <= i < 23:
                        dve.wait_ge(cum_cp if i == 19 else cum_ok, k if i == 19 else 4 * (k - 1) + i - 19)
                        v.tensor_tensor(cum[:, i - 18, :], cum[:, i - 19, :], cand[:, i - 19, :], ALU.add).then_inc(cum_ok, 1)

                def slot_channels(c):
                    if c == 0 and (s is None or k > 1):
                        dve.wait_ge(sc_done, 128 * (k - 1))
                    v.tensor_copy(slot_rows[:, :, c, 0:C], xn2[:].rearrange("p b a c -> p (b a) c")).then_inc(slot_cp, 1)

                if g:
                    dve.wait_ge(v_ps, n(g))
                    if not first(g):
                        dve.wait_ge(va_ok, n(g, 1))
                    v.tensor_tensor(vtmp[:], pV[0:HT, 0:2 * C], bv_bc[:].rearrange("p a c -> p (a c)"), ALU.add).then_inc(v_ok, 1)
                if r2:
                    for i in range(6):
                        route(i)
                if f:
                    dve.wait_ge(xT_hi, n(f))
                    v.tensor_tensor(xa_lo[:], pX[:, 0:T], xa_hi[:].bitcast(F32), ALU.subtract)
                    v.tensor_tensor(xt[CT:128, :], pX[CT:128, T:2 * T], xt[CT:128, :].bitcast(F32), ALU.subtract).then_inc(xT_lo, 1)
                if r2:
                    for i in range(6, 11):
                        route(i)
                for u in range(UNITS):
                    if m:
                        pp, a = u // 2, u % 2
                        dve.wait_ge(s_ps[u % UR], un(m, u))
                        if u == 0 and not first(m):
                            dve.wait_ge(mT_ps, n(m, 1))
                        v.tensor_reduce(mx[:, :, pp, a], pS[u % 2][0:HT, 0:2 * T].rearrange("p (h t) -> p h t", h=2),
                                        AX.X, ALU.max).then_inc(mx_ok[u % UR], 1)
                    if r2:
                        route(11 + u)
                    if u == 3 and r1:
                        dve.wait_ge(y_ps, n(r1))
                        dve.wait_ge(hR_in[r1[1]], 16 * r1[0] + 16)
                        v.tensor_tensor(hR[r1[1]][:].rearrange("p a c -> p (a c)"), pV[0:HT, 0:2 * C],
                                        hR[r1[1]][:].rearrange("p a c -> p (a c)"), ALU.add).then_inc(h2_ok, 1)
                    if 4 <= u < 6 and r1:
                        dve.wait_ge(h2_ok, n(r1))
                        norm_stats(hR[r1[1]], st2, ln2_st, r1, u - 4)
                    if u == 6 and r1:
                        norm_aggregate(st2, mv2, ln2_st, ln2_mv, r1)
                    if u in (7, 8) and r2 and s != B + 4:
                        slot_channels(u - 7)
                    if 9 <= u < 11 and pr:
                        if u == 9:
                            dve.wait_ge(hA_in[pr[1]], 16 * pr[0] + 16)
                            if not first(pr, 2):
                                dve.wait_ge(ln1_pow, n(pr, 2))
                        norm_stats(hA[pr[1]], st1, ln1_st, pr, u - 9)
                    if u == 11 and pr:
                        norm_aggregate(st1, mv1, ln1_st, ln1_mv, pr)
                    if u == 9 and r1:
                        dve.wait_ge(ln2_pow, n(r1))
                        if not first(r1, 2):
                            dve.wait_ge(x2T_ps, n(r1, 2))
                        if r2:
                            dve.wait_ge(slot_cp, 2 * k)
                        for a in range(2):
                            last = v.tensor_scalar(xn2[:, r1[1], a, :], hR[r1[1]][:, a, :], mv2[r1[1]][:, a, 0:1],
                                                   rs2[r1[1]][:, a, 1:2], ALU.subtract, ALU.mult)
                        last.then_inc(xn2_ok, 1)
                if m:
                    dve.wait_ge(mT_ps, n(m))
                    if not first(m):
                        pm = m[1] ^ 1
                        dve.wait_ge(m_out[pm], 16 * (m[0] - (1 if m[1] == 0 else 0)) + 16)
                    v.tensor_scalar(mT[:], pS[0][0:2 * NH, 0:HT], -1.0, None, ALU.mult).then_inc(mT_ok, 1)
                if pr:
                    dve.wait_ge(ln1_pow, n(pr))
                    if not first(pr):
                        dve.wait_ge(xT_ps, n(pr, 1))
                    for a in range(2):
                        v.tensor_scalar(xn[:, a, 0:C], hA[pr[1]][:, a, :], mv1[pr[1]][:, a, 0:1],
                                        rs1[pr[1]][:, a, 1:2], ALU.subtract, ALU.mult)
                        last = v.tensor_scalar(xn[:, a, C:256], hA[pr[1]][:, a, CA:C], mv1[pr[1]][:, a, 0:1],
                                               rs1[pr[1]][:, a, 1:2], ALU.subtract, ALU.mult)
                    last.then_inc(xn_ok, 1)
                if weights:
                    dve.wait_ge(hebb_in, 48 * q + 48)
                    dve.wait_ge(slow_in, 48 * q + 48)
                    if s == 1:
                        dve.wait_ge(s_sm, 16 * small_loads)
                    expert_part(0, q)
                    expert_part(1, q)
                if par == 0 and (s is None or 2 <= s < 2 + 2 * E):
                    expert_part(2, q - 1)
                if r1:
                    dve.wait_ge(rt_ps, n(r1))
                    if r2:
                        dve.wait_ge(rank_ps, k)
                    sl = slice(2 * r1[1], 2 * r1[1] + 2)
                    v.tensor_copy(rt[:, sl, :], pV[0:HT, 384:384 + 2 * RC].rearrange("p (a r) -> p a r", a=2)).then_inc(rt_cp, 1)
                    dve.wait_ge(rt_cp, n(r1))
                    v.tensor_tensor(rsq[:, sl, :], rt[:, sl, 2 * E:], rt[:, sl, 2 * E:], ALU.mult).then_inc(rt_sq, 1)
                    dve.wait_ge(rt_sq, n(r1))
                    if not first(r1, 2):
                        dve.wait_ge(rt_pow, n(r1, 2))
                    v.tensor_reduce(rss[:, sl], rsq[:, sl, :], AX.X, ALU.add).then_inc(rt_ss, 1)
                if r2:
                    dve.wait_ge(rank_ps, k)
                    v.tensor_tensor(rank[:].rearrange("p a e -> p (a e)"), p_rank(), kon[0:HT, K_BASE:K_BASE + 4 * E], ALU.add).then_inc(rank_ok, 1)
                if r2:
                    dve.wait_ge(ed_ok, k)
                    v.tensor_scalar(rinv[:], edl[:], 1.0, None, ALU.add).then_inc(den_ok, 1)
                    dve.wait_ge(rank_ok, k)
                    for c in range(2):
                        last = v.tensor_tensor(rsel[:, c, :, :], hot[:, c, :, :], rank[:], ALU.mult)
                    last.then_inc(rsel_ok, 1)
                    dve.wait_ge(den_ok, k)
                    v.reciprocal(gates[:, 0, :], rinv[:]).then_inc(gate0_ok, 1)
                    dve.wait_ge(rsel_ok, k)
                    v.tensor_reduce(rowf[:].rearrange("p c a -> p (c a)"), rsel[:].rearrange("p c a e -> p (c a) e"), AX.X, ALU.add).then_inc(rowf_ok, 1)
                    dve.wait_ge(gate0_ok, k)
                    v.tensor_tensor(gates[:, 1, :], gates[:, 0, :], edl[:], ALU.mult).then_inc(gate1_ok, 1)
                    dve.wait_ge(rowf_ok, k)
                    dve.wait_ge(gate1_ok, k)
                    if s == B + 4:
                        slot_channels(0)
                        slot_channels(1)
                    v.tensor_copy(rowi[:], rowf[:])
                    for c in range(2):
                        v.tensor_copy(slot_rows[:, :, c, C:C + 1], gates[:, c, :].unsqueeze(2))
                        last = v.tensor_copy(slot_rows[:, :, c, C + 1:C + 2].bitcast(U32), tokf[:].unsqueeze(2))
                    last.then_inc(row_ok, 1)
                    dve.wait_ge(row_ok, k)
                    v.tensor_scalar(tokf[:], tokf[:], float(2 * T), None, ALU.add)
                if bk:
                    dve.wait_ge(o_cp, 2 * n(bk))
                    settle(dve)
                    v.transpose(o_tr, o_raw).then_inc(o_tr_ok, 1)
                    dve.wait_ge(o_tr_ok, n(bk))
                    blocks = o_tr.rearrange("p (b x) -> p b x", x=32)
                    v.reciprocal(osum[:].unsqueeze(2), blocks[:, :, HD:HD + 1]).then_inc(o_rc, 1)
                    dve.wait_ge(o_rc, n(bk))
                    v.tensor_tensor(blocks, blocks, osum[:].unsqueeze(2).to_broadcast([128, OW // 32, 32]), ALU.mult).then_inc(o_mul, 1)
                    dve.wait_ge(o_mul, n(bk))
                    settle(dve)
                    if not first(bk):
                        dve.wait_ge(y_ps, n(bk, 1))
                        settle(dve)
                    v.transpose(o_out, o_tr).then_inc(o_ok, 1)
                if f:
                    for i in range(3):
                        dve.wait_ge(qk_hi_ok, 3 * n(f, 1) + (2 if i < 2 else 3))
                        if i == 0 and not first(f):
                            pf = f[1] ^ 1
                            dve.wait_ge(qk_out[pf], 96 * (f[0] - (1 if f[1] == 0 else 0)) + 96)
                        src = pS[0][:, i * T:(i + 1) * T] if i < 2 else pS[1][:, 0:T]
                        v.scalar_tensor_tensor(qk_lo[:, i, :], src, bqk[:, i:i + 1], qk_hi[:, i, :].bitcast(F32),
                                               ALU.add, ALU.subtract).then_inc(qk_lo_ok, 1)

            run_steps(dve, step)

            links = [0]

            def link(ins):
                links[0] += 1
                ins.then_inc(tch, 1)
                dve.wait_ge(tch, links[0])
            dve.wait_ge(cnt_ps, 1)
            link(v.tensor_copy(cnt[:], pV[0:1, 0:E]))
            kk = kon[0:1, K_KK:K_KK + LIST_TILES].unsqueeze(1).to_broadcast([1, E, LIST_TILES])
            link(v.tensor_tensor(tcmp[:], cnt[:].unsqueeze(2).to_broadcast([1, E, LIST_TILES]), kk, ALU.is_gt))
            link(v.tensor_reduce(nblk[:], tcmp[:], AX.X, ALU.add))
            link(v.tensor_tensor(tcum[:], kon[0:1, K_CUM:K_CUM + E * E].rearrange("p (a b) -> p a b", a=E),
                                 nblk[:].unsqueeze(1).to_broadcast([1, E, E]), ALU.mult))
            link(v.tensor_reduce(ends[:], tcum[:], AX.X, ALU.add))
            jj = kon[0:1, K_JJ:K_JJ + BLOCKS]
            link(v.tensor_tensor(tge[:], jj.unsqueeze(2).to_broadcast([1, BLOCKS, E]),
                                 ends[:].unsqueeze(1).to_broadcast([1, BLOCKS, E]), ALU.is_ge))
            link(v.tensor_reduce(tabf[:, BLOCKS:2 * BLOCKS], tge[:], AX.X, ALU.add))
            link(v.tensor_scalar(tabf[:, BLOCKS:2 * BLOCKS], tabf[:, BLOCKS:2 * BLOCKS], float(E - 1), None, ALU.min))
            link(v.tensor_scalar(twt[:], nblk[:], -128.0, float(CAP), ALU.mult, ALU.add))
            link(v.tensor_tensor(trow[:], tge[:], twt[:].unsqueeze(1).to_broadcast([1, BLOCKS, E]), ALU.mult))
            link(v.tensor_reduce(tabf[:, 0:BLOCKS], trow[:], AX.X, ALU.add))
            link(v.scalar_tensor_tensor(tabf[:, 0:BLOCKS], jj, 128.0, tabf[:, 0:BLOCKS], ALU.mult, ALU.add))
            link(v.tensor_tensor(tabf[:, 2 * BLOCKS:], cnt[:], kon[0:1, K_BASE:K_BASE + E], ALU.add))
            v.tensor_copy(tabi[:], tabf[:]).then_inc(tab_ok, 1)
            dve.wait_ge(tab_ok, 1)

            def square(j, par, guard):
                for i, cols in enumerate((slice(0, 512), slice(512, H))):
                    dve.wait_ge(relu_ok, 2 * j + 1 + i)
                    if guard and i == 0:
                        dve.wait_ge(hT_ps, j - 1)
                    r_ = relu[par][:, cols]
                    v.tensor_tensor(hid[par][:, cols], r_, r_, ALU.mult).then_inc(hid_ok, 1)

            def hidT_half(j, guard):
                dve.wait_ge(hT_ps, j + 1)
                if guard:
                    dve.wait_ge(y2_ps, j)
                v.tensor_copy(hidT[:, 3:6, :], pR[:, 0:384].rearrange("p (k t) -> p k t", k=3)).then_inc(hT_v, 1)

            def output(j, r, par, guard, e):
                dve.wait_ge(y2_ps, j + 1)
                v.tensor_tensor(ysum[par], pV[:, 0:C], b2_bc[:, bass.ds(e, 1), :].rearrange("p a c -> p (a c)"),
                                ALU.add).then_inc(ys_ok, 1)
                dve.wait_ge(ys_ok, j + 1)
                if guard:
                    dve.wait_ge(add_done, 16 * (j - 1))
                v.tensor_scalar(ygate[par], ysum[par], xs[r][:, C:C + 1], None, ALU.mult).then_inc(yg_ok, 1)

            def ffn(t, r, guard, ahead=True):
                j, par = 4 * t + r, r % 2
                hidT_half(j, guard)
                if ahead:
                    square(j + 1, 1 - par, guard)
                e = dve.value_load(tabi[0:1, bass.ds(BLOCKS + j, 1)], min_val=0, max_val=E - 1)
                output(j, r, par, guard, e)

            square(0, 0, False)
            for r in range(4):
                ffn(0, r, r > 0)
            with dve.Fori(1, BLOCKS // 4 - 1) as t:
                for r in range(4):
                    ffn(t, r, True)
            for r in range(4):
                ffn(BLOCKS // 4 - 1, r, True, min(2, 3 - r))

        @block.gpsimd
        def _(pool):
            g = nc.gpsimd
            g.memset(wo_in, 0.0).then_inc(g_pre, 1)
            pool.wait_ge(g_pre, 1)
            for eh in range(2):
                pool.dma_start(wo_in[:, eh, :].rearrange("p (h d) -> p h d", d=32)[:, :, 0:HD],
                               w_out[eh * 96:(eh + 1) * 96, :].rearrange("p (h d) -> p h d", d=HD)).then_inc(s_wo, 16)
            pool.dma_start(wo_in[:, :, HD:HD + 1], b_out.rearrange("(e p a) -> p e a", p=96, a=1),
                           allow_slow_non_contiguous=True).then_inc(s_wo, 16)
            g.memset(kdiag[0][:].bitcast(F32), 0.0)
            g.memset(kdiag[1][:].bitcast(F32), 0.0)
            g.memset(powers[:, 0:2], -0.5)
            g.memset(powers[:, 2:4], 0.5).then_inc(g_pre, 1)
            pool.wait_ge(g_pre, 2)
            pool.wait_ge(v_pre, PRE_SS)
            g.tensor_tensor(r_sc[:, 1:2], r_sc[:, 0:1], powers[0:E, 2:3], ALU.pow).then_inc(g_pre, 1)

            def rsqrt(mv, rs, mv_sem, pe_sem, pow_sem, b):
                pool.wait_ge(mv_sem, n(b))
                settle(pool)
                g.tensor_scalar(rs[b[1]][:, :, 0:1], mv[b[1]][:, :, 1:2], 1e-5, None, ALU.add).then_inc(pe_sem, 1)
                pool.wait_ge(pe_sem, n(b))
                g.tensor_tensor(rs[b[1]][:, :, 1], rs[b[1]][:, :, 0], powers[:, 0:2], ALU.pow).then_inc(pow_sem, 1)

            def scatter(k, j):
                a, c = j // 2, j % 2
                if not (isinstance(k, int) and k + j == 0):
                    pool.wait_ge(sc_done, 128 * k + 16 * j)
                settle(pool)
                g.indirect_dma_start(slots_dram, bass.IndirectOffsetOnAxis(ap=rowi[:, c, a:a + 1], axis=0),
                                     slot_rows[:, a, c, :], None).then_inc(sc_done, 16)

            def step(q, par, s):
                pr, gg, m, bk, r1 = (batch(q, par, o, s) for o in (1, -1, -2, -3, -4))
                if par == 0 and (s is None or 8 <= s < B + 4 or s == LAST):
                    scatter(q - 4, 7)
                turn = iter(range(1, 8))
                drain = s is not None and s > B + 2

                def next_scatter():
                    if par == 1 and (s is None or 7 <= s):
                        scatter(q - 3, next(turn))

                def probe_norms():
                    if r1:
                        pool.wait_ge(rt_ss, n(r1))
                        if r1[1] == 0 and not first(r1, 2):
                            pool.wait_ge(nm_inv, r1[0])
                        sl = slice(2 * r1[1], 2 * r1[1] + 2)
                        g.tensor_tensor(rnm[:, sl], rss[:, sl], powers[:, 2:4], ALU.pow).then_inc(rt_pow, 1)

                def add_hebbian(i):
                    if par == 1 and (s is None or 0 <= s < 2 * E):
                        if i == 0:
                            pool.wait_ge(fast_in, 64 * q + 64)
                            settle(pool)
                        dst, src = expert_loads(expert(q), h_fast1, h_fast2, q)[i]
                        pool.dma_start(dst, src, accum_op=ALU.add).then_inc(hebb_in, 16)

                next_scatter()
                add_hebbian(0)
                next_scatter()
                add_hebbian(1)
                add_hebbian(2)
                if r1:
                    if not first(r1, 2):
                        pool.wait_ge(xn2_ok, n(r1, 2))
                    rsqrt(mv2, rs2, ln2_mv, ln2_pe, ln2_pow, r1)
                next_scatter()
                next_scatter()
                if drain:
                    probe_norms()
                    next_scatter()
                    next_scatter()
                    if s == B + 3:
                        next_scatter()
                if pr:
                    if not first(pr, 2):
                        pool.wait_ge(xn_ok, n(pr, 2))
                    rsqrt(mv1, rs1, ln1_mv, ln1_pe, ln1_pow, pr)
                if m:
                    pool.wait_ge(m_out[m[1]], 16 * m[0] + 16)
                    settle(pool)
                    pool.dma_start(qpack[m[1]][96:98].rearrange("h p t -> h (p t)"),
                                   m_dram[m[1]].rearrange("(h r) t -> h (r t)", h=2)).then_inc(m_in[m[1]], 16)
                if gg:
                    pool.wait_ge(qk_out[gg[1]], 96 * gg[0] + 96)
                    if bk:
                        pool.wait_ge(st_ps[(UNITS - 1) % UR], un(bk, UNITS - 1))
                    settle(pool)
                    d = qk_dram[gg[1]]
                    for a in range(2):
                        rows = slice(16 * a, 16 * a + 16)
                        pool.dma_start(kdiag[gg[1]][48 * a:48 * a + 48, :, a, :],
                                       d[1, :, rows, :].rearrange("g x (p t) -> g x p t", p=PAIRS)).then_inc(qk_in[gg[1]], 16)
                        pool.dma_start(qpack[gg[1]][48 * a:48 * a + 48].rearrange("r p t -> r (p t)"),
                                       d[0, :, rows, :]).then_inc(qk_in[gg[1]], 16)
                if not drain:
                    probe_norms()
                    next_scatter()
                    next_scatter()
                if par == 0 and (s is None or 6 <= s < 6 + B):
                    pool.wait_ge(row_ok, q - 2)
                    scatter(q - 3, 0)

            for i in range(2):
                pool.dma_start(kdiag[i][96:98], head_select).then_inc(s_zero, 16)
            pool.wait_ge(s_dummy, 16 * 2)
            pool.wait_ge(s_zero, 32)
            run_steps(pool, step)
            pool.wait_ge(sc_done, 16 * 4 * B)
            for p_ in range(2):
                pool.wait_ge(h2_out[p_], 8 * B)

            def add(j, r, guard):
                pool.wait_ge(yg_ok, j + 1)
                if guard:
                    pool.wait_ge(add_done, 16 * j)
                settle(pool)
                g.indirect_dma_start(out, bass.IndirectOffsetOnAxis(ap=xs[r][:, C + 1:C + 2].bitcast(U32), axis=0),
                                     ygate[r % 2], None, compute_op=ALU.add).then_inc(add_done, 16)
            for r in range(4):
                add(r, r, r > 0)
            with pool.Fori(1, BLOCKS // 4) as t:
                for r in range(4):
                    add(4 * t + r, r, True)
            pool.wait_ge(add_done, 16 * BLOCKS)



_INS = ["x", "txt", "L0_tok_W", "L0_tok_b", "L0_tok_cls_token", "L0_attn_w_qkv", "L0_attn_b_qkv", "L0_attn_w_out",
        "L0_attn_b_out", "L0_ffn_router_w", "L0_ffn_probe_w", "L0_ffn_router_emb", "L0_ffn_fatigue", "L0_ffn_energy",
        "L0_ffn_w_fast1", "L0_ffn_w_slow1", "L0_ffn_h_fast1", "L0_ffn_m_gate1", "L0_ffn_b1", "L0_ffn_w_fast2",
        "L0_ffn_w_slow2", "L0_ffn_h_fast2", "L0_ffn_m_gate2", "L0_ffn_b2"]


def kernel(**inputs):
    import concourse.bacc as bacc
    from concourse.bass_utils import run_bass_kernel_spmd

    nc = bacc.Bacc("TRN2", target_bir_lowering=False, num_devices=1)
    arrays = {f"in_{k}": np.ascontiguousarray(inputs[k]) for k in _INS}
    arrays.update({f"const_{k}": a for k, a in shape_constants().items()})
    args = [nc.dram_tensor(k, a.shape, mybir.dt.from_np(a.dtype), kind="ExternalInput").ap() for k, a in arrays.items()]
    out = nc.dram_tensor("out_rows", [N + 128, C], F32, kind="ExternalOutput").ap()
    build_program(nc, *args, out)
    r = run_bass_kernel_spmd(nc, [arrays], core_ids=[0])
    return r.results[0]["out_rows"][:N].reshape(B, T, C)
```
